# Optimizing a Trainium2 kernel written in Bass

```python
import numpy as np
import jax
import jax.numpy as jnp

def _softmax(x, axis=-1):
    return jax.nn.softmax(x, axis=axis)

def _gelu(x):
    return jax.nn.gelu(x, approximate=True)

def _silu(x):
    return jax.nn.silu(x)

def _sigmoid(x):
    return jax.nn.sigmoid(x)

def _layernorm(x, axis=-1, eps=1e-05):
    m = jnp.mean(x, axis=axis, keepdims=True)
    v = jnp.var(x, axis=axis, keepdims=True)
    return (x - m) / jnp.sqrt(v + eps)

def _scatter_add(tgt, idx, src, axis=0):
    return tgt.at[idx].add(src)

def _segment_sum(src, seg, n):
    return jax.ops.segment_sum(src, seg, n)
kernel_name = 'mk_cond_seq_d4_seqx_r4_17e415'

def setup_inputs(seed: int=0):
    np.random.seed(seed)
    _w = jnp.asarray

    def _rec_inputs():
        import jax
        import jax.numpy as jnp
        _rk = jax.random.key(seed)
        x = -0.0002928 + 1 * jax.random.normal(jax.random.fold_in(_rk, 1), (32, 256, 256), jnp.float32)
        _lenS = 256 - jax.random.randint(jax.random.fold_in(_rk, 7), (32,), 0, max(1, 256 // 4) + 1, jnp.int32)
        _lenS2 = 256 - jax.random.randint(jax.random.fold_in(_rk, 8), (32,), 0, max(1, 256 // 4) + 1, jnp.int32)
        cond_1024 = 0.0061147 + 1.02565 * jax.random.normal(jax.random.fold_in(_rk, 11), (32, 256), jnp.float32)
        _validS = jnp.arange(256)[None, :] < _lenS[:, None]
        _validS2 = jnp.arange(256)[None, :] < _lenS2[:, None]
        _causal = jnp.tril(jnp.ones((256, 256), dtype=bool))
        mask_BxSxSx11_ik0 = jnp.where(jnp.ones((32, 256, 256, 11), dtype=bool), 0, 1).astype(jnp.int32)
        return (x, cond_1024, mask_BxSxSx11_ik0)
    x, cond_1024, mask_BxSxSx11_ik0 = _rec_inputs()

    def _L0_cond_setup():
        import jax, jax.numpy as jnp
        import numpy as np
        B, T, DIM = (4, 256, 256)
        COND = 256
        HEADS, DH = (16, 64)
        INNER = HEADS * DH
        MLP = 1024
        EPS = 1e-05

        def _layernorm(x):
            mu = jnp.mean(x, axis=-1, keepdims=True)
            var = jnp.mean(jnp.square(x - mu), axis=-1, keepdims=True)
            return (x - mu) * jax.lax.rsqrt(var + EPS)

        def _modulate(x, shift, scale):
            return x * (1.0 + scale) + shift

        def _attention(x, W_qkv, W_out, b_out):
            Bq, Tq, _ = x.shape
            qkv = x @ W_qkv
            q, k, v = jnp.split(qkv, 3, axis=-1)
            q = q.reshape(Bq, Tq, HEADS, DH)
            k = k.reshape(Bq, Tq, HEADS, DH)
            v = v.reshape(Bq, Tq, HEADS, DH)
            scale = DH ** (-0.5)
            attn = jnp.einsum('bqhd,bkhd->bhqk', q, k) * scale
            attn = jax.nn.softmax(attn, axis=-1)
            out = jnp.einsum('bhqk,bkhd->bqhd', attn, v).reshape(Bq, Tq, INNER)
            return out @ W_out + b_out

        def _ff(x, W1, b1, W2, b2):
            return jax.nn.gelu(x @ W1 + b1, approximate=False) @ W2 + b2
        key = jax.random.key(seed)
        ks = jax.random.split(key, 12)
        s = 0.02
        return {'x': jax.random.normal(ks[0], (B, T, DIM), jnp.float32), 'c': jax.random.normal(ks[1], (B, 1, COND), jnp.float32), 'W_mod': jax.random.normal(ks[2], (COND, 6 * DIM), jnp.float32) * s, 'b_mod': jax.random.normal(ks[3], (6 * DIM,), jnp.float32) * s, 'W_qkv': jax.random.normal(ks[4], (DIM, 3 * INNER), jnp.float32) * s, 'W_out': jax.random.normal(ks[5], (INNER, DIM), jnp.float32) * s, 'b_out': jax.random.normal(ks[6], (DIM,), jnp.float32) * s, 'W1': jax.random.normal(ks[7], (DIM, MLP), jnp.float32) * s, 'b1': jax.random.normal(ks[8], (MLP,), jnp.float32) * s, 'W2': jax.random.normal(ks[9], (MLP, DIM), jnp.float32) * s, 'b2': jax.random.normal(ks[10], (DIM,), jnp.float32) * s}
    _L0_cond_all = _L0_cond_setup()
    _L0_cond_in = {k: v for k, v in _L0_cond_all.items() if k in ('W_mod', 'b_mod', 'W_qkv', 'W_out', 'b_out', 'W1', 'b1', 'W2', 'b2')}
    del _L0_cond_all

    def _L1_cond_setup():
        import jax, jax.numpy as jnp
        import numpy as np
        NONGT = 20
        H = 16
        NEG = -9000000000000000.0

        def _gat_attention(self_feat, cond_adj, label_bias, Wq, bq, Wk, bk, Wout, bout):
            B, N, F = self_feat.shape
            ng = min(NONGT, N)
            dh = F // H
            kv = self_feat[:, :ng]
            qh = (self_feat @ Wq.T + bq).reshape(B, N, H, dh)
            kh = (kv @ Wk.T + bk).reshape(B, ng, H, dh)
            aff = jnp.einsum('bnhd,bmhd->bnhm', qh, kh) * (1.0 / np.sqrt(dh))
            mask = cond_adj[:, :, None, :] > 0
            aff = jnp.where(mask, aff, NEG) + label_bias[:, :, None, :]
            w = jax.nn.softmax(aff, axis=-1)
            out_t = jnp.einsum('bnhm,bmf->bnhf', w, kv)
            out = jnp.einsum('bnhf,hgf->bnhg', out_t, Wout) + bout.reshape(H, F // H)
            return out.reshape(B, N, F)

        def _forward(v, q, adj, W_self, b_self, w_bias, b_bias, Wq, bq, Wk, bk, Wout, bout):
            adj_f = adj.astype(jnp.float32)
            exp_v = v
            row_zero = exp_v.sum(-1) == 0
            q_exp = jnp.where(row_zero[..., None], 0.0, q[:, None, :])
            vcq = jnp.concatenate([exp_v, q_exp], axis=-1)
            self_feat = vcq @ W_self.T + b_self
            output = self_feat
            for d in range(2):
                A = adj_f if d == 0 else jnp.swapaxes(adj_f, 1, 2)
                A = A[:, :, :NONGT, :]
                cond = A.sum(-1)
                vb = A @ w_bias + b_bias
                output = output + _gat_attention(self_feat, cond, vb, Wq[d], bq[d], Wk[d], bk[d], Wout[d], bout[d])
            rel = jax.nn.relu(output)
            return exp_v + rel
        key = jax.random.key(seed)
        ks = jax.random.split(key, 8)
        B, N, L, F, Q = (64, 36, 11, 256, 256)
        IN = F + Q
        s = 0.02
        return {'v': jax.random.normal(ks[0], (B, N, F), jnp.float32), 'q': jax.random.normal(ks[1], (B, Q), jnp.float32), 'adj': jax.random.randint(ks[2], (B, N, N, L), 0, 2, jnp.int32), 'W_self': jax.random.normal(ks[3], (F, IN), jnp.float32) * s, 'b_self': jnp.zeros((F,), jnp.float32), 'w_bias': jax.random.normal(ks[4], (L,), jnp.float32) * s, 'b_bias': jnp.zeros((), jnp.float32), 'Wq': jax.random.normal(ks[5], (2, F, F), jnp.float32) * s, 'bq': jnp.zeros((2, F), jnp.float32), 'Wk': jax.random.normal(ks[6], (2, F, F), jnp.float32) * s, 'bk': jnp.zeros((2, F), jnp.float32), 'Wout': jax.random.normal(ks[7], (2, H, F // H, F), jnp.float32) * s, 'bout': jnp.zeros((2, F), jnp.float32)}
    _L1_cond_all = _L1_cond_setup()
    _L1_cond_in = {k: v for k, v in _L1_cond_all.items() if k in ('W_self', 'b_self', 'w_bias', 'b_bias', 'Wq', 'bq', 'Wk', 'bk', 'Wout', 'bout')}
    del _L1_cond_all

    def _L2_cond_setup():
        import jax, jax.numpy as jnp
        import numpy as np
        H = 16
        EPS = 1e-05

        def layer_norm(x, g, b):
            mu = jnp.mean(x, axis=-1, keepdims=True)
            var = jnp.var(x, axis=-1, keepdims=True)
            return (x - mu) * jax.lax.rsqrt(var + EPS) * g + b
        key = jax.random.key(seed)
        ks = jax.random.split(key, 8)
        B, T, D, TE = (4, 1024, 256, 256)
        s = 0.02
        return {'x': jax.random.normal(ks[0], (B, T, D), jnp.float32), 'emb': jax.random.normal(ks[1], (B, 1, TE), jnp.float32), 'gate_msa': jax.random.normal(ks[2], (B, 1, D), jnp.float32), 'norm_g': jnp.ones((D,), jnp.float32), 'norm_b': jnp.zeros((D,), jnp.float32), 'Wq': jax.random.normal(ks[3], (D, D), jnp.float32) * s, 'bq': jnp.zeros((D,), jnp.float32), 'Wk': jax.random.normal(ks[4], (D, D), jnp.float32) * s, 'bk': jnp.zeros((D,), jnp.float32), 'Wv': jax.random.normal(ks[5], (D, D), jnp.float32) * s, 'bv': jnp.zeros((D,), jnp.float32), 'emb_W': jax.random.normal(ks[6], (TE, 2 * D), jnp.float32) * s, 'emb_b': jnp.zeros((2 * D,), jnp.float32), 'sn_g': jnp.ones((D,), jnp.float32), 'sn_b': jnp.zeros((D,), jnp.float32), 'out_W': jax.random.normal(ks[7], (D, D), jnp.float32) * s, 'out_b': jnp.zeros((D,), jnp.float32)}
    _L2_cond_all = _L2_cond_setup()
    _L2_cond_in = {k: v for k, v in _L2_cond_all.items() if k in ('norm_g', 'norm_b', 'Wq', 'bq', 'Wk', 'bk', 'Wv', 'bv', 'emb_W', 'emb_b', 'sn_g', 'sn_b', 'out_W', 'out_b')}
    del _L2_cond_all

    def _L3_cond_setup():
        import jax, jax.numpy as jnp
        import numpy as np
        DIM = 256
        MLP_RATIO = 4
        EPS = 1e-06

        def rmsnorm(x, w):
            return x * jax.lax.rsqrt(jnp.mean(x * x, axis=-1, keepdims=True) + EPS) * w

        def film(x, cond, w, b):
            ss = cond @ w + b
            scale, shift = jnp.split(ss, 2, axis=-1)
            return x * (1.0 + scale[:, None, :]) + shift[:, None, :]
        key = jax.random.key(seed)
        ks = jax.random.split(key, 16)
        B, N, D = (4, 512, DIM)
        H = D * MLP_RATIO
        s = lambda fan_in: 1.0 / np.sqrt(fan_in)
        return {'x': jax.random.normal(ks[0], (B, N, D), jnp.float32), 'cond': jax.random.normal(ks[1], (B, D), jnp.float32), 'norm1_w': jnp.ones((D,), jnp.float32), 'film1_w': jax.random.normal(ks[2], (D, 2 * D), jnp.float32) * s(D), 'film1_b': jnp.zeros((2 * D,), jnp.float32), 'q_w': jax.random.normal(ks[3], (D, D), jnp.float32) * s(D), 'q_b': jnp.zeros((D,), jnp.float32), 'k_w': jax.random.normal(ks[4], (D, D), jnp.float32) * s(D), 'k_b': jnp.zeros((D,), jnp.float32), 'v_w': jax.random.normal(ks[5], (D, D), jnp.float32) * s(D), 'v_b': jnp.zeros((D,), jnp.float32), 'proj_w': jax.random.normal(ks[6], (D, D), jnp.float32) * s(D), 'proj_b': jnp.zeros((D,), jnp.float32), 'norm2_w': jnp.ones((D,), jnp.float32), 'film2_w': jax.random.normal(ks[7], (D, 2 * D), jnp.float32) * s(D), 'film2_b': jnp.zeros((2 * D,), jnp.float32), 'mlp_w1': jax.random.normal(ks[8], (D, H), jnp.float32) * s(D), 'mlp_b1': jnp.zeros((H,), jnp.float32), 'mlp_w2': jax.random.normal(ks[9], (H, D), jnp.float32) * s(H), 'mlp_b2': jnp.zeros((D,), jnp.float32)}
    _L3_cond_all = _L3_cond_setup()
    _L3_cond_in = {k: v for k, v in _L3_cond_all.items() if k in ('norm1_w', 'film1_w', 'film1_b', 'q_w', 'q_b', 'k_w', 'k_b', 'v_w', 'v_b', 'proj_w', 'proj_b', 'norm2_w', 'film2_w', 'film2_b', 'mlp_w1', 'mlp_b1', 'mlp_w2', 'mlp_b2')}
    del _L3_cond_all
    return {'x': x, 'cond_1024': cond_1024, 'mask_BxSxSx11_ik0': mask_BxSxSx11_ik0, 'L0_cond_W_mod': _L0_cond_in['W_mod'], 'L0_cond_b_mod': _L0_cond_in['b_mod'], 'L0_cond_W_qkv': _L0_cond_in['W_qkv'], 'L0_cond_W_out': _L0_cond_in['W_out'], 'L0_cond_b_out': _L0_cond_in['b_out'], 'L0_cond_W1': _L0_cond_in['W1'], 'L0_cond_b1': _L0_cond_in['b1'], 'L0_cond_W2': _L0_cond_in['W2'], 'L0_cond_b2': _L0_cond_in['b2'], 'L1_cond_W_self': _L1_cond_in['W_self'], 'L1_cond_b_self': _L1_cond_in['b_self'], 'L1_cond_w_bias': _L1_cond_in['w_bias'], 'L1_cond_b_bias': _L1_cond_in['b_bias'], 'L1_cond_Wq': _L1_cond_in['Wq'], 'L1_cond_bq': _L1_cond_in['bq'], 'L1_cond_Wk': _L1_cond_in['Wk'], 'L1_cond_bk': _L1_cond_in['bk'], 'L1_cond_Wout': _L1_cond_in['Wout'], 'L1_cond_bout': _L1_cond_in['bout'], 'L2_cond_norm_g': _L2_cond_in['norm_g'], 'L2_cond_norm_b': _L2_cond_in['norm_b'], 'L2_cond_Wq': _L2_cond_in['Wq'], 'L2_cond_bq': _L2_cond_in['bq'], 'L2_cond_Wk': _L2_cond_in['Wk'], 'L2_cond_bk': _L2_cond_in['bk'], 'L2_cond_Wv': _L2_cond_in['Wv'], 'L2_cond_bv': _L2_cond_in['bv'], 'L2_cond_emb_W': _L2_cond_in['emb_W'], 'L2_cond_emb_b': _L2_cond_in['emb_b'], 'L2_cond_sn_g': _L2_cond_in['sn_g'], 'L2_cond_sn_b': _L2_cond_in['sn_b'], 'L2_cond_out_W': _L2_cond_in['out_W'], 'L2_cond_out_b': _L2_cond_in['out_b'], 'L3_cond_norm1_w': _L3_cond_in['norm1_w'], 'L3_cond_film1_w': _L3_cond_in['film1_w'], 'L3_cond_film1_b': _L3_cond_in['film1_b'], 'L3_cond_q_w': _L3_cond_in['q_w'], 'L3_cond_q_b': _L3_cond_in['q_b'], 'L3_cond_k_w': _L3_cond_in['k_w'], 'L3_cond_k_b': _L3_cond_in['k_b'], 'L3_cond_v_w': _L3_cond_in['v_w'], 'L3_cond_v_b': _L3_cond_in['v_b'], 'L3_cond_proj_w': _L3_cond_in['proj_w'], 'L3_cond_proj_b': _L3_cond_in['proj_b'], 'L3_cond_norm2_w': _L3_cond_in['norm2_w'], 'L3_cond_film2_w': _L3_cond_in['film2_w'], 'L3_cond_film2_b': _L3_cond_in['film2_b'], 'L3_cond_mlp_w1': _L3_cond_in['mlp_w1'], 'L3_cond_mlp_b1': _L3_cond_in['mlp_b1'], 'L3_cond_mlp_w2': _L3_cond_in['mlp_w2'], 'L3_cond_mlp_b2': _L3_cond_in['mlp_b2']}

def reference(x, cond_1024, mask_BxSxSx11_ik0, L0_cond_W_mod, L0_cond_b_mod, L0_cond_W_qkv, L0_cond_W_out, L0_cond_b_out, L0_cond_W1, L0_cond_b1, L0_cond_W2, L0_cond_b2, L1_cond_W_self, L1_cond_b_self, L1_cond_w_bias, L1_cond_b_bias, L1_cond_Wq, L1_cond_bq, L1_cond_Wk, L1_cond_bk, L1_cond_Wout, L1_cond_bout, L2_cond_norm_g, L2_cond_norm_b, L2_cond_Wq, L2_cond_bq, L2_cond_Wk, L2_cond_bk, L2_cond_Wv, L2_cond_bv, L2_cond_emb_W, L2_cond_emb_b, L2_cond_sn_g, L2_cond_sn_b, L2_cond_out_W, L2_cond_out_b, L3_cond_norm1_w, L3_cond_film1_w, L3_cond_film1_b, L3_cond_q_w, L3_cond_q_b, L3_cond_k_w, L3_cond_k_b, L3_cond_v_w, L3_cond_v_b, L3_cond_proj_w, L3_cond_proj_b, L3_cond_norm2_w, L3_cond_film2_w, L3_cond_film2_b, L3_cond_mlp_w1, L3_cond_mlp_b1, L3_cond_mlp_w2, L3_cond_mlp_b2):
    import jax
    import jax.numpy as jnp

    def _L0_cond_ref(x, c, W_mod, b_mod, W_qkv, W_out, b_out, W1, b1, W2, b2):
        import jax, jax.numpy as jnp
        import numpy as np
        B, T, DIM = (4, 256, 256)
        COND = 256
        HEADS, DH = (16, 64)
        INNER = HEADS * DH
        MLP = 1024
        EPS = 1e-05

        def _layernorm(x):
            mu = jnp.mean(x, axis=-1, keepdims=True)
            var = jnp.mean(jnp.square(x - mu), axis=-1, keepdims=True)
            return (x - mu) * jax.lax.rsqrt(var + EPS)

        def _modulate(x, shift, scale):
            return x * (1.0 + scale) + shift

        def _attention(x, W_qkv, W_out, b_out):
            Bq, Tq, _ = x.shape
            qkv = x @ W_qkv
            q, k, v = jnp.split(qkv, 3, axis=-1)
            q = q.reshape(Bq, Tq, HEADS, DH)
            k = k.reshape(Bq, Tq, HEADS, DH)
            v = v.reshape(Bq, Tq, HEADS, DH)
            scale = DH ** (-0.5)
            attn = jnp.einsum('bqhd,bkhd->bhqk', q, k) * scale
            attn = jax.nn.softmax(attn, axis=-1)
            out = jnp.einsum('bhqk,bkhd->bqhd', attn, v).reshape(Bq, Tq, INNER)
            return out @ W_out + b_out

        def _ff(x, W1, b1, W2, b2):
            return jax.nn.gelu(x @ W1 + b1, approximate=False) @ W2 + b2
        mod = jax.nn.silu(c) @ W_mod + b_mod
        sh_msa, sc_msa, g_msa, sh_mlp, sc_mlp, g_mlp = jnp.split(mod, 6, axis=-1)
        x = x + g_msa * _attention(_modulate(_layernorm(x), sh_msa, sc_msa), W_qkv, W_out, b_out)
        x = x + g_mlp * _ff(_modulate(_layernorm(x), sh_mlp, sc_mlp), W1, b1, W2, b2)
        return x

    def _L1_cond_ref(v, q, adj, W_self, b_self, w_bias, b_bias, Wq, bq, Wk, bk, Wout, bout):
        import jax, jax.numpy as jnp
        import numpy as np
        NONGT = 20
        H = 16
        NEG = -9000000000000000.0

        def _gat_attention(self_feat, cond_adj, label_bias, Wq, bq, Wk, bk, Wout, bout):
            B, N, F = self_feat.shape
            ng = min(NONGT, N)
            dh = F // H
            kv = self_feat[:, :ng]
            qh = (self_feat @ Wq.T + bq).reshape(B, N, H, dh)
            kh = (kv @ Wk.T + bk).reshape(B, ng, H, dh)
            aff = jnp.einsum('bnhd,bmhd->bnhm', qh, kh) * (1.0 / np.sqrt(dh))
            mask = cond_adj[:, :, None, :] > 0
            aff = jnp.where(mask, aff, NEG) + label_bias[:, :, None, :]
            w = jax.nn.softmax(aff, axis=-1)
            out_t = jnp.einsum('bnhm,bmf->bnhf', w, kv)
            out = jnp.einsum('bnhf,hgf->bnhg', out_t, Wout) + bout.reshape(H, F // H)
            return out.reshape(B, N, F)

        def _forward(v, q, adj, W_self, b_self, w_bias, b_bias, Wq, bq, Wk, bk, Wout, bout):
            adj_f = adj.astype(jnp.float32)
            exp_v = v
            row_zero = exp_v.sum(-1) == 0
            q_exp = jnp.where(row_zero[..., None], 0.0, q[:, None, :])
            vcq = jnp.concatenate([exp_v, q_exp], axis=-1)
            self_feat = vcq @ W_self.T + b_self
            output = self_feat
            for d in range(2):
                A = adj_f if d == 0 else jnp.swapaxes(adj_f, 1, 2)
                A = A[:, :, :NONGT, :]
                cond = A.sum(-1)
                vb = A @ w_bias + b_bias
                output = output + _gat_attention(self_feat, cond, vb, Wq[d], bq[d], Wk[d], bk[d], Wout[d], bout[d])
            rel = jax.nn.relu(output)
            return exp_v + rel
        return _forward(v, q, adj, W_self, b_self, w_bias, b_bias, Wq, bq, Wk, bk, Wout, bout)

    def _L2_cond_ref(x, emb, gate_msa, norm_g, norm_b, Wq, bq, Wk, bk, Wv, bv, emb_W, emb_b, sn_g, sn_b, out_W, out_b):
        import jax, jax.numpy as jnp
        import numpy as np
        H = 16
        EPS = 1e-05

        def layer_norm(x, g, b):
            mu = jnp.mean(x, axis=-1, keepdims=True)
            var = jnp.var(x, axis=-1, keepdims=True)
            return (x - mu) * jax.lax.rsqrt(var + EPS) * g + b
        B, T, D = x.shape
        dh = D // H
        xn = layer_norm(x, norm_g, norm_b)
        q = (xn @ Wq + bq).reshape(B, T, H, dh)
        k = (xn @ Wk + bk).reshape(B, T, H, dh)
        v = (xn @ Wv + bv).reshape(B, T, H, dh)
        q = jax.nn.softmax(q, axis=-1)
        k = jax.nn.softmax(k, axis=1)
        ctx = jnp.einsum('bnhd,bnhl->bhdl', k, v)
        y = jnp.einsum('bnhd,bhdl->bnhl', q, ctx).reshape(B, T, D)
        emb_out = jax.nn.silu(emb) @ emb_W + emb_b
        scale, shift = jnp.split(emb_out, 2, axis=-1)
        h = layer_norm(y, sn_g, sn_b) * (1.0 + scale) + shift
        h = jax.nn.silu(h) @ out_W + out_b
        return x + gate_msa * h

    def _L3_cond_ref(x, cond, norm1_w, film1_w, film1_b, q_w, q_b, k_w, k_b, v_w, v_b, proj_w, proj_b, norm2_w, film2_w, film2_b, mlp_w1, mlp_b1, mlp_w2, mlp_b2):
        import jax, jax.numpy as jnp
        import numpy as np
        DIM = 256
        MLP_RATIO = 4
        EPS = 1e-06

        def rmsnorm(x, w):
            return x * jax.lax.rsqrt(jnp.mean(x * x, axis=-1, keepdims=True) + EPS) * w

        def film(x, cond, w, b):
            ss = cond @ w + b
            scale, shift = jnp.split(ss, 2, axis=-1)
            return x * (1.0 + scale[:, None, :]) + shift[:, None, :]
        B, N, D = x.shape
        x_in = x
        h = film(rmsnorm(x, norm1_w), cond, film1_w, film1_b)
        Q = h @ q_w + q_b
        K = h @ k_w + k_b
        V = h @ v_w + v_b
        scores = jnp.einsum('bnd,bmd->bnm', Q, K) * D ** (-0.5)
        attn = jax.nn.softmax(scores, axis=-1)
        out = jnp.einsum('bnm,bmd->bnd', attn, V)
        x = x_in + (out @ proj_w + proj_b)
        x_in = x
        h = film(rmsnorm(x, norm2_w), cond, film2_w, film2_b)
        h = jax.nn.gelu(h @ mlp_w1 + mlp_b1, approximate=False) @ mlp_w2 + mlp_b2
        return x_in + h
    x = _L0_cond_ref(x, cond_1024[:, None, :], L0_cond_W_mod, L0_cond_b_mod, L0_cond_W_qkv, L0_cond_W_out, L0_cond_b_out, L0_cond_W1, L0_cond_b1, L0_cond_W2, L0_cond_b2)
    x = _L1_cond_ref(x, cond_1024, mask_BxSxSx11_ik0, L1_cond_W_self, L1_cond_b_self, L1_cond_w_bias, L1_cond_b_bias, L1_cond_Wq, L1_cond_bq, L1_cond_Wk, L1_cond_bk, L1_cond_Wout, L1_cond_bout)
    x = _L2_cond_ref(x, cond_1024[:, None, :], cond_1024[:, None, :], L2_cond_norm_g, L2_cond_norm_b, L2_cond_Wq, L2_cond_bq, L2_cond_Wk, L2_cond_bk, L2_cond_Wv, L2_cond_bv, L2_cond_emb_W, L2_cond_emb_b, L2_cond_sn_g, L2_cond_sn_b, L2_cond_out_W, L2_cond_out_b)
    x = _L3_cond_ref(x, cond_1024, L3_cond_norm1_w, L3_cond_film1_w, L3_cond_film1_b, L3_cond_q_w, L3_cond_q_b, L3_cond_k_w, L3_cond_k_b, L3_cond_v_w, L3_cond_v_b, L3_cond_proj_w, L3_cond_proj_b, L3_cond_norm2_w, L3_cond_film2_w, L3_cond_film2_b, L3_cond_mlp_w1, L3_cond_mlp_b1, L3_cond_mlp_w2, L3_cond_mlp_b2)
    return x

_drawn_inputs = setup_inputs


def setup_inputs(seed=0):
    import zlib

    import numpy as np

    out = dict(_drawn_inputs(seed))
    spreads = {'L1_cond_b_self': (0.0, 0.1),
     'L1_cond_bq': (0.0, 0.1),
     'L1_cond_bk': (0.0, 0.1),
     'L1_cond_bout': (0.0, 0.1),
     'L2_cond_norm_g': (1.0, 0.592),
     'L2_cond_norm_b': (0.0, 0.392),
     'L2_cond_bq': (0.0, 0.8),
     'L2_cond_bk': (0.0, 2.0),
     'L2_cond_bv': (0.0, 0.1),
     'L2_cond_emb_b': (0.0, 0.344),
     'L2_cond_sn_g': (1.0, 0.2),
     'L2_cond_sn_b': (0.0, 0.396),
     'L2_cond_out_b': (0.0, 0.1),
     'L3_cond_norm1_w': (1.0, 0.2),
     'L3_cond_film1_b': (0.0, 0.1),
     'L3_cond_q_b': (0.0, 0.287),
     'L3_cond_k_b': (0.0, 2.0),
     'L3_cond_v_b': (0.0, 0.1),
     'L3_cond_proj_b': (0.0, 0.1),
     'L3_cond_norm2_w': (1.0, 0.2),
     'L3_cond_film2_b': (0.0, 0.1),
     'L3_cond_mlp_b1': (0.0, 0.1),
     'L3_cond_mlp_b2': (0.0, 0.1)}
    factors = {'L0_cond_b_mod': 8.0,
     'L0_cond_W_qkv': 5.244,
     'L0_cond_W_out': 5.061,
     'L0_cond_b_out': 8.0,
     'L0_cond_W1': 2.678,
     'L0_cond_b1': 33.635,
     'L0_cond_b2': 8.0,
     'L2_cond_Wq': 8.0,
     'L2_cond_Wk': 8.0}
    for name, (base, spread) in spreads.items():
        noise = np.random.default_rng([zlib.crc32(name.encode()), seed]).standard_normal(out[name].shape)
        drawn = base * np.exp(spread * noise) if base else spread * noise
        out[name] = jnp.asarray(drawn.astype(out[name].dtype))
    for name, factor in factors.items():
        out[name] = (out[name] * factor).astype(out[name].dtype)
    return out
```

```python
from contextlib import ExitStack

import concourse.bass as bass
from concourse import mybir

F32 = mybir.dt.float32
I32 = mybir.dt.int32
ALU = mybir.AluOpType
ACT = mybir.ActivationFunctionType
AX = mybir.AxisListType

P = 128
BATCH, TOK, DIM = 32, 256, 256
TT = TOK // P
DC = DIM // P
HEADS, DH = 16, 64
INNER = HEADS * DH
GROUPS, GH = 4, 4
PAIRS = HEADS // 2
MLP = 1024
FC = MLP // P
GAT_H, GAT_D, NONGT, LABELS = 16, 16, 20, 11
NEG = 9000000000000000.0
GAT_ROWS = GH * NONGT
EPS = (1e-5, 1e-6)
PIECES, COL_PIECES = 13, 10

PROJ_USES = [("qk", 0), ("v", 0), ("qk", 1)]
for _h in range(HEADS):
    if _h % 2 == 1 and (_h + 3) // 2 < PAIRS:
        PROJ_USES.append(("qk", (_h + 3) // 2))
    if _h % 4 == 2 and _h // 4 + 1 < GROUPS:
        PROJ_USES.append(("v", _h // 4 + 1))
    if _h % 4 == 1 and _h > 1:
        PROJ_USES.append(("ot", _h // 4 - 1))
PROJ_USES.append(("ot", GROUPS - 1))
NPROJ = len(PROJ_USES)

PE_STEPS = ("attn_proj", "norm_t0", "up0", "up1", "up2", "up3", "down", "x2_t", "self_feat", "self_t",
            "gat_kvw", "gat_k", "gat_q0", "gat_s0", "gat_q1", "gat_s1", "gat_e00", "gat_e01", "gat_o0",
            "gat_e10", "gat_e11", "gat_o1", "norm_t1", "lin_q", "lin_k", "lin_v", "lin_k_t", "lin_ctx",
            "lin_q_t", "lin_y", "norm_t2", "lin_out", "norm_t3", "q3", "k3", "v3", "s3", "p3_t", "o3",
            "proj3", "norm_t4", "up3_0", "up3_1", "up3_2", "up3_3", "down3")
ACT_STEPS = ("norm_h0", "gelu0", "gelu1", "gelu2", "gelu3", "x2_c", "self_c", "gat_qc0", "gat_qc1",
             "gat_exp0", "gat_exp1", "gat_ec00", "gat_ec01", "gat_ec10", "gat_ec11", "norm_h1", "lin_qexp",
             "lin_kexp", "lin_k_c", "lin_q_c", "norm_h2", "lin_tanh", "norm_h3", "q3_c", "k3_c", "exp3",
             "p3_c", "o3_c", "norm_h4", "gelu3_0", "gelu3_1", "gelu3_2", "gelu3_3")
DVE_STEPS = ("cols", "x1_gated", "x1", "stats0", "mv0", "z0", "adj_w", "adj_sum", "adj_on", "adj_neg",
             "adj_bias", "x2_gated", "x2", "row_sum", "row_on", "u", "kv_rep", "vbd", "kbd",
             "gat_m0", "gat_b0", "gat_max0", "gat_sub0", "gat_m1", "gat_b1", "gat_max1", "gat_sub1",
             "gat_den0", "gat_rec0", "gat_den1", "gat_rec1", "gat_n0", "gat_acc0", "gat_n1", "gat_acc1", "x3",
             "stats1", "mv1", "z1", "lin_qb", "lin_qmax", "lin_qsub", "lin_kmax", "lin_kmb", "lin_kbias",
             "lin_vb", "lin_qden", "lin_qrec", "lin_krec", "ctx_s", "y", "stats2", "mv2", "z2",
             "silu2", "x4_gated", "x4", "stats3", "mv3", "z3", "v3_b", "max3", "rec3", "p3_n",
             "x5", "stats4", "mv4", "z4", "out")
POOL_STEPS = ("var0", "rstd0", "gb2", "xr2", "acc", "var1", "rstd1", "gob", "xr4", "var2", "rstd2",
              "sq3", "ms3", "var3", "rstd3", "xr5", "sq4", "ms4", "var4", "rstd4", "xr6")

COLS = {}
_n = 0
for _name, _k in (("b1", FC), ("b1_3", FC), ("b_self", DC), ("bq_a", DC), ("bq_b", DC), ("bk_a", DC),
                  ("bk_b", DC), ("norm_g", DC), ("norm_b", DC), ("bk", DC), ("q_b3", DC), ("k_b3", DC),
                  ("mod_b", 2 * 5 * DC), ("mod_w", 5 * DC), ("mod_0", 5 * DC), ("b_bias", 1), ("half", 1)):
    COLS[_name] = (_n, _k)
    _n += _k
NCOLS = _n
WEIGHTS = (("wqkv", 2, 3 * INNER), ("w_out", INNER // P, DIM), ("w1", 2, MLP), ("w2", FC, DIM), ("w_self", 2, DIM),
           ("w_gq", 2, 2 * DIM), ("w_gk", 2, 2 * DIM), ("w_gout", 2, 2 * DIM), ("w_lq", 2, DIM), ("w_lk", 2, DIM),
           ("w_lv", 2, DIM), ("w_lo", 2, DIM), ("w_q3", 2, DIM), ("w_k3", 2, DIM), ("w_v3", 2, DIM), ("w_p3", 2, DIM),
           ("w1_3", 2, MLP), ("w2_3", FC, DIM))
SETUP_DVE = 7
PHASES_AT = {0: (0,), 1: (1,), 2: (2, 3), 3: (4, 5), 4: (6,), 5: (7,), 6: (8,), 7: (9,), 8: (10, 11), 9: (12,), 10: (13,),
             11: (14, 15), 12: (16, 17), 13: (18, 19, 20), 14: (21,), 15: (22,), 16: (23, 24, 25), 17: (26,), 18: (27, 28),
             19: (29,), 20: (30,), 21: (31,), 22: (32,), 23: (33, 34), 24: (35, 36), 25: (37,), 26: (38,), 27: (39,),
             28: (40,), 29: (41,), 30: (42,), 31: (43,), 32: (44,), 33: (45,)}
ROWS = ("b_out", "b2", "b_self", "bout_a", "bout_b", "bq", "bv", "out_b", "v_b3", "proj_b3", "b2_3", "mod_g", "mod_m")
MASKS = {"ident": P, "head_k": 8 * NONGT, "head_v": DIM, "head_c": P}


def build(nc, t, out):
    with ExitStack() as ctx:
        def sb(name, shape, dt=F32):
            return ctx.enter_context(nc.sbuf_tensor(name, shape, dt))

        def sem(name):
            return ctx.enter_context(nc.semaphore(name))

        w = {n: sb("w_" + n, [P, k, c]) for n, k, c in WEIGHTS}
        cols = sb("cols", [P, NCOLS])
        rows = sb("rows", [P, len(ROWS), DIM])
        masks = sb("masks", [P, sum(MASKS.values())])
        w_bias = sb("w_bias", [P, LABELS])
        col_table = sb("col_table", [P, BATCH, 5, 2, DC])
        qs_cols = sb("qs_cols", [P, 3, DC])
        gat_row = sb("gat_row", [P, DIM])
        minus_half = sb("minus_half", [P, TT])
        eps = sb("eps", [P, 2, TT])
        wait_pad = sb("wait_pad", [P, 1])

        def col(name, k=0):
            return cols[:, COLS[name][0] + k:COLS[name][0] + k + 1]

        def row(name):
            return rows[:, ROWS.index(name), :]

        at, m = 0, {}
        for name, width in MASKS.items():
            m[name] = masks[:, at:at + width]
            at += width
        ident = m["ident"]

        def per_tile(ap):
            return ap.unsqueeze(1).broadcast_to([P, TT, ap.shape[-1]])

        xa = sb("xa", [P, TT, DIM])
        x_resid = sb("x_resid", [P, TT, DIM])
        gated_row = sb("gated_row", [P, DIM])
        g_msa = sb("g_msa", [P, DIM])
        za = sb("za", [P, TT, DIM])
        ha = sb("ha", [P, DC, TOK])
        stat_a = sb("stat_a", [P, TT, 6])
        mv_a = sb("mv_a", [P, TT, 2])
        var_a = sb("var_a", [P, TT])
        rstd_a = sb("rstd_a", [P, TT])
        cols_a = sb("cols_a", [P, 2, DC])
        qk = sb("qk", [P, 2, 2, TOK])
        v = sb("v", [P, 2, TT, GH * DH])
        neg_max = sb("neg_max", [P, 2, TT])
        row_sum = sb("row_sum", [P, HEADS, TT])
        row_rec = sb("row_rec", [P, 2, GH * TT])
        probs = sb("probs", [P, 2, TT, TOK])
        probs_t = sb("probs_t", [P, 2, TT, TOK])
        o_n = sb("o_n", [P, 2, TT, GH * DH])
        o_t = sb("o_t", [P, INNER // P, TOK])

        x_odd = sb("x_odd", [P, TT, DIM])
        x_even = sb("x_even", [P, TT, DIM])
        resid = sb("resid", [P, TT, DIM])
        gate_bias = sb("gate_bias", [P, DIM])
        mod_rows = sb("mod_rows", [P, 3, DIM])
        z = sb("z", [P, TT, DIM])
        h = sb("h", [P, DC, TOK])
        g = sb("g", [P, FC, TOK])
        e = sb("e", [P, 2, 2 * 320])
        tmp = sb("tmp", [P, 6, 2 * 256])
        kv_rep = sb("kv_rep", [P, DC, GH, NONGT])
        kbd = sb("kbd", [P, 2, DC, 8 * NONGT])
        vbd = sb("vbd", [P, 2, DIM])
        adj = sb("adj", [P, 2 * TT * NONGT, LABELS], I32)
        adj_v = sb("adj_v", [P, 4, 2 * TT * NONGT])
        cols_b = sb("cols_b", [P, 4, 2, DC])
        stat_b = sb("stat_b", [P, TT, 6])
        mv_b = sb("mv_b", [P, TT, 2])
        var_b = sb("var_b", [P, TT])
        rstd_b = sb("rstd_b", [P, TT])
        ms_b = sb("ms_b", [P, 2, TT])
        small = sb("small", [P, 8, 2 * 16])
        y_out = sb("y_out", [P, TT, DIM])
        adj_mul = e[:, :, :].rearrange("p a b -> p (a b)")[:, 0:2 * TT * NONGT * LABELS].rearrange("p (r l) -> p r l", l=LABELS)
        setup_rows = e[0:BATCH, :, :].rearrange("p a b -> p (a b)")[:, 0:3 * DIM]
        gt = g[:, :, :].rearrange("p a b -> p (a b)").rearrange("p (d t n) -> p d t n", d=2, t=TT)

        def tile(k, rows_=P):
            return tmp[0:rows_, k, :].rearrange("p (a b) -> p a b", a=2)

        ps_s = ctx.enter_context(nc.psum_tensor("ps_s", [P, 2, 512], F32))
        ps_t = ctx.enter_context(nc.psum_tensor("ps_t", [P, 512], F32))
        ps_o = ctx.enter_context(nc.psum_tensor("ps_o", [P, 512], F32))
        ps_p = ctx.enter_context(nc.psum_tensor("ps_p", [P, 512], F32))
        ps_b = ctx.enter_context(nc.psum_tensor("ps_b", [P, 3, 512], F32))

        def bank(k, rows_=P):
            return ps_b[0:rows_, k, :].rearrange("p (a b) -> p a b", a=2)

        small_in = sem("small_in")
        front_w_in = sem("front_w_in")
        back_w_in = sem("back_w_in")
        piece_in = [sem(f"piece_in{k}") for k in range(6)]
        x_in = sem("x_in")
        gate_in = sem("gate_in")
        rows_in = sem("rows_in")
        adj_in = sem("adj_in")
        stored = sem("stored")
        setup_act, setup_dve, setup_pe = sem("setup_act"), sem("setup_dve"), sem("setup_pe")
        stats_a_ready, mv_a_ready, var_a_ready, rstd_a_ready = (sem(n) for n in ("stats_a", "mv_a_s", "var_a_s", "rstd_a_s"))
        za_ready, za_turned, ha_ready, cols_a_ready = (sem(n) for n in ("za_ready", "za_turned", "ha_ready", "cols_a_ready"))
        gated_row_ready, resid_ready = sem("gated_row_ready"), sem("resid_ready")
        projected, proj_copied = sem("projected"), sem("proj_copied")
        scored, max_ready, probs_ready = sem("scored"), sem("max_ready"), sem("probs_ready")
        probs_turned, probs_copied, weighted = sem("probs_turned"), sem("probs_copied"), sem("weighted")
        sum_inverted, o_ready = sem("sum_inverted"), sem("o_ready")
        pe_done, act_done, dve_done, pool_done = (sem(n) for n in ("pe_done", "act_done", "dve_done", "pool_done"))

        def pe_at(name, b):
            return b * len(PE_STEPS) + PE_STEPS.index(name) + 2

        def act_at(name, b):
            return b * len(ACT_STEPS) + ACT_STEPS.index(name) + 2

        def dve_at(name, b):
            return b * len(DVE_STEPS) + DVE_STEPS.index(name) + 2

        def pool_at(name, b):
            return b * len(POOL_STEPS) + POOL_STEPS.index(name) + 2

        def proj_at(kind, k, i):
            return i * NPROJ + PROJ_USES.index((kind, k)) + 1

        scratch = t["scratch"]
        block = ctx.enter_context(nc.Block())

        @block.sync
        def _(sp):
            sp.dma_start(cols[:], t["cols"]).then_inc(small_in, 16)
            sp.dma_start(ha[:, :, 0:BATCH], t["cond_t"]).then_inc(small_in, 16)
            sp.dma_start(rows[:], t["rows"].broadcast_to([P, len(ROWS), DIM])).then_inc(small_in, 16)
            sp.dma_start(masks[:], t["masks"]).then_inc(small_in, 16)
            sp.dma_start(w_bias[:], t["w_bias"].broadcast_to([P, LABELS])).then_inc(small_in, 16)
            for k in range(PIECES):
                if k >= 6:
                    sp.wait_ge(setup_pe, k - 5)
                sp.dma_start(tile(k % 6), t["w_mod"][k]).then_inc(piece_in[k % 6], 16)
            sp.dma_start(xa[:], t["x"][0]).then_inc(x_in, 16)
            for name in ("wqkv", "w_out"):
                sp.dma_start(w[name][:], t[name]).then_inc(front_w_in, 16)
            sp.wait_ge(setup_dve, 3)
            sp.dma_start(scratch, setup_rows).then_inc(stored, 16)
            for name, _, _ in WEIGHTS:
                if name not in ("wqkv", "w_out"):
                    sp.dma_start(w[name][:], t[name]).then_inc(back_w_in, 16)
            sp.wait_ge(stored, 16)

            def body(i, front, back, prelude):
                b = i - 1
                if back:
                    sp.wait_ge(dve_done, b * len(DVE_STEPS) + 1)
                    sp.wait_ge(pool_done, b * len(POOL_STEPS) + 1)
                    sp.dma_start(mod_rows[:, 0:2, :], scratch[bass.ds(b, 1), DIM:3 * DIM].rearrange("a (r c) -> a r c", r=2)
                                 .broadcast_to([P, 2, DIM])).then_inc(rows_in, 16)
                    sp.dma_start(mod_rows[:, 2, :], t["cond"][bass.ds(b, 1), :].broadcast_to([P, DIM])).then_inc(rows_in, 16)
                    sp.dma_start(adj[:], t["adj"][bass.ds(b, 1)].rearrange("a p r l -> (a p) r l")).then_inc(adj_in, 16)
                    sp.wait_ge(dve_done, dve_at("x1", b))
                if front:
                    sp.dma_start(g_msa[:], scratch[bass.ds(i, 1), 0:DIM].broadcast_to([P, DIM])).then_inc(gate_in, 16)
                if prelude:
                    sp.wait_ge(resid_ready, i + 1)
                    sp.wait_ge(za_ready, i + 1)
                    sp.dma_start(xa[:], t["x"][bass.ds(i + 1, 1)].rearrange("a p t c -> (a p) t c")).then_inc(x_in, 16)
                if back:
                    sp.wait_ge(dve_done, dve_at("out", b))
                    sp.dma_start(out[bass.ds(b, 1)].rearrange("a p t c -> (a p) t c"), y_out[:]).then_inc(stored, 16)

            body(0, True, False, True)
            with sp.Fori(1, BATCH - 1) as i:
                body(i, True, True, True)
            body(BATCH - 1, True, True, False)
            body(BATCH, False, True, False)
            sp.wait_ge(stored, 16 * (BATCH + 1))

        @block.tensor
        def _(pe):
            mm = nc.tensor.matmul

            pe.wait_ge(small_in, 16 * 5)
            pe.wait_ge(setup_dve, 2)
            for k in range(PIECES):
                pe.wait_ge(piece_in[k % 6], 16 * (k // 6 + 1))
                src = za if (k < 6 or k in (10, 11)) else ha
                for c in range(DC if k < COL_PIECES else 1):
                    for kk in range(DC):
                        if k < COL_PIECES:
                            n = (k * DC + c) * BATCH
                            last = mm(ps_b[:, n // 512, n % 512:n % 512 + BATCH], tile(k % 6)[:, kk, c * P:c * P + P],
                                      src[:, kk, 0:BATCH], start=(kk == 0), stop=(kk == 1))
                        else:
                            o = (k - COL_PIECES) * DIM
                            last = mm(ps_o[0:BATCH, o:o + DIM] if o < 512 else ps_t[0:BATCH, 0:DIM],
                                      src[:, kk, 0:BATCH], tile(k % 6)[:, kk, :], start=(kk == 0), stop=(kk == 1))
                last.then_inc(setup_pe, 1)
            pe.wait_ge(setup_dve, SETUP_DVE)
            pe.wait_ge(front_w_in, 32)
            pe.nop().then_inc(pe_done, 1)

            def turn(dst, src, width=P):
                for a in range(2):
                    for c in range(2):
                        last = nc.tensor.transpose(dst[:, c, a * P:a * P + P], src[:, a, c * P:c * P + P], ident)
                return last

            def to_tokens(dst, src, weights, width=DIM):
                kk = src.shape[1]
                for tt in range(TT):
                    for k in range(kk):
                        last = mm(dst[:, tt, 0:width], src[:, k, tt * P:tt * P + P], weights[:, k, :],
                                  start=(k == 0), stop=(k == kk - 1))
                return last

            def to_features(dst, src, weights, first=0):
                kk = src.shape[1]
                for c in range(2):
                    for k in range(kk):
                        last = mm(dst[:, c, :], weights[:, k, first + c * P:first + c * P + P], src[:, k, :],
                                  start=(k == 0), stop=(k == kk - 1))
                return last

            def prelude(i):
                pe.wait_ge(za_ready, i + 1)
                if not (isinstance(i, int) and i == 0):
                    pe.wait_ge(proj_copied, proj_at("ot", 2, i - 1))
                turn(ps_p[:].rearrange("p (a b) -> p a b", a=2), za).then_inc(za_turned, 1)

            def proj(kind, k, i, guard=True):
                n = PROJ_USES.index((kind, k))
                bank_p = ps_p[:].rearrange("p (a b) -> p a b", a=2)
                if (kind, k) == ("qk", 0):
                    pe.wait_ge(ha_ready, i + 1)
                if not (isinstance(i, int) and i == 0 and n == 0):
                    pe.wait_ge(proj_copied, i * NPROJ + n)
                if kind == "qk":
                    for c in range(2):
                        for kk in range(DC):
                            last = mm(bank_p[:, c, :], w["wqkv"][:, kk, c * INNER + k * P:c * INNER + k * P + P],
                                      ha[:, kk, :], start=(kk == 0), stop=(kk == 1))
                elif kind == "v":
                    last = to_tokens(bank_p, ha, w["wqkv"][:, :, 2 * INNER + k * 256:2 * INNER + (k + 1) * 256])
                else:
                    pe.wait_ge(o_ready, i * GROUPS + k + 1)
                    if k == GROUPS - 1 and guard:
                        pe.wait_ge(ha_ready, i + 2)
                    last = turn(bank_p, o_n[:, k % 2])
                last.then_inc(projected, 1)

            def scores(hd, i):
                pair, r = hd // 2, hd % 2 * DH
                pe.wait_ge(proj_copied, proj_at("qk", pair, i))
                if hd >= 2:
                    pe.wait_ge(probs_ready, i * HEADS + hd - 1)
                elif not (isinstance(i, int) and i == 0):
                    pe.wait_ge(probs_ready, i * HEADS)
                for tt in range(TT):
                    last = mm(ps_s[:, hd % 2, tt * TOK:(tt + 1) * TOK], qk[r:r + DH, pair % 2, 0, tt * P:tt * P + P],
                              qk[r:r + DH, pair % 2, 1, :], start=True, stop=True)
                last.then_inc(scored, 1)

            def turn_probs(hd, i):
                pe.wait_ge(probs_ready, i * HEADS + hd + 1)
                if not (isinstance(i, int) and i == 0 and hd == 0):
                    pe.wait_ge(probs_copied, i * HEADS + hd)
                turn(ps_t[:].rearrange("p (a b) -> p a b", a=2), probs[:, hd % 2]).then_inc(probs_turned, 1)

            def weigh(hd, i):
                grp = hd // GH
                pe.wait_ge(probs_copied, i * HEADS + hd + 1)
                if hd % GH == 0:
                    pe.wait_ge(proj_copied, proj_at("v", grp, i))
                    if not (isinstance(i, int) and i == 0 and grp == 0):
                        pe.wait_ge(o_ready, i * GROUPS + grp)
                for tt in range(TT):
                    for kt in range(TT):
                        o = (tt * GH + hd % GH) * DH
                        last = mm(ps_o[:, o:o + DH], probs_t[:, hd % 2, kt, tt * P:tt * P + P],
                                  v[:, grp % 2, kt, hd % GH * DH:hd % GH * DH + DH], start=(kt == 0), stop=(kt == 1))
                last.then_inc(weighted, 1)

            def attn_proj(b):
                pe.wait_ge(proj_copied, proj_at("ot", GROUPS - 1, b))
                pe.wait_ge(act_done, b * len(ACT_STEPS) + 1)
                to_tokens(bank(0), o_t, w["w_out"]).then_inc(pe_done, 1)

            def norm_t(n, b, k, engine_sem, free):
                pe.wait_ge(dve_done, dve_at(f"z{n}", b))
                pe.wait_ge(engine_sem, free)
                turn(bank(k), z).then_inc(pe_done, 1)

            def up(j, b, k, name, weights, engine_sem, free):
                if j == 0:
                    pe.wait_ge(act_done, act_at(name, b))
                pe.wait_ge(engine_sem, free)
                to_features(bank(k), h, weights, first=j * 256).then_inc(pe_done, 1)

            def phases(b):
                A, D = (lambda n: act_at(n, b)), (lambda n: dve_at(n, b))
                prev = b * len(DVE_STEPS) + 1
                w1, w1_3 = w["w1"], w["w1_3"]

                def p0(): attn_proj(b)
                def p1(): norm_t(0, b, 1, act_done, b * len(ACT_STEPS) + 1)
                def p2(): up(0, b, 2, "norm_h0", w1, dve_done, prev)
                def p3(): up(1, b, 0, "", w1, dve_done, D("x1_gated"))
                def p4(): up(2, b, 1, "", w1, act_done, A("norm_h0"))
                def p5(): up(3, b, 2, "", w1, act_done, A("gelu0"))

                def p6():
                    pe.wait_ge(act_done, A("gelu3"))
                    to_tokens(bank(0), g, w["w2"]).then_inc(pe_done, 1)

                def p7():
                    pe.wait_ge(dve_done, D("x2"))
                    pe.wait_ge(act_done, A("gelu2"))
                    turn(bank(1), x_even).then_inc(pe_done, 1)

                def p8():
                    pe.wait_ge(act_done, A("x2_c"))
                    to_tokens(bank(2), tile(0), w["w_self"]).then_inc(pe_done, 1)

                def p9():
                    pe.wait_ge(dve_done, D("u"))
                    turn(bank(0), tile(1)).then_inc(pe_done, 1)

                def p10():
                    pe.wait_ge(dve_done, D("kv_rep"))
                    for d in range(2):
                        for k in range(DC):
                            last = mm(bank(1, GAT_ROWS)[:, d, :], kv_rep[:, k].rearrange("p a b -> p (a b)"),
                                      w["w_gout"][:, k, d * DIM:(d + 1) * DIM], start=(k == 0), stop=(k == 1))
                    last.then_inc(pe_done, 1)

                def p11():
                    pe.wait_ge(act_done, A("self_c"))
                    for d in range(2):
                        for c in range(DC):
                            for k in range(DC):
                                o = (d * DC + c) * NONGT
                                last = mm(ps_b[:, 2, o:o + NONGT], w["w_gk"][:, k, d * DIM + c * P:d * DIM + c * P + P],
                                          tile(2)[:, k, 0:NONGT], start=(k == 0), stop=(k == 1))
                    last.then_inc(pe_done, 1)

                def gat_q(d, free=None):
                    if d == 1:
                        pe.wait_ge(act_done, A("gat_qc0"))
                    to_features(bank(0), tile(2), w["w_gq"], first=d * DIM).then_inc(pe_done, 1)

                def gat_s(d):
                    pe.wait_ge(act_done, A(f"gat_qc{d}"))
                    pe.wait_ge(dve_done, D("kbd") if d == 0 else D("gat_m0"))
                    for tt in range(TT):
                        for c in range(DC):
                            last = mm(ps_b[:, 1 + tt, c * 160:(c + 1) * 160], tile(3 + d)[:, c, tt * P:tt * P + P],
                                      kbd[:, d, c, :], start=True, stop=True)
                    last.then_inc(pe_done, 1)

                def gat_e(d, tt):
                    pe.wait_ge(act_done, A(f"gat_exp{d}"))
                    if (d, tt) == (0, 0):
                        pe.wait_ge(act_done, A("gat_qc1"))
                    elif (d, tt) == (0, 1):
                        pe.wait_ge(dve_done, D("gat_m1"))
                    else:
                        pe.wait_ge(act_done, A(f"gat_ec0{tt}"))
                    for k in range(GROUPS):
                        last = nc.tensor.transpose(ps_b[0:GAT_ROWS, tt, k * P:(k + 1) * P],
                                                   e[:, d, tt * 320 + k * GAT_ROWS:tt * 320 + (k + 1) * GAT_ROWS], ident)
                    last.then_inc(pe_done, 1)

                def gat_o(d):
                    pe.wait_ge(act_done, A(f"gat_ec{d}1"))
                    if d == 1:
                        pe.wait_ge(dve_done, D("gat_n0"))
                    for tt in range(TT):
                        for k in range(GROUPS):
                            last = mm(bank(2)[:, tt, k * 64:(k + 1) * 64], gt[0:GAT_ROWS, d, tt, k * P:(k + 1) * P],
                                      vbd[0:GAT_ROWS, d, k * 64:(k + 1) * 64], start=True, stop=True)
                    last.then_inc(pe_done, 1)

                def p22():
                    norm_t(1, b, 0, act_done, A("gat_ec10"))

                def p23():
                    pe.wait_ge(act_done, A("norm_h1"))
                    to_tokens(bank(1), h, w["w_lq"]).then_inc(pe_done, 1)

                def p24():
                    pe.wait_ge(dve_done, D("gat_n1"))
                    to_features(bank(2), h, w["w_lk"]).then_inc(pe_done, 1)

                def p25():
                    to_tokens(bank(0), h, w["w_lv"]).then_inc(pe_done, 1)

                def p26():
                    pe.wait_ge(act_done, A("lin_kexp"))
                    pe.wait_ge(dve_done, D("lin_qb"))
                    turn_back(bank(1), tile(2)).then_inc(pe_done, 1)

                def p27():
                    pe.wait_ge(act_done, A("lin_k_c"))
                    pe.wait_ge(dve_done, D("lin_vb"))
                    for c in range(DC):
                        for tt in range(TT):
                            last = mm(ps_b[:, 2, c * P:(c + 1) * P], tile(3)[:, tt, c * P:(c + 1) * P],
                                      tile(1)[:, tt, c * P:(c + 1) * P], start=(tt == 0), stop=(tt == 1))
                    last.then_inc(pe_done, 1)

                def p28():
                    pe.wait_ge(act_done, A("lin_qexp"))
                    turn(bank(0), tile(0)).then_inc(pe_done, 1)

                def p29():
                    pe.wait_ge(act_done, A("lin_q_c"))
                    pe.wait_ge(dve_done, D("ctx_s"))
                    for tt in range(TT):
                        for c in range(DC):
                            last = mm(bank(1)[:, tt, c * P:(c + 1) * P], tile(4)[:, c, tt * P:(tt + 1) * P],
                                      tmp[:, 5, c * P:(c + 1) * P], start=True, stop=True)
                    last.then_inc(pe_done, 1)

                def p30(): norm_t(2, b, 2, dve_done, D("ctx_s"))

                def p31():
                    pe.wait_ge(dve_done, D("silu2"))
                    to_tokens(bank(0), tile(2), w["w_lo"]).then_inc(pe_done, 1)

                def p32(): norm_t(3, b, 1, dve_done, D("y"))

                def p33():
                    pe.wait_ge(act_done, A("norm_h3"))
                    to_features(bank(2), h, w["w_q3"]).then_inc(pe_done, 1)

                def p34():
                    pe.wait_ge(dve_done, D("x4_gated"))
                    to_features(bank(0), h, w["w_k3"]).then_inc(pe_done, 1)

                def p35():
                    to_tokens(bank(1), h, w["w_v3"]).then_inc(pe_done, 1)

                def p36():
                    pe.wait_ge(act_done, A("k3_c"))
                    for tt in range(TT):
                        for k in range(DC):
                            last = mm(bank(2)[:, tt, :], tile(0)[:, k, tt * P:(tt + 1) * P], tile(1)[:, k, :],
                                      start=(k == 0), stop=(k == 1))
                    last.then_inc(pe_done, 1)

                def p37():
                    pe.wait_ge(dve_done, D("p3_n"))
                    turn(bank(0), tile(3)).then_inc(pe_done, 1)

                def p38():
                    pe.wait_ge(act_done, A("p3_c"))
                    pe.wait_ge(dve_done, D("v3_b"))
                    for c in range(DC):
                        for kt in range(TT):
                            last = mm(bank(1)[:, c, :], tile(2)[:, kt, c * P:(c + 1) * P], tile(4)[:, kt, :],
                                      start=(kt == 0), stop=(kt == 1))
                    last.then_inc(pe_done, 1)

                def p39():
                    pe.wait_ge(act_done, A("o3_c"))
                    to_tokens(bank(2), tile(5), w["w_p3"]).then_inc(pe_done, 1)

                def p40(): norm_t(4, b, 0, act_done, A("p3_c"))
                def p41(): up(0, b, 1, "norm_h4", w1_3, act_done, A("o3_c"))
                def p42(): up(1, b, 2, "", w1_3, dve_done, D("x5"))
                def p43(): up(2, b, 0, "", w1_3, act_done, A("norm_h4"))
                def p44(): up(3, b, 1, "", w1_3, act_done, A("gelu3_0"))

                def p45():
                    pe.wait_ge(act_done, A("gelu3_3"))
                    to_tokens(bank(2), g, w["w2_3"]).then_inc(pe_done, 1)

                return [p0, p1, p2, p3, p4, p5, p6, p7, p8, p9, p10, p11, lambda: gat_q(0), lambda: gat_s(0),
                        lambda: gat_q(1), lambda: gat_s(1), lambda: gat_e(0, 0), lambda: gat_e(0, 1), lambda: gat_o(0),
                        lambda: gat_e(1, 0), lambda: gat_e(1, 1), lambda: gat_o(1), p22, p23, p24, p25, p26, p27, p28,
                        p29, p30, p31, p32, p33, p34, p35, p36, p37, p38, p39, p40, p41, p42, p43, p44, p45]

            def turn_back(dst, src):
                for c in range(DC):
                    for tt in range(TT):
                        last = nc.tensor.transpose(dst[:, tt, c * P:(c + 1) * P], src[:, c, tt * P:(tt + 1) * P], ident)
                return last

            def body(i, front, back, pre):
                b = i - 1
                back_phases = phases(b) if back else []
                if front:
                    proj("qk", 0, i)
                    proj("v", 0, i)
                for n in PHASES_AT[0]:
                    if back:
                        back_phases[n]()
                if front:
                    scores(0, i)
                    proj("qk", 1, i)
                for hd in range(HEADS):
                    if front and hd + 1 < HEADS:
                        scores(hd + 1, i)
                    for n in PHASES_AT[2 * hd + 1] if back else ():
                        back_phases[n]()
                    if front:
                        turn_probs(hd, i)
                    for n in PHASES_AT[2 * hd + 2] if back else ():
                        back_phases[n]()
                    if front:
                        if hd:
                            weigh(hd - 1, i)
                        if hd % 2 == 1 and (hd + 3) // 2 < PAIRS:
                            proj("qk", (hd + 3) // 2, i)
                        if hd % 4 == 2 and hd // 4 + 1 < GROUPS:
                            proj("v", hd // 4 + 1, i)
                        if hd % 4 == 1 and hd > 1:
                            proj("ot", hd // 4 - 1, i)
                        if hd == 14 and pre:
                            prelude(i + 1)
                if front:
                    weigh(HEADS - 1, i)
                for n in PHASES_AT[33] if back else ():
                    back_phases[n]()
                if front:
                    proj("ot", GROUPS - 1, i, guard=pre)

            prelude(0)
            body(0, True, False, True)
            pe.wait_ge(back_w_in, 16 * (len(WEIGHTS) - 2))
            with pe.Fori(1, BATCH - 1) as i:
                body(i, True, True, True)
            body(BATCH - 1, True, True, False)
            body(BATCH, False, True, False)

        @block.scalar
        def _(act):
            go = nc.scalar.activation
            act.wait_ge(small_in, 16 * 5)
            go(za[:, :, 0:BATCH], ha[:, :, 0:BATCH], ACT.Tanh, scale=0.5).then_inc(setup_act, 1)
            for d, name in enumerate(("bq_a", "bq_b")):
                go(qs_cols[:, d, :], cols[:, COLS[name][0]:COLS[name][0] + DC], ACT.Copy, scale=GAT_D ** -0.5)
            go(qs_cols[:, 2, :], cols[:, COLS["q_b3"][0]:COLS["q_b3"][0] + DC], ACT.Copy, scale=DIM ** -0.5).then_inc(act_done, 1)

            def affine(dst, src, scale_cols, shift_cols):
                for c in range(DC):
                    last = go(dst[:, c, :], src[:, c, :], ACT.Identity, bias=shift_cols[:, c:c + 1], scale=scale_cols[:, c:c + 1])
                return last

            def prelude(i):
                act.wait_ge(za_turned, i + 1)
                act.wait_ge(cols_a_ready, i + 1)
                if isinstance(i, int) and i == 0:
                    act.wait_ge(setup_pe, PIECES)
                else:
                    act.wait_ge(projected, proj_at("qk", PAIRS - 1, i - 1))
                affine(ha, ps_p[:].rearrange("p (a b) -> p a b", a=2), cols_a[:, 0], cols_a[:, 1]).then_inc(ha_ready, 1)

            def copy_proj(kind, k, i):
                act.wait_ge(projected, proj_at(kind, k, i))
                if kind == "qk":
                    if k >= 2:
                        act.wait_ge(scored, i * HEADS + 2 * k - 2)
                    elif not (isinstance(i, int) and i == 0):
                        act.wait_ge(scored, i * HEADS)
                    go(qk[:, k % 2, 0, :], ps_p[:, 0:TOK], ACT.Copy, scale=DH ** -0.5)
                    last = go(qk[:, k % 2, 1, :], ps_p[:, TOK:2 * TOK], ACT.Copy)
                elif kind == "v":
                    if k >= 2:
                        act.wait_ge(weighted, i * HEADS + GH * (k - 1))
                    elif not (isinstance(i, int) and i == 0):
                        act.wait_ge(weighted, i * HEADS)
                    last = go(v[:, k % 2], ps_p[:].rearrange("p (a b) -> p a b", a=2), ACT.Copy)
                else:
                    if not isinstance(i, int) or i > 0:
                        act.wait_ge(pe_done, pe_at("attn_proj", i - 1))
                    last = go(o_t[:, 2 * k:2 * k + 2, :], ps_p[:].rearrange("p (a b) -> p a b", a=2), ACT.Copy)
                last.then_inc(proj_copied, 1)

            def exps(hd, i):
                act.wait_ge(max_ready, i * HEADS + hd + 1)
                if hd >= 2:
                    act.wait_ge(probs_turned, i * HEADS + hd - 1)
                elif not (isinstance(i, int) and i == 0):
                    act.wait_ge(probs_turned, i * HEADS)
                    act.wait_ge(sum_inverted, i * GROUPS)
                for tt in range(TT):
                    last = go(probs[:, hd % 2, tt, :], ps_s[:, hd % 2, tt * TOK:(tt + 1) * TOK], ACT.Exp,
                              bias=neg_max[:, hd % 2, tt:tt + 1], accum_out=row_sum[:, hd, tt:tt + 1])
                last.then_inc(probs_ready, 1)

            def phases(b):
                PE, D = (lambda n: pe_at(n, b)), (lambda n: dve_at(n, b))
                f = {}

                def norm_h(n, k):
                    def run():
                        act.wait_ge(pe_done, PE(f"norm_t{n}"))
                        if n == 0:
                            act.wait_ge(dve_done, D("cols"))
                        if n == 1:
                            s, o = COLS["norm_g"][0], COLS["norm_b"][0]
                            affine(h, bank(k), cols[:, s:s + DC], cols[:, o:o + DC]).then_inc(act_done, 1)
                        else:
                            j = {0: 0, 2: 1, 3: 2, 4: 3}[n]
                            affine(h, bank(k), cols_b[:, j, 0], cols_b[:, j, 1]).then_inc(act_done, 1)
                    return run

                def gelu(j, k, step, bias):
                    def run():
                        act.wait_ge(pe_done, PE(step))
                        for c in range(2):
                            last = go(g[:, 2 * j + c, :], bank(k)[:, c, :], ACT.Gelu, bias=col(bias, 2 * j + c))
                        last.then_inc(act_done, 1)
                    return run

                def copy(dst, k, step, waits=()):
                    def run():
                        act.wait_ge(pe_done, PE(step))
                        go(dst, bank(k), ACT.Copy).then_inc(act_done, 1)
                    return run

                def self_c():
                    act.wait_ge(pe_done, PE("self_t"))
                    for c in range(DC):
                        last = go(tile(2)[:, c, :], bank(0)[:, c, :], ACT.Identity, bias=col("b_self", c))
                    last.then_inc(act_done, 1)

                def query(dst, k, step, j, scale):
                    def run():
                        act.wait_ge(pe_done, PE(step))
                        for c in range(DC):
                            last = go(dst[:, c, :], bank(k)[:, c, :], ACT.Identity, bias=qs_cols[:, j, c:c + 1], scale=scale)
                        last.then_inc(act_done, 1)
                    return run

                def gat_exp(d):
                    def run():
                        act.wait_ge(dve_done, D(f"gat_sub{d}"))
                        go(e[:, d, :], e[:, d, :], ACT.Exp).then_inc(act_done, 1)
                    return run

                def gat_ec(d, tt):
                    def run():
                        act.wait_ge(pe_done, PE(f"gat_e{d}{tt}"))
                        go(gt[0:GAT_ROWS, d, tt, :], ps_b[0:GAT_ROWS, tt, :], ACT.Copy).then_inc(act_done, 1)
                    return run

                def lin_qexp():
                    act.wait_ge(dve_done, D("lin_qsub"))
                    go(tile(0), tile(0), ACT.Exp).then_inc(act_done, 1)

                def lin_kexp():
                    act.wait_ge(pe_done, PE("lin_k"))
                    act.wait_ge(dve_done, D("lin_kbias"))
                    for c in range(DC):
                        last = go(tile(2)[:, c, :], bank(2)[:, c, :], ACT.Exp, bias=small[:, 4, c:c + 1],
                                  accum_out=small[:, 5, c:c + 1])
                    last.then_inc(act_done, 1)

                def lin_tanh():
                    act.wait_ge(act_done, act_at("norm_h2", b))
                    go(tile(1), h[:], ACT.Tanh, scale=0.5).then_inc(act_done, 1)

                def k3_c():
                    act.wait_ge(pe_done, PE("k3"))
                    for c in range(DC):
                        last = go(tile(1)[:, c, :], bank(0)[:, c, :], ACT.Identity, bias=col("k_b3", c))
                    last.then_inc(act_done, 1)

                def exp3():
                    act.wait_ge(pe_done, PE("s3"))
                    act.wait_ge(dve_done, D("max3"))
                    for tt in range(TT):
                        last = go(tile(3)[:, tt, :], bank(2)[:, tt, :], ACT.Exp, bias=small[:, 6, tt:tt + 1],
                                  accum_out=small[:, 7, tt:tt + 1])
                    last.then_inc(act_done, 1)

                return {1: [norm_h(0, 1)], 2: [gelu(0, 2, "up0", "b1")], 3: [gelu(1, 0, "up1", "b1")],
                        4: [gelu(2, 1, "up2", "b1")], 5: [gelu(3, 2, "up3", "b1")], 7: [copy(tile(0), 1, "x2_t")],
                        9: [self_c], 12: [query(tile(3), 0, "gat_q0", 0, GAT_D ** -0.5)],
                        14: [query(tile(4), 0, "gat_q1", 1, GAT_D ** -0.5)], 15: [gat_exp(0), gat_exp(1)],
                        16: [gat_ec(0, 0)], 17: [gat_ec(0, 1)], 19: [gat_ec(1, 0)], 20: [gat_ec(1, 1)],
                        22: [norm_h(1, 0)], 23: [lin_qexp], 24: [lin_kexp], 26: [copy(tile(3), 1, "lin_k_t")],
                        28: [copy(tile(4), 0, "lin_q_t")], 30: [norm_h(2, 2), lin_tanh], 32: [norm_h(3, 1)],
                        33: [query(tile(0), 2, "q3", 2, DIM ** -0.5)], 34: [k3_c], 36: [exp3],
                        37: [copy(tile(4), 0, "p3_t")], 38: [copy(tile(5), 1, "o3")], 40: [norm_h(4, 0)],
                        41: [gelu(0, 1, "up3_0", "b1_3")], 42: [gelu(1, 2, "up3_1", "b1_3")],
                        43: [gelu(2, 0, "up3_2", "b1_3")], 44: [gelu(3, 1, "up3_3", "b1_3")]}

            def body(i, front, back, pre):
                b = i - 1
                back_phases = phases(b) if back else {}

                def run(slot):
                    for n in PHASES_AT[slot]:
                        for f in back_phases.get(n, ()):
                            f()
                if front:
                    copy_proj("qk", 0, i)
                    copy_proj("v", 0, i)
                run(0)
                if front:
                    exps(0, i)
                    copy_proj("qk", 1, i)
                for hd in range(HEADS):
                    if front and hd + 1 < HEADS:
                        exps(hd + 1, i)
                    run(2 * hd + 1)
                    run(2 * hd + 2)
                    if front:
                        if hd % 2 == 1 and (hd + 3) // 2 < PAIRS:
                            copy_proj("qk", (hd + 3) // 2, i)
                        if hd % 4 == 2 and hd // 4 + 1 < GROUPS:
                            copy_proj("v", hd // 4 + 1, i)
                        if hd % 4 == 1 and hd > 1:
                            copy_proj("ot", hd // 4 - 1, i)
                        if hd == 14 and pre:
                            prelude(i + 1)
                run(33)
                if front:
                    copy_proj("ot", GROUPS - 1, i)

            prelude(0)
            body(0, True, False, True)
            with act.Fori(1, BATCH - 1) as i:
                body(i, True, True, True)
            body(BATCH - 1, True, True, False)
            body(BATCH, False, True, False)

        @block.vector
        def _(dve):
            V = nc.vector
            tt_ = V.tensor_tensor

            dve.wait_ge(setup_act, 1)
            dve.wait_ge(small_in, 16 * 5)
            V.scalar_tensor_tensor(za[:, :, 0:BATCH], za[:, :, 0:BATCH], 1.0, ha[:, :, 0:BATCH], ALU.add, ALU.mult).then_inc(setup_dve, 1)
            dve.wait_ge(setup_dve, 1)
            V.tensor_scalar(za[:, :, 0:BATCH], za[:, :, 0:BATCH], 0.5, None, ALU.mult).then_inc(setup_dve, 1)
            dve.wait_ge(setup_pe, PIECES)
            tt_(setup_rows[:, 0:DIM], ps_o[0:BATCH, 0:DIM], row("mod_g")[0:BATCH], ALU.add)
            tt_(setup_rows[:, DIM:2 * DIM], ps_o[0:BATCH, DIM:2 * DIM], row("mod_m")[0:BATCH], ALU.add)
            V.tensor_copy(setup_rows[:, 2 * DIM:], ps_t[0:BATCH, 0:DIM]).then_inc(setup_dve, 1)
            gf = g[:].rearrange("p a b -> p (a b)")
            mod = gf[:, 0:5 * 2 * DC * BATCH]
            nb = COLS["mod_b"][0]
            for lo_, hi_, k in ((0, 512, 0), (512, 640, 1)):
                n0, n1 = lo_ // BATCH, hi_ // BATCH
                last = tt_(mod[:, lo_:hi_].rearrange("p (n b) -> p n b", b=BATCH),
                           ps_b[:, k, 0:hi_ - lo_].rearrange("p (n b) -> p n b", b=BATCH),
                           cols[:, nb + n0:nb + n1].unsqueeze(2).broadcast_to([P, n1 - n0, BATCH]), ALU.add)
            last.then_inc(setup_dve, 1)
            dve.wait_ge(setup_dve, 4)
            mod4 = mod.rearrange("p (n s c b) -> p n s c b", n=5, s=2, c=DC)
            for n in range(5):
                for c in range(DC):
                    jw, j0 = COLS["mod_w"][0] + n * DC + c, COLS["mod_0"][0] + n * DC + c
                    V.tensor_scalar(col_table[:, :, n, 0, c], mod4[:, n, 0, c, :], 1.0, cols[:, jw:jw + 1], ALU.add, ALU.mult)
                    last = V.tensor_scalar(gf[:, 1024 + (n * DC + c) * BATCH:1024 + (n * DC + c + 1) * BATCH], mod4[:, n, 0, c, :],
                                           1.0, cols[:, j0:j0 + 1], ALU.add, ALU.mult)
            last.then_inc(setup_dve, 1)
            dve.wait_ge(setup_dve, 5)
            for n in range(5):
                for c in range(DC):
                    tt_(col_table[:, :, n, 1, c], gf[:, 1024 + (n * DC + c) * BATCH:1024 + (n * DC + c + 1) * BATCH],
                        mod4[:, n, 1, c, :], ALU.add)
            V.memset(minus_half[:], -0.5)
            V.memset(eps[:, 0, :], EPS[0])
            V.memset(eps[:, 1, :], EPS[1])
            last = tt_(gat_row[:], row("bout_a"), row("bout_b"), ALU.add)
            last.then_inc(setup_dve, 1)
            dve.wait_ge(setup_dve, 6)
            tt_(gat_row[:], gat_row[:], row("b_self"), ALU.add).then_inc(setup_dve, 1)
            dve.wait_ge(setup_dve, SETUP_DVE)
            V.memset(small[:], 0.0).then_inc(dve_done, 1)

            def norm_stats(dst, mv, x, s_stats):
                for tt in range(TT):
                    last = V.bn_stats(dst[:, tt, :], x[:, tt, :])
                return last

            def norm_mv(dst, mv):
                for tt in range(TT):
                    last = V.bn_aggr(mv[:, tt, :], dst[:, tt, :])
                return last

            def norm_z(dst, x, mv, rstd, centre=True):
                for tt in range(TT):
                    if centre:
                        last = V.tensor_scalar(dst[:, tt, :], x[:, tt, :], mv[:, tt, 0:1], rstd[:, tt:tt + 1], ALU.subtract, ALU.mult)
                    else:
                        last = V.tensor_scalar(dst[:, tt, :], x[:, tt, :], rstd[:, tt:tt + 1], None, ALU.mult)
                return last

            def prelude_stats(i):
                dve.wait_ge(x_in, 16 * i + 16)
                norm_stats(stat_a, mv_a, xa, None).then_inc(stats_a_ready, 1)
                dve.wait_ge(stats_a_ready, i + 1)
                V.memset(wait_pad[:], 0.0)
                norm_mv(stat_a, mv_a).then_inc(mv_a_ready, 1)

            def prelude_z(i):
                if isinstance(i, int) and i == 0:
                    dve.wait_ge(setup_dve, SETUP_DVE)
                else:
                    dve.wait_ge(ha_ready, i)
                V.tensor_copy(cols_a[:], col_table[:, i, 0, :, :]).then_inc(cols_a_ready, 1)
                dve.wait_ge(rstd_a_ready, i + 1)
                if not (isinstance(i, int) and i == 0):
                    dve.wait_ge(za_turned, i)
                else:
                    dve.wait_ge(setup_pe, PIECES)
                norm_z(za, xa, mv_a, rstd_a).then_inc(za_ready, 1)

            def maxes(hd, i):
                dve.wait_ge(scored, i * HEADS + hd + 1)
                if hd >= 2:
                    dve.wait_ge(probs_ready, i * HEADS + hd - 1)
                elif not (isinstance(i, int) and i == 0):
                    dve.wait_ge(probs_ready, i * HEADS)
                V.tensor_reduce(neg_max[:, hd % 2, :], ps_s[:, hd % 2, :].rearrange("p (a b) -> p a b", a=2), AX.X, ALU.max,
                                negate=True).then_inc(max_ready, 1)

            def copy_probs(hd, i):
                dve.wait_ge(probs_turned, i * HEADS + hd + 1)
                if hd >= 2:
                    dve.wait_ge(weighted, i * HEADS + hd - 1)
                elif not (isinstance(i, int) and i == 0):
                    dve.wait_ge(weighted, i * HEADS)
                V.tensor_copy(probs_t[:, hd % 2], ps_t[:].rearrange("p (a b) -> p a b", a=2)).then_inc(probs_copied, 1)

            def normalise(grp, i):
                dve.wait_ge(probs_ready, i * HEADS + GH * grp + GH)
                V.reciprocal(row_rec[:, grp % 2, :], row_sum[:, GH * grp:GH * grp + GH, :].rearrange("p a b -> p (a b)")).then_inc(sum_inverted, 1)
                dve.wait_ge(sum_inverted, i * GROUPS + grp + 1)
                dve.wait_ge(weighted, i * HEADS + GH * grp + GH)
                if grp >= 2:
                    dve.wait_ge(projected, proj_at("ot", grp - 2, i))
                elif not (isinstance(i, int) and i == 0):
                    dve.wait_ge(projected, i * NPROJ)
                rec = row_rec[:, grp % 2, :].rearrange("p (h t) -> p t h", t=TT)
                tt_(o_n[:, grp % 2].rearrange("p t (h d) -> p t h d", d=DH), ps_o[:].rearrange("p (t h d) -> p t h d", t=TT, d=DH),
                    rec.unsqueeze(3).broadcast_to([P, TT, GH, DH]), ALU.mult).then_inc(o_ready, 1)

            def phases(b):
                PE, A, D, PO = (lambda n: pe_at(n, b)), (lambda n: act_at(n, b)), (lambda n: dve_at(n, b)), (lambda n: pool_at(n, b))

                def stats(n, x):
                    norm_stats(stat_b, mv_b, x, None).then_inc(dve_done, 1)
                    dve.wait_ge(dve_done, D(f"stats{n}"))
                    V.memset(wait_pad[:], 0.0)
                    norm_mv(stat_b, mv_b).then_inc(dve_done, 1)

                def zed(n, x):
                    dve.wait_ge(pool_done, PO(f"rstd{n}"))
                    norm_z(z, x, mv_b, rstd_b, centre=n < 3).then_inc(dve_done, 1)

                def d0():
                    dve.wait_ge(act_done, b * len(ACT_STEPS) + 1)
                    V.tensor_copy(cols_b[:], col_table[:, b, 1:5, :, :]).then_inc(dve_done, 1)
                    dve.wait_ge(pe_done, PE("attn_proj"))
                    dve.wait_ge(gate_in, 16 * b + 16)
                    tt_(x_odd[:], bank(0), per_tile(g_msa[:]), ALU.mult).then_inc(dve_done, 1)
                    dve.wait_ge(dve_done, D("x1_gated"))
                    dve.wait_ge(resid_ready, b + 1)
                    tt_(x_odd[:], x_odd[:], x_resid[:], ALU.add).then_inc(dve_done, 1)
                    dve.wait_ge(dve_done, D("x1"))
                    stats(0, x_odd)
                    zed(0, x_odd)

                def d1():
                    dve.wait_ge(adj_in, 16 * b + 16)
                    tt_(adj_mul, adj[:], w_bias[:].unsqueeze(1).broadcast_to([P, 2 * TT * NONGT, LABELS]), ALU.mult).then_inc(dve_done, 1)
                    dve.wait_ge(dve_done, D("adj_w"))
                    V.tensor_reduce(adj_v[:, 0, :], adj_mul, AX.X, ALU.add)
                    V.tensor_reduce(adj_v[:, 1, :], adj[:], AX.X, ALU.add).then_inc(dve_done, 1)
                    dve.wait_ge(dve_done, D("adj_sum"))
                    V.tensor_scalar(adj_v[:, 2, :], adj_v[:, 1, :], 0.0, None, ALU.is_gt).then_inc(dve_done, 1)
                    dve.wait_ge(dve_done, D("adj_on"))
                    V.tensor_scalar(adj_v[:, 3, :], adj_v[:, 2, :], NEG, -NEG, ALU.mult, ALU.add).then_inc(dve_done, 1)
                    dve.wait_ge(dve_done, D("adj_neg"))
                    V.scalar_tensor_tensor(adj_v[:, 3, :], adj_v[:, 0, :], col("b_bias"), adj_v[:, 3, :], ALU.add, ALU.add).then_inc(dve_done, 1)

                def d6():
                    dve.wait_ge(pe_done, PE("down"))
                    dve.wait_ge(rows_in, 32 * b + 32)
                    tt_(x_even[:], bank(0), per_tile(mod_rows[:, 0, :]), ALU.mult).then_inc(dve_done, 1)
                    dve.wait_ge(dve_done, D("x2_gated"))
                    dve.wait_ge(pool_done, PO("xr2"))
                    tt_(x_even[:], x_even[:], resid[:], ALU.add).then_inc(dve_done, 1)
                    dve.wait_ge(dve_done, D("x2"))
                    V.tensor_reduce(small[:, 0, 0:TT], x_even[:], AX.X, ALU.add).then_inc(dve_done, 1)
                    dve.wait_ge(dve_done, D("row_sum"))
                    V.tensor_scalar(small[:, 0, TT:2 * TT], small[:, 0, 0:TT], 0.0, None, ALU.not_equal).then_inc(dve_done, 1)

                def d8():
                    dve.wait_ge(pe_done, PE("self_feat"))
                    dve.wait_ge(dve_done, D("row_on"))
                    for tt in range(TT):
                        last = V.scalar_tensor_tensor(tile(1)[:, tt, :], mod_rows[:, 1, :], small[:, 0, TT + tt:TT + tt + 1],
                                                      bank(2)[:, tt, :], ALU.mult, ALU.add)
                    last.then_inc(dve_done, 1)

                def d9():
                    dve.wait_ge(act_done, A("self_c"))
                    for c in range(DC):
                        last = V.tensor_copy(kv_rep[:, c], tile(2)[:, c, 0:NONGT].unsqueeze(1).broadcast_to([P, GH, NONGT]))
                    last.then_inc(dve_done, 1)

                def d10():
                    dve.wait_ge(pe_done, PE("gat_kvw"))
                    tt_(vbd[0:GAT_ROWS], bank(1, GAT_ROWS), m["head_v"][0:GAT_ROWS].unsqueeze(1).broadcast_to([GAT_ROWS, 2, DIM]),
                        ALU.mult).then_inc(dve_done, 1)

                def d11():
                    dve.wait_ge(pe_done, PE("gat_k"))
                    for d in range(2):
                        for c in range(DC):
                            o = (d * DC + c) * NONGT
                            last = V.scalar_tensor_tensor(kbd[:, d, c, :].rearrange("p (a b) -> p a b", b=NONGT),
                                                          ps_b[:, 2, o:o + NONGT].unsqueeze(1).broadcast_to([P, 8, NONGT]),
                                                          col("bk_a" if d == 0 else "bk_b", c),
                                                          m["head_k"].rearrange("p (a b) -> p a b", b=NONGT), ALU.add, ALU.mult)
                    last.then_inc(dve_done, 1)

                def gat_scores(d):
                    on = adj_v[:, 2, d * TT * NONGT:(d + 1) * TT * NONGT].rearrange("p (t n) -> p t n", t=TT)
                    bias = adj_v[:, 3, d * TT * NONGT:(d + 1) * TT * NONGT].rearrange("p (t n) -> p t n", t=TT)
                    ed = e[:, d, :].rearrange("p (t h n) -> p t h n", t=TT, n=NONGT)
                    ed3 = e[:, d, :].rearrange("p (r n) -> p r n", n=NONGT)
                    wide = [P, TT, GAT_H, NONGT]

                    def run():
                        dve.wait_ge(pe_done, PE(f"gat_s{d}"))
                        if d == 0:
                            dve.wait_ge(dve_done, D("adj_bias"))
                        tt_(ed, ps_b[:, 1:3, 0:320].rearrange("p t (h n) -> p t h n", n=NONGT), on.unsqueeze(2).broadcast_to(wide),
                            ALU.mult).then_inc(dve_done, 1)
                        dve.wait_ge(dve_done, D(f"gat_m{d}"))
                        tt_(ed, ed, bias.unsqueeze(2).broadcast_to(wide), ALU.add).then_inc(dve_done, 1)
                        dve.wait_ge(dve_done, D(f"gat_b{d}"))
                        V.tensor_reduce(small[:, 1 + d, :], ed3, AX.X, ALU.max).then_inc(dve_done, 1)
                        dve.wait_ge(dve_done, D(f"gat_max{d}"))
                        tt_(ed3, ed3, small[:, 1 + d, :].unsqueeze(2).broadcast_to([P, 2 * GAT_H, NONGT]), ALU.subtract).then_inc(dve_done, 1)
                    return run

                def gat_den(d):
                    def run():
                        dve.wait_ge(act_done, A(f"gat_exp{d}"))
                        V.tensor_reduce(small[:, 1 + d, :], e[:, d, :].rearrange("p (r n) -> p r n", n=NONGT), AX.X, ALU.add).then_inc(dve_done, 1)
                        dve.wait_ge(dve_done, D(f"gat_den{d}"))
                        V.reciprocal(small[:, 1 + d, :], small[:, 1 + d, :]).then_inc(dve_done, 1)
                    return run

                def gat_out(d):
                    def run():
                        dve.wait_ge(pe_done, PE(f"gat_o{d}"))
                        dve.wait_ge(dve_done, D("gat_rec1" if d == 0 else "gat_acc0"))
                        tt_(tile(0).rearrange("p t (h g) -> p (t h) g", g=GAT_D), ps_b[:, 2, :].rearrange("p (r g) -> p r g", g=GAT_D),
                            small[:, 1 + d, :].unsqueeze(2).broadcast_to([P, 2 * GAT_H, GAT_D]), ALU.mult).then_inc(dve_done, 1)
                        dve.wait_ge(dve_done, D(f"gat_n{d}"))
                        dve.wait_ge(pool_done, PO("acc"))
                        tt_(tile(5), tile(5), tile(0), ALU.add).then_inc(dve_done, 1)
                        if d == 1:
                            dve.wait_ge(dve_done, D("gat_acc1"))
                            V.scalar_tensor_tensor(x_odd[:], tile(5), 0.0, x_even[:], ALU.max, ALU.add).then_inc(dve_done, 1)
                            dve.wait_ge(dve_done, D("x3"))
                            stats(1, x_odd)
                            zed(1, x_odd)
                    return run

                def d23():
                    dve.wait_ge(pe_done, PE("lin_q"))
                    tt_(tile(0), bank(1), per_tile(row("bq")), ALU.add).then_inc(dve_done, 1)
                    q3 = tile(0).rearrange("p t (h d) -> p (t h) d", d=16)
                    dve.wait_ge(dve_done, D("lin_qb"))
                    V.tensor_reduce(small[:, 3, :], q3, AX.X, ALU.max).then_inc(dve_done, 1)
                    dve.wait_ge(dve_done, D("lin_qmax"))
                    tt_(q3, q3, small[:, 3, :].unsqueeze(2).broadcast_to([P, 32, 16]), ALU.subtract).then_inc(dve_done, 1)

                def d24():
                    dve.wait_ge(pe_done, PE("lin_k"))
                    V.tensor_reduce(small[:, 4, 2:4], bank(2), AX.X, ALU.max).then_inc(dve_done, 1)
                    k0 = COLS["bk"][0]
                    dve.wait_ge(dve_done, D("lin_kmax"))
                    tt_(small[:, 4, 4:6], small[:, 4, 2:4], cols[:, k0:k0 + DC], ALU.add).then_inc(dve_done, 1)
                    dve.wait_ge(dve_done, D("lin_kmb"))
                    tt_(small[:, 4, 0:2], cols[:, k0:k0 + DC], small[:, 4, 4:6], ALU.subtract).then_inc(dve_done, 1)

                def d25():
                    dve.wait_ge(pe_done, PE("lin_v"))
                    tt_(tile(1), bank(0), per_tile(row("bv")), ALU.add).then_inc(dve_done, 1)

                def d26():
                    dve.wait_ge(act_done, A("lin_qexp"))
                    V.tensor_reduce(small[:, 3, :], tile(0).rearrange("p t (h d) -> p (t h) d", d=16), AX.X, ALU.add).then_inc(dve_done, 1)
                    dve.wait_ge(dve_done, D("lin_qden"))
                    V.reciprocal(small[:, 3, :], small[:, 3, :]).then_inc(dve_done, 1)
                    dve.wait_ge(act_done, A("lin_kexp"))
                    V.reciprocal(small[:, 5, 2:4], small[:, 5, 0:2]).then_inc(dve_done, 1)

                def d27():
                    dve.wait_ge(pe_done, PE("lin_ctx"))
                    dve.wait_ge(dve_done, D("lin_krec"))
                    for c in range(DC):
                        last = V.scalar_tensor_tensor(tmp[:, 5, c * P:(c + 1) * P], ps_b[:, 2, c * P:(c + 1) * P], small[:, 5, 2 + c:3 + c],
                                                      m["head_c"], ALU.mult, ALU.mult)
                    last.then_inc(dve_done, 1)

                def d29():
                    dve.wait_ge(pe_done, PE("lin_y"))
                    tt_(tile(0).rearrange("p t (h d) -> p (t h) d", d=16), ps_b[:, 1, :].rearrange("p (r d) -> p r d", d=16),
                        small[:, 3, :].unsqueeze(2).broadcast_to([P, 32, 16]), ALU.mult).then_inc(dve_done, 1)
                    dve.wait_ge(dve_done, D("y"))
                    stats(2, tile(0))
                    zed(2, tile(0))

                def d30():
                    dve.wait_ge(act_done, A("lin_tanh"))
                    V.scalar_tensor_tensor(tile(2), tile(1), 1.0, h[:], ALU.add, ALU.mult).then_inc(dve_done, 1)

                def d31():
                    dve.wait_ge(pe_done, PE("lin_out"))
                    for tt in range(TT):
                        last = V.scalar_tensor_tensor(x_even[:, tt, :], bank(0)[:, tt, :], 0.5, mod_rows[:, 2, :], ALU.mult, ALU.mult)
                    last.then_inc(dve_done, 1)
                    dve.wait_ge(dve_done, D("x4_gated"))
                    dve.wait_ge(pool_done, PO("xr4"))
                    tt_(x_even[:], x_even[:], resid[:], ALU.add).then_inc(dve_done, 1)
                    dve.wait_ge(dve_done, D("x4"))
                    stats(3, x_even)
                    zed(3, x_even)

                def d35():
                    dve.wait_ge(pe_done, PE("v3"))
                    tt_(tile(2), bank(1), per_tile(row("v_b3")), ALU.add).then_inc(dve_done, 1)

                def d36a():
                    dve.wait_ge(pe_done, PE("s3"))
                    V.tensor_reduce(small[:, 6, 0:TT], bank(2), AX.X, ALU.max, negate=True).then_inc(dve_done, 1)

                def d36b():
                    dve.wait_ge(act_done, A("exp3"))
                    V.reciprocal(small[:, 7, 2:4], small[:, 7, 0:2]).then_inc(dve_done, 1)
                    dve.wait_ge(dve_done, D("rec3"))
                    for tt in range(TT):
                        last = V.tensor_scalar(tile(3)[:, tt, :], tile(3)[:, tt, :], small[:, 7, 2 + tt:3 + tt], None, ALU.mult)
                    last.then_inc(dve_done, 1)

                def d39():
                    dve.wait_ge(pe_done, PE("proj3"))
                    dve.wait_ge(pool_done, PO("xr5"))
                    tt_(x_odd[:], bank(2), resid[:], ALU.add).then_inc(dve_done, 1)
                    dve.wait_ge(dve_done, D("x5"))
                    stats(4, x_odd)
                    zed(4, x_odd)

                def d45():
                    dve.wait_ge(pe_done, PE("down3"))
                    dve.wait_ge(pool_done, PO("xr6"))
                    dve.wait_ge(stored, 16 * b + 16)
                    tt_(y_out[:], bank(2), resid[:], ALU.add).then_inc(dve_done, 1)

                return {0: [d0], 3: [d1], 6: [d6], 8: [d8], 9: [d9], 10: [d10], 11: [d11], 13: [gat_scores(0)],
                        15: [gat_scores(1), gat_den(0)], 16: [gat_den(1)], 18: [gat_out(0)], 21: [gat_out(1)], 23: [d23],
                        24: [d24], 25: [d25], 26: [d26], 27: [d27], 29: [d29], 30: [d30], 31: [d31], 35: [d35],
                        36: [d36a, d36b], 39: [d39], 45: [d45]}

            def body(i, front, back, pre):
                b = i - 1
                back_phases = phases(b) if back else {}

                def run(slot):
                    for n in PHASES_AT[slot]:
                        for f in back_phases.get(n, ()):
                            f()
                run(0)
                if front:
                    maxes(0, i)
                for hd in range(HEADS):
                    if front and hd + 1 < HEADS:
                        maxes(hd + 1, i)
                    run(2 * hd + 1)
                    if front:
                        copy_probs(hd, i)
                    if hd == 11 and pre:
                        prelude_stats(i + 1)
                    if hd == 13 and pre:
                        prelude_z(i + 1)
                    run(2 * hd + 2)
                    if front and hd and hd % GH == 0:
                        normalise(hd // GH - 1, i)
                if front:
                    normalise(GROUPS - 1, i)
                run(33)

            prelude_stats(0)
            prelude_z(0)
            body(0, True, False, True)
            with dve.Fori(1, BATCH - 1) as i:
                body(i, True, True, True)
            body(BATCH - 1, True, True, False)
            body(BATCH, False, True, False)

        @block.gpsimd
        def _(pool):
            G = nc.gpsimd
            pool.wait_ge(setup_dve, SETUP_DVE)
            G.memset(ms_b[:], 0.0).then_inc(pool_done, 1)

            def prelude(i):
                pool.wait_ge(mv_a_ready, i + 1)
                G.tensor_tensor(var_a[:], mv_a[:, :, 1], eps[:, 0, :], ALU.add).then_inc(var_a_ready, 1)
                pool.wait_ge(var_a_ready, i + 1)
                G.tensor_tensor(rstd_a[:], var_a[:], minus_half[:], ALU.pow).then_inc(rstd_a_ready, 1)

            def front_resid(i):
                pool.wait_ge(gate_in, 16 * i + 16)
                pool.wait_ge(x_in, 16 * i + 16)
                G.tensor_tensor(gated_row[:], g_msa[:], row("b_out"), ALU.mult).then_inc(gated_row_ready, 1)
                pool.wait_ge(gated_row_ready, i + 1)
                if not isinstance(i, int) or i > 0:
                    pool.wait_ge(dve_done, dve_at("x1", i - 1))
                G.tensor_tensor(x_resid[:], xa[:], per_tile(gated_row[:]), ALU.add).then_inc(resid_ready, 1)

            def phases(b):
                D, PO = (lambda n: dve_at(n, b)), (lambda n: pool_at(n, b))

                def rstd(n):
                    pool.wait_ge(dve_done, D(f"mv{n}"))
                    if n >= 3:
                        G.tensor_tensor(ms_b[:, 0, :], mv_b[:, :, 0], mv_b[:, :, 0], ALU.mult).then_inc(pool_done, 1)
                        pool.wait_ge(pool_done, PO(f"sq{n}"))
                        G.tensor_tensor(ms_b[:, 1, :], ms_b[:, 0, :], mv_b[:, :, 1], ALU.add).then_inc(pool_done, 1)
                        pool.wait_ge(pool_done, PO(f"ms{n}"))
                        G.tensor_tensor(var_b[:], ms_b[:, 1, :], eps[:, 1, :], ALU.add).then_inc(pool_done, 1)
                    else:
                        G.tensor_tensor(var_b[:], mv_b[:, :, 1], eps[:, 0, :], ALU.add).then_inc(pool_done, 1)
                    pool.wait_ge(pool_done, PO(f"var{n}"))
                    G.tensor_tensor(rstd_b[:], var_b[:], minus_half[:], ALU.pow).then_inc(pool_done, 1)

                def g0():
                    rstd(0)
                    pool.wait_ge(rows_in, 32 * b + 32)
                    G.tensor_tensor(gate_bias[:], mod_rows[:, 0, :], row("b2"), ALU.mult).then_inc(pool_done, 1)
                    pool.wait_ge(pool_done, PO("gb2"))
                    G.tensor_tensor(resid[:], x_odd[:], per_tile(gate_bias[:]), ALU.add).then_inc(pool_done, 1)

                def g8():
                    pool.wait_ge(dve_done, D("u"))
                    G.tensor_tensor(tile(5), tile(1), per_tile(gat_row[:]), ALU.add).then_inc(pool_done, 1)

                def g21():
                    rstd(1)
                    G.tensor_tensor(gate_bias[:], mod_rows[:, 2, :], row("out_b"), ALU.mult).then_inc(pool_done, 1)
                    pool.wait_ge(pool_done, PO("gob"))
                    G.tensor_tensor(resid[:], x_odd[:], per_tile(gate_bias[:]), ALU.add).then_inc(pool_done, 1)

                def g29():
                    rstd(2)

                def g31():
                    rstd(3)
                    G.tensor_tensor(resid[:], x_even[:], per_tile(row("proj_b3")), ALU.add).then_inc(pool_done, 1)

                def g39():
                    rstd(4)
                    G.tensor_tensor(resid[:], x_odd[:], per_tile(row("b2_3")), ALU.add).then_inc(pool_done, 1)

                return {0: [g0], 8: [g8], 21: [g21], 29: [g29], 31: [g31], 39: [g39]}

            def body(i, front, back, pre):
                b = i - 1
                back_phases = phases(b) if back else {}

                def run(slot):
                    for n in PHASES_AT[slot]:
                        for f in back_phases.get(n, ()):
                            f()
                run(0)
                for hd in range(HEADS):
                    run(2 * hd + 1)
                    if hd == 1 and front:
                        front_resid(i)
                    if hd == 11 and pre:
                        prelude(i + 1)
                    run(2 * hd + 2)
                run(33)

            prelude(0)
            body(0, True, False, True)
            with pool.Fori(1, BATCH - 1) as i:
                body(i, True, True, True)
            body(BATCH - 1, True, True, False)
            body(BATCH, False, True, False)


def kernel(**inputs):
    import numpy as np
    import concourse.bacc as bacc
    from concourse.bass_utils import run_bass_kernel_spmd

    a = {k: np.asarray(v) for k, v in inputs.items()}

    def chunks(wt):
        return wt.reshape(wt.shape[0] // P, P, wt.shape[1]).transpose(1, 0, 2)

    def columns(vec):
        return vec.reshape(-1, P).T

    f1, f2 = "L3_cond_film1_", "L3_cond_film2_"
    w_mod, b_mod = a["L0_cond_W_mod"], a["L0_cond_b_mod"]
    parts = [(w_mod, b_mod, 1), (w_mod, b_mod, 0), (w_mod, b_mod, 4), (w_mod, b_mod, 3),
             (a["L2_cond_emb_W"], a["L2_cond_emb_b"], 0), (a["L2_cond_emb_W"], a["L2_cond_emb_b"], 1),
             (a[f1 + "w"], a[f1 + "b"], 0), (a[f1 + "w"], a[f1 + "b"], 1),
             (a[f2 + "w"], a[f2 + "b"], 0), (a[f2 + "w"], a[f2 + "b"], 1),
             (w_mod, b_mod, 2), (w_mod, b_mod, 5)]
    pieces = [chunks(wt[:, n * DIM:(n + 1) * DIM]) for wt, _, n in parts] + [chunks(a["L1_cond_W_self"][:, DIM:].T)]
    one, zero = np.ones(DIM, np.float32), np.zeros(DIM, np.float32)
    vectors = {
        "b1": a["L0_cond_b1"], "b1_3": a["L3_cond_mlp_b1"], "b_self": a["L1_cond_b_self"],
        "bq_a": a["L1_cond_bq"][0], "bq_b": a["L1_cond_bq"][1], "bk_a": a["L1_cond_bk"][0], "bk_b": a["L1_cond_bk"][1],
        "norm_g": a["L2_cond_norm_g"], "norm_b": a["L2_cond_norm_b"], "bk": a["L2_cond_bk"],
        "q_b3": a["L3_cond_q_b"], "k_b3": a["L3_cond_k_b"],
        "mod_b": np.concatenate([v[n * DIM:(n + 1) * DIM] for _, v, n in parts[:COL_PIECES]]),
        "mod_w": np.concatenate([one, one, a["L2_cond_sn_g"], a["L3_cond_norm1_w"], a["L3_cond_norm2_w"]]),
        "mod_0": np.concatenate([zero, zero, a["L2_cond_sn_b"], zero, zero]),
        "b_bias": np.broadcast_to(a["L1_cond_b_bias"], (P,)), "half": np.full(P, 0.5, np.float32),
    }
    row_vectors = [a["L0_cond_b_out"], a["L0_cond_b2"], a["L1_cond_b_self"], a["L1_cond_bout"][0], a["L1_cond_bout"][1],
                   a["L2_cond_bq"], a["L2_cond_bv"], a["L2_cond_out_b"], a["L3_cond_v_b"], a["L3_cond_proj_b"],
                   a["L3_cond_mlp_b2"], b_mod[2 * DIM:3 * DIM], b_mod[5 * DIM:]]
    p = np.arange(P)[:, None]
    masks = np.concatenate([
        p == np.arange(P)[None, :],
        p // 16 == np.repeat(np.arange(8), NONGT)[None, :],
        p // NONGT == np.arange(DIM)[None, :] // GAT_D % GH,
        p // 16 == np.arange(P)[None, :] // 16], axis=1).astype(np.float32)
    mask = a["mask_BxSxSx11_ik0"]
    labels = np.stack([mask[:, :, :NONGT].reshape(BATCH, TT, P, NONGT, LABELS).transpose(0, 2, 1, 3, 4),
                       mask[:, :NONGT].transpose(0, 2, 1, 3).reshape(BATCH, TT, P, NONGT, LABELS).transpose(0, 2, 1, 3, 4)], axis=2)
    w2d = {
        "wqkv": a["L0_cond_W_qkv"], "w_out": a["L0_cond_W_out"], "w1": a["L0_cond_W1"], "w2": a["L0_cond_W2"],
        "w_self": a["L1_cond_W_self"][:, :DIM].T, "w_gq": np.concatenate([m.T for m in a["L1_cond_Wq"]], axis=1),
        "w_gk": np.concatenate([m.T for m in a["L1_cond_Wk"]], axis=1),
        "w_gout": np.concatenate([m.reshape(DIM, DIM).T for m in a["L1_cond_Wout"]], axis=1),
        "w_lq": a["L2_cond_Wq"], "w_lk": a["L2_cond_Wk"], "w_lv": a["L2_cond_Wv"], "w_lo": a["L2_cond_out_W"],
        "w_q3": a["L3_cond_q_w"], "w_k3": a["L3_cond_k_w"], "w_v3": a["L3_cond_v_w"], "w_p3": a["L3_cond_proj_w"],
        "w1_3": a["L3_cond_mlp_w1"], "w2_3": a["L3_cond_mlp_w2"],
    }
    arrays = {
        "x": a["x"].reshape(BATCH, TT, P, DIM).transpose(0, 2, 1, 3),
        "cond": a["cond_1024"], "cond_t": chunks(a["cond_1024"].T),
        "cols": np.concatenate([columns(vectors[n]) for n in COLS], axis=1),
        "rows": np.stack(row_vectors)[None], "masks": masks, "w_bias": a["L1_cond_w_bias"][None],
        "w_mod": np.stack(pieces), "adj": labels.reshape(BATCH, P, 2 * TT * NONGT, LABELS),
        **{n: chunks(w2d[n]) for n, _, _ in WEIGHTS},
    }
    arrays = {k: np.ascontiguousarray(v) for k, v in arrays.items()}

    nc = bacc.Bacc("TRN2", target_bir_lowering=False, num_devices=1)
    t = {k: nc.dram_tensor("in_" + k, v.shape, mybir.dt.from_np(v.dtype), kind="ExternalInput").ap() for k, v in arrays.items()}
    t["scratch"] = nc.dram_tensor("mod_rows_scratch", (BATCH, 3 * DIM), F32, kind="Internal").ap()
    out = nc.dram_tensor("out", (BATCH, P, TT, DIM), F32, kind="ExternalOutput").ap()
    build(nc, t, out)
    got = run_bass_kernel_spmd(nc, [{"in_" + k: v for k, v in arrays.items()}], core_ids=[0]).results[0]["out"]
    return got.reshape(BATCH, P, TT, DIM).transpose(0, 2, 1, 3).reshape(BATCH, TOK, DIM)
```

```python
from contextlib import ExitStack

import concourse.bass as bass
from concourse import mybir

F32 = mybir.dt.float32
I32 = mybir.dt.int32
ALU = mybir.AluOpType
ACT = mybir.ActivationFunctionType
AX = mybir.AxisListType

P = 128
BATCH, TOK, DIM = 32, 256, 256
TT = TOK // P
DC = DIM // P
HEADS, DH = 16, 64
INNER = HEADS * DH
GROUPS, GH = 4, 4
PAIRS = HEADS // 2
MLP = 1024
FC = MLP // P
GAT_H, GAT_D, NONGT, LABELS = 16, 16, 20, 11
NEG = 9000000000000000.0
GAT_ROWS = GH * NONGT
EPS = (1e-5, 1e-6)
PIECES, COL_PIECES = 13, 10

PROJ_USES = [("qk", 0), ("v", 0), ("qk", 1)]
for _h in range(HEADS):
    if _h % 2 == 1 and (_h + 3) // 2 < PAIRS:
        PROJ_USES.append(("qk", (_h + 3) // 2))
    if _h % 4 == 2 and _h // 4 + 1 < GROUPS:
        PROJ_USES.append(("v", _h // 4 + 1))
NPROJ = len(PROJ_USES)

PE_MID = ("attn_proj", "norm_t0", "up0", "up1", "down0", "up2", "down1", "up3", "down2", "down", "x2_t", "self_feat",
          "self_t", "gat_kvw", "gat_k", "gat_q0", "gat_q1", "gat_s0", "gat_s1", "gat_e00", "gat_e01", "gat_o0",
          "gat_e10", "gat_e11", "gat_o1")
PE_BACK = ("norm_t1", "lin_q", "lin_k", "lin_v", "lin_k_t", "lin_q_t", "lin_ctx", "lin_y", "norm_t2", "lin_out",
           "norm_t3", "q3", "k3", "v3", "s3", "p3_t", "o3", "proj3", "norm_t4", "up3_0", "up3_1", "down3_0", "up3_2",
           "down3_1", "up3_3", "down3_2", "down3")
ACT_MID = ("norm_h0", "gelu0", "gelu1", "gelu2", "gelu3", "x2_c", "self_c", "gat_qc0", "gat_qc1", "gat_exp0",
           "gat_exp1", "gat_ec00", "gat_ec01", "gat_ec10", "gat_ec11")
ACT_BACK = ("norm_h1", "lin_qexp", "lin_kexp", "lin_k_c", "lin_q_c", "norm_h2", "lin_tanh", "norm_h3", "q3_c", "k3_c",
            "exp3", "p3_c", "o3_c", "norm_h4", "gelu3_0", "gelu3_1", "gelu3_2", "gelu3_3")
DVE_MID = ("cols0", "x1_gated", "x1", "stats0", "mv0", "z0", "adj_w", "adj_sum", "adj_on", "adj_neg", "adj_bias",
           "x2_gated", "x2", "row_sum", "row_on", "u", "kv_rep", "vbd", "kbd", "gat_m0", "gat_b0", "gat_max0",
           "gat_sub0", "gat_m1", "gat_b1", "gat_max1", "gat_sub1", "gat_den0", "gat_rec0", "gat_den1", "gat_rec1",
           "gat_n0", "gat_acc0", "gat_n1", "gat_acc1", "x3")
DVE_BACK = ("cols2", "stats1", "mv1", "z1", "lin_qb", "lin_qmax", "lin_qsub", "lin_kmax", "lin_kmb", "lin_kbias",
            "lin_vb", "lin_qden", "lin_qrec", "lin_krec", "ctx_s", "y", "stats2", "mv2", "z2", "silu2", "x4_gated",
            "x4", "stats3", "mv3", "z3", "v3_b", "max3", "rec3", "p3_n", "x5", "stats4", "mv4", "z4", "out")
POOL_MID = ("var0", "rstd0", "gb2", "xr2", "acc")
POOL_BACK = ("var1", "rstd1", "gob", "xr4", "var2", "rstd2", "sq3", "ms3", "var3", "rstd3", "xr5", "sq4", "ms4",
             "var4", "rstd4", "xr6")

COLS = {}
_n = 0
for _name, _k in (("b1", FC), ("b1_3", FC), ("b_self", DC), ("bq_a", DC), ("bq_b", DC), ("bk_a", DC),
                  ("bk_b", DC), ("norm_g", DC), ("norm_b", DC), ("bk", DC), ("q_b3", DC), ("k_b3", DC),
                  ("mod_b", 2 * 5 * DC), ("mod_w", 5 * DC), ("mod_0", 5 * DC), ("b_bias", 1)):
    COLS[_name] = (_n, _k)
    _n += _k
NCOLS = _n
WEIGHTS = (("wqkv", 2, 3 * INNER), ("w_out", INNER // P, DIM), ("w1", 2, MLP), ("w2", FC, DIM), ("w_self", 2, DIM),
           ("w_gq", 2, 2 * DIM), ("w_gk", 2, 2 * DIM), ("w_gout", 2, 2 * DIM), ("w_lq", 2, DIM), ("w_lk", 2, DIM),
           ("w_lv", 2, DIM), ("w_lo", 2, DIM), ("w_q3", 2, DIM), ("w_k3", 2, DIM), ("w_v3", 2, DIM), ("w_p3", 2, DIM),
           ("w1_3", 2, MLP), ("w2_3", FC, DIM))
SMALL_LOADS = 6
SETUP_DVE = 7
ROWS = ("b_out", "b2", "bq", "bv", "out_b", "v_b3", "proj_b3", "b2_3")
SETUP_ROWS = ("b_self", "bout_a", "bout_b", "mod_g", "mod_m")
MASKS = {"ident": P, "head_k": 8 * NONGT, "head_v": DIM, "head_c": P}
MID_AT = {0: ("attn_proj",), 1: ("norm_t0",), 2: ("up0",), 3: ("up1", "down0"), 4: ("up2", "down1"), 5: ("up3", "down2"),
          6: ("down",), 7: ("x2_t",), 8: ("self_feat",), 9: ("self_t",), 10: ("gat_kvw", "gat_k"),
          11: ("gat_q0", "gat_q1"), 12: ("gat_s0",), 13: ("gat_s1",), 14: ("gat_e00", "gat_e01"), 15: ("gat_o0", "gat_e10"),
          16: ("gat_e11",), 17: ("gat_o1",)}
BACK_AT = {0: ("norm_t1",), 1: ("lin_q", "lin_k"), 2: ("lin_v", "lin_k_t"), 3: ("lin_q_t", "lin_ctx"), 4: ("lin_y",),
           5: ("norm_t2",), 6: ("lin_out",), 7: ("norm_t3",), 8: ("q3", "k3"), 9: ("v3", "s3"), 10: ("p3_t",), 11: ("o3",),
           12: ("proj3",), 13: ("norm_t4",), 14: ("up3_0",), 15: ("up3_1", "down3_0"), 16: ("up3_2", "down3_1"),
           17: ("up3_3", "down3_2", "down3")}


def build(nc, t, out):
    with ExitStack() as ctx:
        def sb(name, shape, dt=F32):
            return ctx.enter_context(nc.sbuf_tensor(name, shape, dt))

        def sem(name):
            return ctx.enter_context(nc.semaphore(name))

        w = {n: sb("w_" + n, [P, k, c]) for n, k, c in WEIGHTS}
        cols = sb("cols", [P, NCOLS])
        rows = sb("rows", [P, len(ROWS), DIM])
        masks = sb("masks", [P, sum(MASKS.values())])
        w_bias = sb("w_bias", [P, LABELS])
        col_table = sb("col_table", [P, BATCH, 5, 2, DC])
        qs_cols = sb("qs_cols", [P, 3, DC])
        gat_row = sb("gat_row", [P, DIM])
        minus_half = sb("minus_half", [P, TT])
        eps = sb("eps", [P, 2, TT])
        wait_pad = sb("wait_pad", [P, 3])

        def col(name, k=0):
            return cols[:, COLS[name][0] + k:COLS[name][0] + k + 1]

        def row(name):
            return rows[:, ROWS.index(name), :]

        at, m = 0, {}
        for name, width in MASKS.items():
            m[name] = masks[:, at:at + width]
            at += width
        ident = m["ident"]

        def per_tile(ap):
            return ap.unsqueeze(1).broadcast_to([P, TT, ap.shape[-1]])

        xa = sb("xa", [P, TT, DIM])
        x_resid = sb("x_resid", [P, TT, DIM])
        gated_row = sb("gated_row", [P, DIM])
        g_msa = sb("g_msa", [P, DIM])
        za = sb("za", [P, TT, DIM])
        ha = sb("ha", [P, DC, TOK])
        stat_a = sb("stat_a", [P, TT, 6])
        mv_a = sb("mv_a", [P, TT, 2])
        var_a = sb("var_a", [P, TT])
        rstd_a = sb("rstd_a", [P, TT])
        cols_a = sb("cols_a", [P, 2, DC])
        qk = sb("qk", [P, 2, 2, TOK])
        v = sb("v", [P, 2, TT, GH * DH])
        neg_max = sb("neg_max", [P, 2, TT])
        row_sum = sb("row_sum", [P, 2, TT])
        row_rec = sb("row_rec", [P, 2, TT])
        probs = sb("probs", [P, 2, TT, TOK])
        probs_t = sb("probs_t", [P, 2, TT, TOK])
        o_t = sb("o_t", [P, INNER // P, TOK])

        x_mid = sb("x_mid", [P, TT, DIM])
        resid_mid = sb("resid_mid", [P, TT, DIM])
        gate_bias_mid = sb("gate_bias_mid", [P, DIM])
        mod_rows = sb("mod_rows", [P, 2, DIM])
        h_mid = sb("h_mid", [P, DC, TOK])
        g_mid = sb("g_mid", [P, 2, 2, TOK])
        tmp = sb("tmp", [P, 6, 2 * 256])
        kv_rep = sb("kv_rep", [P, DC, GH, NONGT])
        kbd = sb("kbd", [P, 2, DC, 8 * NONGT])
        vbd = sb("vbd", [P, 2, DIM])
        adj = sb("adj", [P, 2 * TT * NONGT, LABELS], I32)
        adj_v = sb("adj_v", [P, 4, 2 * TT * NONGT])
        cols_mid = sb("cols_mid", [P, 2, DC])
        small_mid = sb("small_mid", [P, 3, 2 * 16])
        x3 = sb("x3", [P, TT, DIM])
        x_back = sb("x_back", [P, TT, DIM])
        resid_back = sb("resid_back", [P, TT, DIM])
        gate_bias_back = sb("gate_bias_back", [P, DIM])
        cond_row = sb("cond_row", [P, DIM])
        h_back = sb("h_back", [P, DC, TOK])
        g_back = sb("g_back", [P, 2, 2, TOK])
        tmp_back = sb("tmp_back", [P, 5, 2 * 256])
        cols_back = sb("cols_back", [P, 3, 2, DC])
        small_back = sb("small_back", [P, 5, 2 * 16])
        ms_back = sb("ms_back", [P, 2, TT])
        y_out = sb("y_out", [P, TT, DIM])
        stat_mid, stat_back = sb("stat_mid", [P, TT, 6]), sb("stat_back", [P, TT, 6])
        mv_mid, mv_back = sb("mv_mid", [P, TT, 2]), sb("mv_back", [P, TT, 2])
        var_mid, var_back = sb("var_mid", [P, TT]), sb("var_back", [P, TT])
        rstd_mid, rstd_back = sb("rstd_mid", [P, TT]), sb("rstd_back", [P, TT])

        tmp_flat = tmp[:, :, :].rearrange("p a b -> p (a b)")
        adj_mul = tmp_flat[:, 0:2 * TT * NONGT * LABELS].rearrange("p (r l) -> p r l", l=LABELS)
        e = [tmp_flat[:, 0:640], tmp_flat[:, 3 * 512:3 * 512 + 640]]
        e_t = g_mid[:, :, :, :].rearrange("p a b c -> p a (b c)")
        setup_rows = tmp_flat[0:BATCH, 0:3 * DIM]
        setup_in_rows = o_t[:, 0:len(SETUP_ROWS), :]

        def tile(k, rows_=P):
            return tmp[0:rows_, k, :].rearrange("p (a b) -> p a b", a=2)

        def tile_b(k):
            return tmp_back[:, k, :].rearrange("p (a b) -> p a b", a=2)

        ps_s = ctx.enter_context(nc.psum_tensor("ps_s", [P, 512], F32))
        ps_t = ctx.enter_context(nc.psum_tensor("ps_t", [P, 512], F32))
        ps_o = ctx.enter_context(nc.psum_tensor("ps_o", [P, 512], F32))
        ps_p = ctx.enter_context(nc.psum_tensor("ps_p", [P, 512], F32))
        ps_m = ctx.enter_context(nc.psum_tensor("ps_m", [P, 2, 512], F32))
        ps_b = ctx.enter_context(nc.psum_tensor("ps_b", [P, 2, 512], F32))

        def mid(k, rows_=P):
            return ps_m[0:rows_, k, :].rearrange("p (a b) -> p a b", a=2)

        def back(k):
            return ps_b[:, k, :].rearrange("p (a b) -> p a b", a=2)

        small_in = sem("small_in")
        front_w_in = sem("front_w_in")
        rest_w_in = sem("rest_w_in")
        piece_in = [sem(f"piece_in{k}") for k in range(6)]
        x_in = sem("x_in")
        gate_in = sem("gate_in")
        rows_in = sem("rows_in")
        cond_in = sem("cond_in")
        adj_in = sem("adj_in")
        stored = sem("stored")
        setup_act, setup_dve, setup_pe = sem("setup_act"), sem("setup_dve"), sem("setup_pe")
        stats_a_ready, mv_a_ready, var_a_ready, rstd_a_ready = (sem(n) for n in ("stats_a", "mv_a_s", "var_a_s", "rstd_a_s"))
        za_ready, za_turned, ha_ready, cols_a_ready = (sem(n) for n in ("za_ready", "za_turned", "ha_ready", "cols_a_ready"))
        gated_row_ready, resid_ready = sem("gated_row_ready"), sem("resid_ready")
        projected, proj_copied = sem("projected"), sem("proj_copied")
        scored, max_ready, probs_ready = sem("scored"), sem("max_ready"), sem("probs_ready")
        probs_turned, probs_copied, weighted = sem("probs_turned"), sem("probs_copied"), sem("weighted")
        sum_inverted, probs_normal = sem("sum_inverted"), sem("probs_normal")
        o_copied = sem("o_copied")
        pe_mid, act_mid, dve_mid, pool_mid = (sem(n) for n in ("pe_mid", "act_mid", "dve_mid", "pool_mid"))
        pe_back, act_back, dve_back, pool_back = (sem(n) for n in ("pe_back", "act_back", "dve_back", "pool_back"))

        def step_at(steps, name, b):
            return b * len(steps) + steps.index(name) + 2

        def proj_at(kind, k, i):
            return i * NPROJ + PROJ_USES.index((kind, k)) + 1

        def later(i):
            return not isinstance(i, int) or i > 0

        def run_schedule(eng, body):
            body(0, True, False, False, True)
            body(1, True, True, False, True)
            with eng.Fori(2, BATCH - 1) as i:
                body(i, True, True, True, True)
            body(BATCH - 1, True, True, True, False)
            body(BATCH, False, True, True, False)
            body(BATCH + 1, False, False, True, False)

        scratch = t["scratch"]
        block = ctx.enter_context(nc.Block())

        @block.sync
        def _(sp):
            sp.dma_start(cols[:], t["cols"]).then_inc(small_in, 16)
            sp.dma_start(ha[:, :, 0:BATCH], t["cond_t"]).then_inc(small_in, 16)
            for k in range(6):
                sp.dma_start(tile(k), t["w_mod"][k]).then_inc(piece_in[k], 16)
            sp.dma_start(rows[:], t["rows"].broadcast_to([P, len(ROWS), DIM])).then_inc(small_in, 16)
            sp.dma_start(setup_in_rows, t["setup_rows"].broadcast_to([P, len(SETUP_ROWS), DIM])).then_inc(small_in, 16)
            sp.dma_start(masks[:], t["masks"]).then_inc(small_in, 16)
            sp.dma_start(w_bias[:], t["w_bias"].broadcast_to([P, LABELS])).then_inc(small_in, 16)
            for k in range(6, PIECES):
                sp.wait_ge(setup_pe, k - 5)
                sp.dma_start(tile(k % 6), t["w_mod"][k]).then_inc(piece_in[k % 6], 16)
            sp.dma_start(xa[:], t["x"][0]).then_inc(x_in, 16)
            sp.dma_start(w["wqkv"][:], t["wqkv"]).then_inc(front_w_in, 16)
            sp.wait_ge(setup_dve, 3)
            sp.dma_start(scratch, setup_rows).then_inc(stored, 16)
            for name, _, _ in WEIGHTS:
                if name != "wqkv":
                    sp.dma_start(w[name][:], t[name]).then_inc(rest_w_in, 16)
            sp.wait_ge(stored, 16)

            def body(i, front, middle, rear, pre):
                if middle:
                    b = i - 1
                    sp.wait_ge(dve_mid, b * len(DVE_MID) + 1)
                    sp.wait_ge(pool_mid, b * len(POOL_MID) + 1)
                    sp.dma_start(mod_rows[:], scratch[bass.ds(b, 1), DIM:3 * DIM].rearrange("a (r c) -> a r c", r=2)
                                 .broadcast_to([P, 2, DIM])).then_inc(rows_in, 16)
                    sp.dma_start(adj[:], t["adj"][bass.ds(b, 1)].rearrange("a p r l -> (a p) r l")).then_inc(adj_in, 16)
                if rear:
                    b = i - 2
                    sp.wait_ge(dve_back, b * len(DVE_BACK) + 1)
                    sp.wait_ge(pool_back, b * len(POOL_BACK) + 1)
                    sp.dma_start(cond_row[:], t["cond"][bass.ds(b, 1), :].broadcast_to([P, DIM])).then_inc(cond_in, 16)
                if middle:
                    sp.wait_ge(dve_mid, step_at(DVE_MID, "x1", i - 1))
                if front:
                    sp.dma_start(g_msa[:], scratch[bass.ds(i, 1), 0:DIM].broadcast_to([P, DIM])).then_inc(gate_in, 16)
                if pre:
                    sp.wait_ge(resid_ready, i + 1)
                    sp.wait_ge(za_ready, i + 1)
                    sp.dma_start(xa[:], t["x"][bass.ds(i + 1, 1)].rearrange("a p t c -> (a p) t c")).then_inc(x_in, 16)
                if rear:
                    sp.wait_ge(dve_back, step_at(DVE_BACK, "out", i - 2))
                    sp.dma_start(out[bass.ds(i - 2, 1)].rearrange("a p t c -> (a p) t c"), y_out[:]).then_inc(stored, 16)

            run_schedule(sp, body)
            sp.wait_ge(stored, 16 * (BATCH + 1))

        @block.tensor
        def _(pe):
            mm = nc.tensor.matmul

            pe.wait_ge(small_in, 16 * SMALL_LOADS)
            pe.wait_ge(setup_dve, 2)
            for k in range(PIECES):
                pe.wait_ge(piece_in[k % 6], 16 * (k // 6 + 1))
                src = za if (k < 6 or k in (10, 11)) else ha
                for c in range(DC if k < COL_PIECES else 1):
                    for kk in range(DC):
                        if k < COL_PIECES:
                            n = (k * DC + c) * BATCH
                            last = mm(ps_b[:, n // 512, n % 512:n % 512 + BATCH], tile(k % 6)[:, kk, c * P:c * P + P],
                                      src[:, kk, 0:BATCH], start=(kk == 0), stop=(kk == 1))
                        else:
                            o = (k - COL_PIECES) * DIM
                            last = mm(ps_o[0:BATCH, o:o + DIM] if o < 512 else ps_t[0:BATCH, 0:DIM],
                                      src[:, kk, 0:BATCH], tile(k % 6)[:, kk, :], start=(kk == 0), stop=(kk == 1))
                last.then_inc(setup_pe, 1)
            pe.wait_ge(setup_dve, SETUP_DVE)
            pe.wait_ge(front_w_in, 16)
            pe.nop().then_inc(pe_mid, 1)
            pe.nop().then_inc(pe_back, 1)

            def turn(dst, src):
                for a in range(2):
                    for c in range(2):
                        last = nc.tensor.transpose(dst[:, c, a * P:a * P + P], src[:, a, c * P:c * P + P], ident)
                return last

            def to_tokens(dst, src, weights):
                kk = src.shape[1]
                for tt in range(TT):
                    for k in range(kk):
                        last = mm(dst[:, tt, :], src[:, k, tt * P:tt * P + P], weights[:, k, :], start=(k == 0), stop=(k == kk - 1))
                return last

            def to_features(dst, src, weights, first=0):
                kk = src.shape[1]
                for c in range(2):
                    for k in range(kk):
                        last = mm(dst[:, c, :], weights[:, k, first + c * P:first + c * P + P], src[:, k, :],
                                  start=(k == 0), stop=(k == kk - 1))
                return last

            def down_part(dst, hidden, weights, j):
                for tt in range(TT):
                    for k in range(2):
                        last = mm(dst[:, tt, :], hidden[:, k, tt * P:tt * P + P], weights[:, 2 * j + k, :],
                                  start=(j == 0 and tt == 0 and k == 0), stop=(j == 3 and tt == 1 and k == 1),
                                  skip_group_check=True)
                return last

            def prelude(i):
                pe.wait_ge(za_ready, i + 1)
                if later(i):
                    pe.wait_ge(proj_copied, i * NPROJ)
                turn(ps_p[:].rearrange("p (a b) -> p a b", a=2), za).then_inc(za_turned, 1)

            def proj(kind, k, i):
                n = PROJ_USES.index((kind, k))
                bank_p = ps_p[:].rearrange("p (a b) -> p a b", a=2)
                if n == 0:
                    pe.wait_ge(ha_ready, i + 1)
                else:
                    pe.wait_ge(proj_copied, i * NPROJ + n)
                if kind == "qk":
                    for c in range(2):
                        for kk in range(DC):
                            last = mm(bank_p[:, c, :], w["wqkv"][:, kk, c * INNER + k * P:c * INNER + k * P + P],
                                      ha[:, kk, :], start=(kk == 0), stop=(kk == 1))
                else:
                    last = to_tokens(bank_p, ha, w["wqkv"][:, :, 2 * INNER + k * 256:2 * INNER + (k + 1) * 256])
                last.then_inc(projected, 1)

            def scores(hd, i):
                pair, r = hd // 2, hd % 2 * DH
                pe.wait_ge(proj_copied, proj_at("qk", pair, i))
                for tt in range(TT):
                    last = mm(ps_s[:, tt * TOK:(tt + 1) * TOK], qk[r:r + DH, pair % 2, 0, tt * P:tt * P + P],
                              qk[r:r + DH, pair % 2, 1, :], start=True, stop=True)
                last.then_inc(scored, 1)

            def turn_probs(hd, i):
                pe.wait_ge(probs_normal, i * HEADS + hd + 1)
                if hd or later(i):
                    pe.wait_ge(probs_copied, i * HEADS + hd)
                turn(ps_t[:].rearrange("p (a b) -> p a b", a=2), probs[:, hd % 2]).then_inc(probs_turned, 1)

            def weigh(hd, i):
                grp = hd // GH
                pe.wait_ge(probs_copied, i * HEADS + hd + 1)
                if hd % GH == 0:
                    pe.wait_ge(proj_copied, proj_at("v", grp, i))
                    if grp or later(i):
                        pe.wait_ge(o_copied, i * GROUPS + grp)
                r, c = hd % 2 * DH, hd % GH // 2 * TOK
                for kt in range(TT):
                    last = mm(ps_o[r:r + DH, c:c + TOK], v[:, grp % 2, kt, hd % GH * DH:hd % GH * DH + DH],
                              probs_t[:, hd % 2, kt, :], start=(kt == 0), stop=(kt == 1))
                last.then_inc(weighted, 1)

            def mid_steps(b):
                def A(n): return step_at(ACT_MID, n, b)
                def D(n): return step_at(DVE_MID, n, b)

                def attn_proj():
                    pe.wait_ge(o_copied, GROUPS * (b + 1))
                    pe.wait_ge(act_mid, b * len(ACT_MID) + 1)
                    return to_tokens(mid(0), o_t, w["w_out"])

                def norm_t0():
                    pe.wait_ge(dve_mid, D("z0"))
                    return turn(mid(1), tile(5))

                def up(j):
                    def run():
                        pe.wait_ge(act_mid, A("norm_h0") if j == 0 else A(f"gelu{j - 1}"))
                        return to_features(mid(0), h_mid, w["w1"], first=j * 256)
                    return run

                def down(j):
                    def run():
                        pe.wait_ge(act_mid, A(f"gelu{j}"))
                        return down_part(mid(1), g_mid[:, j % 2], w["w2"], j)
                    return run

                def x2_t():
                    pe.wait_ge(dve_mid, D("x2"))
                    return turn(mid(0), x_mid)

                def self_feat():
                    pe.wait_ge(act_mid, A("x2_c"))
                    return to_tokens(mid(1), tile(0), w["w_self"])

                def self_t():
                    pe.wait_ge(dve_mid, D("u"))
                    return turn(mid(0), tile(1))

                def gat_kvw():
                    pe.wait_ge(dve_mid, D("kv_rep"))
                    for d in range(2):
                        for k in range(DC):
                            last = mm(mid(1, GAT_ROWS)[:, d, :], kv_rep[:, k].rearrange("p a b -> p (a b)"),
                                      w["w_gout"][:, k, d * DIM:(d + 1) * DIM], start=(k == 0), stop=(k == 1))
                    return last

                def gat_k():
                    for d in range(2):
                        for c in range(DC):
                            for k in range(DC):
                                o = (d * DC + c) * NONGT
                                last = mm(ps_m[:, 0, o:o + NONGT], w["w_gk"][:, k, d * DIM + c * P:d * DIM + c * P + P],
                                          tile(2)[:, k, 0:NONGT], start=(k == 0), stop=(k == 1))
                    return last

                def gat_q(d):
                    def run():
                        pe.wait_ge(dve_mid, D("vbd") if d == 0 else D("kbd"))
                        return to_features(mid(1 - d), tile(2), w["w_gq"], first=d * DIM)
                    return run

                def gat_s(d):
                    def run():
                        if d == 0:
                            pe.wait_ge(act_mid, A("gat_qc1"))
                        else:
                            pe.wait_ge(dve_mid, D("gat_m0"))
                        for tt in range(TT):
                            for c in range(DC):
                                last = mm(ps_m[:, tt, c * 160:(c + 1) * 160], tile(3 + d)[:, c, tt * P:tt * P + P],
                                          kbd[:, d, c, :], start=True, stop=True)
                        return last
                    return run

                def gat_e(d, tt, bank, free):
                    def run():
                        pe.wait_ge(act_mid, A(f"gat_exp{d}"))
                        free()
                        for k in range(GROUPS):
                            last = nc.tensor.transpose(ps_m[0:GAT_ROWS, bank, k * P:(k + 1) * P],
                                                       e[d][:, tt * 320 + k * GAT_ROWS:tt * 320 + (k + 1) * GAT_ROWS], ident)
                        return last
                    return run

                def gat_o(d):
                    def run():
                        pe.wait_ge(act_mid, A(f"gat_ec{d}1"))
                        for tt in range(TT):
                            for k in range(GROUPS):
                                last = mm(mid(d)[:, tt, k * 64:(k + 1) * 64], e_t[0:GAT_ROWS, tt, k * P:(k + 1) * P],
                                          vbd[0:GAT_ROWS, d, k * 64:(k + 1) * 64], start=True, stop=True)
                        return last
                    return run

                return {"attn_proj": attn_proj, "norm_t0": norm_t0, "up0": up(0), "up1": up(1), "up2": up(2), "up3": up(3),
                        "down0": down(0), "down1": down(1), "down2": down(2), "down": down(3), "x2_t": x2_t,
                        "self_feat": self_feat, "self_t": self_t, "gat_kvw": gat_kvw, "gat_k": gat_k, "gat_q0": gat_q(0),
                        "gat_q1": gat_q(1), "gat_s0": gat_s(0), "gat_s1": gat_s(1),
                        "gat_e00": gat_e(0, 0, 0, lambda: pe.wait_ge(dve_mid, D("gat_m1"))),
                        "gat_e01": gat_e(0, 1, 1, lambda: None),
                        "gat_e10": gat_e(1, 0, 1, lambda: pe.wait_ge(act_mid, A("gat_ec01"))),
                        "gat_e11": gat_e(1, 1, 0, lambda: pe.wait_ge(dve_mid, D("gat_n0"))),
                        "gat_o0": gat_o(0), "gat_o1": gat_o(1)}

            def back_steps(b):
                def A(n): return step_at(ACT_BACK, n, b)
                def D(n): return step_at(DVE_BACK, n, b)

                def norm_t(n):
                    def run():
                        pe.wait_ge(dve_back, D(f"z{n}"))
                        return turn(back(0), tile_b(4))
                    return run

                def lin_q():
                    pe.wait_ge(act_back, A("norm_h1"))
                    return to_tokens(back(1), h_back, w["w_lq"])

                def lin_k():
                    return to_features(back(0), h_back, w["w_lk"])

                def lin_v():
                    pe.wait_ge(dve_back, D("lin_qb"))
                    return to_tokens(back(1), h_back, w["w_lv"])

                def lin_k_t():
                    pe.wait_ge(act_back, A("lin_kexp"))
                    for c in range(DC):
                        for tt in range(TT):
                            last = nc.tensor.transpose(back(0)[:, tt, c * P:(c + 1) * P], tile_b(2)[:, c, tt * P:(tt + 1) * P], ident)
                    return last

                def lin_q_t():
                    pe.wait_ge(dve_back, D("lin_vb"))
                    return turn(back(1), tile_b(0))

                def lin_ctx():
                    pe.wait_ge(act_back, A("lin_k_c"))
                    for c in range(DC):
                        for tt in range(TT):
                            last = mm(ps_b[:, 0, c * P:(c + 1) * P], tile_b(3)[:, tt, c * P:(c + 1) * P],
                                      tile_b(1)[:, tt, c * P:(c + 1) * P], start=(tt == 0), stop=(tt == 1))
                    return last

                def lin_y():
                    pe.wait_ge(act_back, A("lin_q_c"))
                    pe.wait_ge(dve_back, D("ctx_s"))
                    for tt in range(TT):
                        for c in range(DC):
                            last = mm(back(1)[:, tt, c * P:(c + 1) * P], tile_b(4)[:, c, tt * P:(tt + 1) * P],
                                      tmp_back[:, 2, c * P:(c + 1) * P], start=True, stop=True)
                    return last

                def lin_out():
                    pe.wait_ge(dve_back, D("silu2"))
                    return to_tokens(back(1), tile_b(2), w["w_lo"])

                def q3():
                    pe.wait_ge(act_back, A("norm_h3"))
                    return to_features(back(1), h_back, w["w_q3"])

                def k3():
                    return to_features(back(0), h_back, w["w_k3"])

                def v3():
                    pe.wait_ge(act_back, A("q3_c"))
                    return to_tokens(back(1), h_back, w["w_v3"])

                def s3():
                    pe.wait_ge(act_back, A("k3_c"))
                    for tt in range(TT):
                        for k in range(DC):
                            last = mm(back(0)[:, tt, :], tile_b(0)[:, k, tt * P:(tt + 1) * P], tile_b(1)[:, k, :],
                                      start=(k == 0), stop=(k == 1))
                    return last

                def p3_t():
                    pe.wait_ge(dve_back, D("p3_n"))
                    return turn(back(1), tile_b(3))

                def o3():
                    pe.wait_ge(act_back, A("p3_c"))
                    for c in range(DC):
                        for kt in range(TT):
                            last = mm(back(0)[:, c, :], tile_b(2)[:, kt, c * P:(c + 1) * P], tile_b(4)[:, kt, :],
                                      start=(kt == 0), stop=(kt == 1))
                    return last

                def proj3():
                    pe.wait_ge(act_back, A("o3_c"))
                    return to_tokens(back(1), tile_b(3), w["w_p3"])

                def up(j):
                    def run():
                        pe.wait_ge(act_back, A("norm_h4") if j == 0 else A(f"gelu3_{j - 1}"))
                        return to_features(back(1), h_back, w["w1_3"], first=j * 256)
                    return run

                def down(j):
                    def run():
                        pe.wait_ge(act_back, A(f"gelu3_{j}"))
                        return down_part(back(0), g_back[:, j % 2], w["w2_3"], j)
                    return run

                return {"norm_t1": norm_t(1), "lin_q": lin_q, "lin_k": lin_k, "lin_v": lin_v, "lin_k_t": lin_k_t,
                        "lin_q_t": lin_q_t, "lin_ctx": lin_ctx, "lin_y": lin_y, "norm_t2": norm_t(2), "lin_out": lin_out,
                        "norm_t3": norm_t(3), "q3": q3, "k3": k3, "v3": v3, "s3": s3, "p3_t": p3_t, "o3": o3, "proj3": proj3,
                        "norm_t4": norm_t(4), "up3_0": up(0), "up3_1": up(1), "up3_2": up(2), "up3_3": up(3),
                        "down3_0": down(0), "down3_1": down(1), "down3_2": down(2), "down3": down(3)}

            def body(i, front, middle, rear, pre):
                mids = mid_steps(i - 1) if middle else {}
                backs = back_steps(i - 2) if rear else {}

                def run_mid(place):
                    for name in MID_AT[place] if middle else ():
                        mids[name]().then_inc(pe_mid, 1)

                def run_back(place):
                    for name in BACK_AT[place] if rear else ():
                        backs[name]().then_inc(pe_back, 1)

                if front:
                    proj("qk", 0, i)
                    proj("v", 0, i)
                run_back(0)
                run_mid(0)
                if front:
                    scores(0, i)
                    proj("qk", 1, i)
                for hd in range(HEADS):
                    if front:
                        turn_probs(hd, i)
                        if hd + 1 < HEADS:
                            scores(hd + 1, i)
                    run_mid(hd + 1)
                    if front:
                        weigh(hd, i)
                        if hd % 2 == 1 and (hd + 3) // 2 < PAIRS:
                            proj("qk", (hd + 3) // 2, i)
                        if hd % 4 == 2 and hd // 4 + 1 < GROUPS:
                            proj("v", hd // 4 + 1, i)
                        if hd == 14 and pre:
                            prelude(i + 1)
                    run_back(hd + 1)
                run_mid(17)
                run_back(17)
                if isinstance(i, int) and i == 0:
                    pe.wait_ge(rest_w_in, 16 * (len(WEIGHTS) - 1))

            prelude(0)
            run_schedule(pe, body)

        @block.scalar
        def _(act):
            go = nc.scalar.activation
            act.wait_ge(small_in, 16 * SMALL_LOADS)
            go(za[:, :, 0:BATCH], ha[:, :, 0:BATCH], ACT.Tanh, scale=0.5).then_inc(setup_act, 1)
            go(qs_cols[:, 0, :], cols[:, COLS["bq_a"][0]:COLS["bq_a"][0] + DC], ACT.Copy, scale=GAT_D ** -0.5)
            go(qs_cols[:, 1, :], cols[:, COLS["bq_b"][0]:COLS["bq_b"][0] + DC], ACT.Copy, scale=GAT_D ** -0.5).then_inc(act_mid, 1)
            go(qs_cols[:, 2, :], cols[:, COLS["q_b3"][0]:COLS["q_b3"][0] + DC], ACT.Copy, scale=DIM ** -0.5).then_inc(act_back, 1)
            act.wait_ge(setup_dve, SETUP_DVE)
            act.wait_ge(setup_pe, PIECES)

            def affine(dst, src, scale_cols, shift_cols):
                for c in range(DC):
                    last = go(dst[:, c, :], src[:, c, :], ACT.Identity, bias=shift_cols[:, c:c + 1], scale=scale_cols[:, c:c + 1])
                return last

            def prelude(i):
                act.wait_ge(za_turned, i + 1)
                act.wait_ge(cols_a_ready, i + 1)
                affine(ha, ps_p[:].rearrange("p (a b) -> p a b", a=2), cols_a[:, 0], cols_a[:, 1]).then_inc(ha_ready, 1)

            def copy_proj(kind, k, i):
                act.wait_ge(projected, proj_at(kind, k, i))
                if kind == "qk":
                    go(qk[:, k % 2, 0, :], ps_p[:, 0:TOK], ACT.Copy, scale=DH ** -0.5)
                    last = go(qk[:, k % 2, 1, :], ps_p[:, TOK:2 * TOK], ACT.Copy)
                else:
                    last = go(v[:, k % 2], ps_p[:].rearrange("p (a b) -> p a b", a=2), ACT.Copy)
                last.then_inc(proj_copied, 1)

            def exps(hd, i):
                act.wait_ge(max_ready, i * HEADS + hd + 1)
                for tt in range(TT):
                    last = go(probs[:, hd % 2, tt, :], ps_s[:, tt * TOK:(tt + 1) * TOK], ACT.Exp,
                              bias=neg_max[:, hd % 2, tt:tt + 1], accum_out=row_sum[:, hd % 2, tt:tt + 1])
                last.then_inc(probs_ready, 1)

            def copy_o(grp, i):
                act.wait_ge(weighted, i * HEADS + GH * (grp + 1))
                if later(i):
                    act.wait_ge(pe_mid, step_at(PE_MID, "attn_proj", i - 1))
                go(o_t[:, 2 * grp:2 * grp + 2, :], ps_o[:].rearrange("p (a b) -> p a b", a=2), ACT.Copy).then_inc(o_copied, 1)

            def mid_steps(b):
                def PE(n): return step_at(PE_MID, n, b)
                def D(n): return step_at(DVE_MID, n, b)

                def norm_h0():
                    act.wait_ge(pe_mid, PE("norm_t0"))
                    act.wait_ge(dve_mid, D("cols0"))
                    affine(h_mid, mid(1), cols_mid[:, 0], cols_mid[:, 1]).then_inc(act_mid, 1)

                def gelu(j):
                    def run():
                        act.wait_ge(pe_mid, PE(f"up{j}"))
                        for c in range(2):
                            last = go(g_mid[:, j % 2, c, :], mid(0)[:, c, :], ACT.Gelu, bias=col("b1", 2 * j + c))
                        last.then_inc(act_mid, 1)
                    return run

                def x2_c():
                    act.wait_ge(pe_mid, PE("x2_t"))
                    go(tile(0), mid(0), ACT.Copy).then_inc(act_mid, 1)

                def self_c():
                    act.wait_ge(pe_mid, PE("self_t"))
                    for c in range(DC):
                        last = go(tile(2)[:, c, :], mid(0)[:, c, :], ACT.Identity, bias=col("b_self", c))
                    last.then_inc(act_mid, 1)

                def gat_qc(d):
                    def run():
                        act.wait_ge(pe_mid, PE(f"gat_q{d}"))
                        for c in range(DC):
                            last = go(tile(3 + d)[:, c, :], mid(1 - d)[:, c, :], ACT.Identity, bias=qs_cols[:, d, c:c + 1],
                                      scale=GAT_D ** -0.5)
                        last.then_inc(act_mid, 1)
                    return run

                def gat_exp(d):
                    def run():
                        act.wait_ge(dve_mid, D(f"gat_sub{d}"))
                        go(e[d], e[d], ACT.Exp).then_inc(act_mid, 1)
                    return run

                def gat_ec(d, tt, bank):
                    def run():
                        act.wait_ge(pe_mid, PE(f"gat_e{d}{tt}"))
                        go(e_t[0:GAT_ROWS, tt, :], ps_m[0:GAT_ROWS, bank, :], ACT.Copy).then_inc(act_mid, 1)
                    return run

                return {"norm_t0": norm_h0, "up0": gelu(0), "up1": gelu(1), "up2": gelu(2), "up3": gelu(3), "x2_t": x2_c,
                        "self_t": self_c, "gat_q0": gat_qc(0), "gat_q1": gat_qc(1), "gat_s0": gat_exp(0), "gat_s1": gat_exp(1),
                        "gat_e00": gat_ec(0, 0, 0), "gat_e01": gat_ec(0, 1, 1), "gat_e10": gat_ec(1, 0, 1), "gat_e11": gat_ec(1, 1, 0)}

            def back_steps(b):
                def PE(n): return step_at(PE_BACK, n, b)
                def D(n): return step_at(DVE_BACK, n, b)

                def norm_h(n):
                    def run():
                        act.wait_ge(pe_back, PE(f"norm_t{n}"))
                        if n == 1:
                            act.wait_ge(dve_back, D("cols2"))
                            s, o = COLS["norm_g"][0], COLS["norm_b"][0]
                            affine(h_back, back(0), cols[:, s:s + DC], cols[:, o:o + DC]).then_inc(act_back, 1)
                        else:
                            affine(h_back, back(0), cols_back[:, n - 2, 0], cols_back[:, n - 2, 1]).then_inc(act_back, 1)
                    return run

                def norm_h2():
                    norm_h(2)()
                    act.wait_ge(act_back, step_at(ACT_BACK, "norm_h2", b))
                    go(tile_b(1), h_back[:], ACT.Tanh, scale=0.5).then_inc(act_back, 1)

                def lin_qexp():
                    act.wait_ge(dve_back, D("lin_qsub"))
                    go(tile_b(0), tile_b(0), ACT.Exp).then_inc(act_back, 1)

                def lin_kexp():
                    act.wait_ge(dve_back, D("lin_kbias"))
                    for c in range(DC):
                        last = go(tile_b(2)[:, c, :], back(0)[:, c, :], ACT.Exp, bias=small_back[:, 1, c:c + 1],
                                  accum_out=small_back[:, 2, c:c + 1])
                    last.then_inc(act_back, 1)

                def copy(dst, k, step):
                    def run():
                        act.wait_ge(pe_back, PE(step))
                        go(dst, back(k), ACT.Copy).then_inc(act_back, 1)
                    return run

                def q3_c():
                    act.wait_ge(pe_back, PE("q3"))
                    for c in range(DC):
                        last = go(tile_b(0)[:, c, :], back(1)[:, c, :], ACT.Identity, bias=qs_cols[:, 2, c:c + 1], scale=DIM ** -0.5)
                    last.then_inc(act_back, 1)

                def k3_c():
                    act.wait_ge(pe_back, PE("k3"))
                    for c in range(DC):
                        last = go(tile_b(1)[:, c, :], back(0)[:, c, :], ACT.Identity, bias=col("k_b3", c))
                    last.then_inc(act_back, 1)

                def exp3():
                    act.wait_ge(dve_back, D("max3"))
                    for tt in range(TT):
                        last = go(tile_b(3)[:, tt, :], back(0)[:, tt, :], ACT.Exp, bias=small_back[:, 3, tt:tt + 1],
                                  accum_out=small_back[:, 4, tt:tt + 1])
                    last.then_inc(act_back, 1)

                def gelu(j):
                    def run():
                        act.wait_ge(pe_back, PE(f"up3_{j}"))
                        for c in range(2):
                            last = go(g_back[:, j % 2, c, :], back(1)[:, c, :], ACT.Gelu, bias=col("b1_3", 2 * j + c))
                        last.then_inc(act_back, 1)
                    return run

                return {"norm_t1": norm_h(1), "lin_q": lin_qexp, "lin_k": lin_kexp, "lin_k_t": copy(tile_b(3), 0, "lin_k_t"),
                        "lin_q_t": copy(tile_b(4), 1, "lin_q_t"), "norm_t2": norm_h2, "norm_t3": norm_h(3), "q3": q3_c, "k3": k3_c,
                        "s3": exp3, "p3_t": copy(tile_b(4), 1, "p3_t"), "o3": copy(tile_b(3), 0, "o3"), "norm_t4": norm_h(4),
                        "up3_0": gelu(0), "up3_1": gelu(1), "up3_2": gelu(2), "up3_3": gelu(3)}

            def body(i, front, middle, rear, pre):
                mids = mid_steps(i - 1) if middle else {}
                backs = back_steps(i - 2) if rear else {}

                def run(at, steps, place):
                    for name in at[place]:
                        if name in steps:
                            steps[name]()
                if front:
                    copy_proj("qk", 0, i)
                    copy_proj("v", 0, i)
                run(BACK_AT, backs, 0)
                run(MID_AT, mids, 0)
                if front:
                    exps(0, i)
                    copy_proj("qk", 1, i)
                for hd in range(HEADS):
                    if front and hd + 1 < HEADS:
                        exps(hd + 1, i)
                    run(MID_AT, mids, hd + 1)
                    if front:
                        if hd % 4 == 3:
                            copy_o(hd // 4, i)
                        if hd % 2 == 1 and (hd + 3) // 2 < PAIRS:
                            copy_proj("qk", (hd + 3) // 2, i)
                        if hd % 4 == 2 and hd // 4 + 1 < GROUPS:
                            copy_proj("v", hd // 4 + 1, i)
                        if hd == 14 and pre:
                            prelude(i + 1)
                    run(BACK_AT, backs, hd + 1)
                run(MID_AT, mids, 17)
                run(BACK_AT, backs, 17)

            prelude(0)
            run_schedule(act, body)

        @block.vector
        def _(dve):
            V = nc.vector
            tt_ = V.tensor_tensor

            dve.wait_ge(setup_act, 1)
            dve.wait_ge(small_in, 16 * SMALL_LOADS)
            V.scalar_tensor_tensor(za[:, :, 0:BATCH], za[:, :, 0:BATCH], 1.0, ha[:, :, 0:BATCH], ALU.add, ALU.mult).then_inc(setup_dve, 1)
            dve.wait_ge(setup_dve, 1)
            V.tensor_scalar(za[:, :, 0:BATCH], za[:, :, 0:BATCH], 0.5, None, ALU.mult).then_inc(setup_dve, 1)
            srow = {n: setup_in_rows[:, k, :] for k, n in enumerate(SETUP_ROWS)}
            dve.wait_ge(setup_pe, PIECES)
            tt_(setup_rows[:, 0:DIM], ps_o[0:BATCH, 0:DIM], srow["mod_g"][0:BATCH], ALU.add)
            tt_(setup_rows[:, DIM:2 * DIM], ps_o[0:BATCH, DIM:2 * DIM], srow["mod_m"][0:BATCH], ALU.add)
            V.tensor_copy(setup_rows[:, 2 * DIM:], ps_t[0:BATCH, 0:DIM]).then_inc(setup_dve, 1)
            ncols = 5 * 2 * DC * BATCH
            mod = tmp_flat[:, 1024:1024 + ncols]
            scaled0 = tmp_flat[:, 2048:2048 + ncols // 2]
            for lo, hi, k in ((0, 512, 0), (512, ncols, 1)):
                n0, n1 = lo // BATCH + COLS["mod_b"][0], hi // BATCH + COLS["mod_b"][0]
                last = tt_(mod[:, lo:hi].rearrange("p (n b) -> p n b", b=BATCH),
                           ps_b[:, k, 0:hi - lo].rearrange("p (n b) -> p n b", b=BATCH),
                           cols[:, n0:n1].unsqueeze(2).broadcast_to([P, n1 - n0, BATCH]), ALU.add)
            last.then_inc(setup_dve, 1)
            dve.wait_ge(setup_dve, 4)
            mod5 = mod.rearrange("p (n s c b) -> p n s c b", n=5, s=2, c=DC)
            for n in range(5):
                for c in range(DC):
                    k = n * DC + c
                    jw, j0 = COLS["mod_w"][0] + k, COLS["mod_0"][0] + k
                    V.tensor_scalar(col_table[:, :, n, 0, c], mod5[:, n, 0, c, :], 1.0, cols[:, jw:jw + 1], ALU.add, ALU.mult)
                    last = V.tensor_scalar(scaled0[:, k * BATCH:(k + 1) * BATCH], mod5[:, n, 0, c, :],
                                           1.0, cols[:, j0:j0 + 1], ALU.add, ALU.mult)
            last.then_inc(setup_dve, 1)
            dve.wait_ge(setup_dve, 5)
            for n in range(5):
                for c in range(DC):
                    k = n * DC + c
                    tt_(col_table[:, :, n, 1, c], scaled0[:, k * BATCH:(k + 1) * BATCH], mod5[:, n, 1, c, :], ALU.add)
            V.memset(minus_half[:], -0.5)
            V.memset(eps[:, 0, :], EPS[0])
            V.memset(eps[:, 1, :], EPS[1])
            tt_(gat_row[:], srow["bout_a"], srow["bout_b"], ALU.add).then_inc(setup_dve, 1)
            dve.wait_ge(setup_dve, 6)
            tt_(gat_row[:], gat_row[:], srow["b_self"], ALU.add).then_inc(setup_dve, 1)
            V.memset(wait_pad[:, 0:1], 0.0).then_inc(dve_mid, 1)
            V.memset(wait_pad[:, 1:2], 0.0).then_inc(dve_back, 1)

            def norm_stats(dst, x):
                for tt in range(TT):
                    last = V.bn_stats(dst[:, tt, :], x[:, tt, :])
                return last

            def norm_mv(mv, src):
                V.memset(wait_pad[:, 2:3], 0.0)
                for tt in range(TT):
                    last = V.bn_aggr(mv[:, tt, :], src[:, tt, :])
                return last

            def norm_z(dst, x, mv, rstd, centre=True):
                for tt in range(TT):
                    if centre:
                        last = V.tensor_scalar(dst[:, tt, :], x[:, tt, :], mv[:, tt, 0:1], rstd[:, tt:tt + 1], ALU.subtract, ALU.mult)
                    else:
                        last = V.tensor_scalar(dst[:, tt, :], x[:, tt, :], rstd[:, tt:tt + 1], None, ALU.mult)
                return last

            def prelude_stats(i):
                dve.wait_ge(x_in, 16 * i + 16)
                norm_stats(stat_a, xa).then_inc(stats_a_ready, 1)
                dve.wait_ge(stats_a_ready, i + 1)
                norm_mv(mv_a, stat_a).then_inc(mv_a_ready, 1)

            def prelude_z(i):
                if later(i):
                    dve.wait_ge(ha_ready, i)
                else:
                    dve.wait_ge(setup_dve, SETUP_DVE)
                V.tensor_copy(cols_a[:], col_table[:, i, 0, :, :]).then_inc(cols_a_ready, 1)
                dve.wait_ge(rstd_a_ready, i + 1)
                norm_z(za, xa, mv_a, rstd_a).then_inc(za_ready, 1)

            def maxes(hd, i):
                dve.wait_ge(scored, i * HEADS + hd + 1)
                V.tensor_reduce(neg_max[:, hd % 2, :], ps_s[:].rearrange("p (a b) -> p a b", a=2), AX.X, ALU.max,
                                negate=True).then_inc(max_ready, 1)

            def normalise(hd, i):
                dve.wait_ge(probs_ready, i * HEADS + hd + 1)
                V.reciprocal(row_rec[:, hd % 2, :], row_sum[:, hd % 2, :]).then_inc(sum_inverted, 1)
                dve.wait_ge(sum_inverted, i * HEADS + hd + 1)
                for tt in range(TT):
                    last = V.tensor_scalar(probs[:, hd % 2, tt, :], probs[:, hd % 2, tt, :], row_rec[:, hd % 2, tt:tt + 1], None, ALU.mult)
                last.then_inc(probs_normal, 1)

            def copy_probs(hd, i):
                dve.wait_ge(probs_turned, i * HEADS + hd + 1)
                V.tensor_copy(probs_t[:, hd % 2], ps_t[:].rearrange("p (a b) -> p a b", a=2)).then_inc(probs_copied, 1)

            def mid_steps(b):
                def PE(n): return step_at(PE_MID, n, b)
                def A(n): return step_at(ACT_MID, n, b)
                def D(n): return step_at(DVE_MID, n, b)
                def PO(n): return step_at(POOL_MID, n, b)

                def attn_proj():
                    dve.wait_ge(act_mid, b * len(ACT_MID) + 1)
                    V.tensor_copy(cols_mid[:], col_table[:, b, 1, :, :]).then_inc(dve_mid, 1)
                    dve.wait_ge(dve_mid, D("cols0"))
                    dve.wait_ge(gate_in, 16 * b + 16)
                    dve.wait_ge(pe_mid, PE("attn_proj"))
                    tt_(x_mid[:], mid(0), per_tile(g_msa[:]), ALU.mult).then_inc(dve_mid, 1)
                    dve.wait_ge(dve_mid, D("x1_gated"))
                    dve.wait_ge(resid_ready, b + 1)
                    tt_(x_mid[:], x_mid[:], x_resid[:], ALU.add).then_inc(dve_mid, 1)
                    dve.wait_ge(dve_mid, D("x1"))
                    norm_stats(stat_mid, x_mid).then_inc(dve_mid, 1)
                    dve.wait_ge(dve_mid, D("stats0"))
                    norm_mv(mv_mid, stat_mid).then_inc(dve_mid, 1)

                def norm_t0():
                    dve.wait_ge(pool_mid, PO("rstd0"))
                    norm_z(tile(5), x_mid, mv_mid, rstd_mid).then_inc(dve_mid, 1)

                def up0():
                    dve.wait_ge(adj_in, 16 * b + 16)
                    dve.wait_ge(dve_mid, D("z0"))
                    tt_(adj_mul, adj[:], w_bias[:].unsqueeze(1).broadcast_to([P, 2 * TT * NONGT, LABELS]), ALU.mult).then_inc(dve_mid, 1)
                    dve.wait_ge(dve_mid, D("adj_w"))
                    V.tensor_reduce(adj_v[:, 0, :], adj_mul, AX.X, ALU.add)
                    V.tensor_reduce(adj_v[:, 1, :], adj[:], AX.X, ALU.add).then_inc(dve_mid, 1)

                def up1():
                    dve.wait_ge(dve_mid, D("adj_sum"))
                    V.tensor_scalar(adj_v[:, 2, :], adj_v[:, 1, :], 0.0, None, ALU.is_gt).then_inc(dve_mid, 1)
                    dve.wait_ge(dve_mid, D("adj_on"))
                    V.tensor_scalar(adj_v[:, 3, :], adj_v[:, 2, :], NEG, -NEG, ALU.mult, ALU.add).then_inc(dve_mid, 1)
                    dve.wait_ge(dve_mid, D("adj_neg"))
                    V.scalar_tensor_tensor(adj_v[:, 3, :], adj_v[:, 0, :], col("b_bias"), adj_v[:, 3, :], ALU.add, ALU.add).then_inc(dve_mid, 1)

                def down():
                    dve.wait_ge(rows_in, 16 * b + 16)
                    dve.wait_ge(pool_mid, PO("xr2"))
                    dve.wait_ge(pe_mid, PE("down"))
                    tt_(x_mid[:], mid(1), per_tile(mod_rows[:, 0, :]), ALU.mult).then_inc(dve_mid, 1)
                    dve.wait_ge(dve_mid, D("x2_gated"))
                    tt_(x_mid[:], x_mid[:], resid_mid[:], ALU.add).then_inc(dve_mid, 1)
                    dve.wait_ge(dve_mid, D("x2"))
                    V.tensor_reduce(small_mid[:, 0, 0:TT], x_mid[:], AX.X, ALU.add).then_inc(dve_mid, 1)
                    dve.wait_ge(dve_mid, D("row_sum"))
                    V.tensor_scalar(small_mid[:, 0, TT:2 * TT], small_mid[:, 0, 0:TT], 0.0, None, ALU.not_equal).then_inc(dve_mid, 1)

                def self_feat():
                    dve.wait_ge(pe_mid, PE("self_feat"))
                    dve.wait_ge(dve_mid, D("row_on"))
                    for tt in range(TT):
                        last = V.scalar_tensor_tensor(tile(1)[:, tt, :], mod_rows[:, 1, :], small_mid[:, 0, TT + tt:TT + tt + 1],
                                                      mid(1)[:, tt, :], ALU.mult, ALU.add)
                    last.then_inc(dve_mid, 1)

                def self_t():
                    dve.wait_ge(act_mid, A("self_c"))
                    for c in range(DC):
                        last = V.tensor_copy(kv_rep[:, c], tile(2)[:, c, 0:NONGT].unsqueeze(1).broadcast_to([P, GH, NONGT]))
                    last.then_inc(dve_mid, 1)

                def gat_kvw():
                    dve.wait_ge(pe_mid, PE("gat_kvw"))
                    tt_(vbd[0:GAT_ROWS], mid(1, GAT_ROWS), m["head_v"][0:GAT_ROWS].unsqueeze(1).broadcast_to([GAT_ROWS, 2, DIM]),
                        ALU.mult).then_inc(dve_mid, 1)

                def gat_k():
                    dve.wait_ge(pe_mid, PE("gat_k"))
                    for d in range(2):
                        for c in range(DC):
                            o = (d * DC + c) * NONGT
                            last = V.scalar_tensor_tensor(kbd[:, d, c, :].rearrange("p (a b) -> p a b", b=NONGT),
                                                          ps_m[:, 0, o:o + NONGT].unsqueeze(1).broadcast_to([P, 8, NONGT]),
                                                          col("bk_a" if d == 0 else "bk_b", c),
                                                          m["head_k"].rearrange("p (a b) -> p a b", b=NONGT), ALU.add, ALU.mult)
                    last.then_inc(dve_mid, 1)

                def gat_s(d):
                    on = adj_v[:, 2, d * TT * NONGT:(d + 1) * TT * NONGT].rearrange("p (t n) -> p t n", t=TT)
                    bias = adj_v[:, 3, d * TT * NONGT:(d + 1) * TT * NONGT].rearrange("p (t n) -> p t n", t=TT)
                    ed = e[d].rearrange("p (t h n) -> p t h n", t=TT, n=NONGT)
                    ed3 = e[d].rearrange("p (r n) -> p r n", n=NONGT)
                    wide = [P, TT, GAT_H, NONGT]

                    def run():
                        if d == 0:
                            dve.wait_ge(pool_mid, PO("acc"))
                        dve.wait_ge(pe_mid, PE(f"gat_s{d}"))
                        tt_(ed, ps_m[:, :, 0:320].rearrange("p t (h n) -> p t h n", n=NONGT), on.unsqueeze(2).broadcast_to(wide),
                            ALU.mult).then_inc(dve_mid, 1)
                        dve.wait_ge(dve_mid, D(f"gat_m{d}"))
                        tt_(ed, ed, bias.unsqueeze(2).broadcast_to(wide), ALU.add).then_inc(dve_mid, 1)
                        dve.wait_ge(dve_mid, D(f"gat_b{d}"))
                        V.tensor_reduce(small_mid[:, 1 + d, :], ed3, AX.X, ALU.max).then_inc(dve_mid, 1)
                        dve.wait_ge(dve_mid, D(f"gat_max{d}"))
                        tt_(ed3, ed3, small_mid[:, 1 + d, :].unsqueeze(2).broadcast_to([P, 2 * GAT_H, NONGT]), ALU.subtract).then_inc(dve_mid, 1)
                    return run

                def gat_e(d):
                    def run():
                        dve.wait_ge(act_mid, A(f"gat_exp{d}"))
                        V.tensor_reduce(small_mid[:, 1 + d, :], e[d].rearrange("p (r n) -> p r n", n=NONGT), AX.X, ALU.add).then_inc(dve_mid, 1)
                        dve.wait_ge(dve_mid, D(f"gat_den{d}"))
                        V.reciprocal(small_mid[:, 1 + d, :], small_mid[:, 1 + d, :]).then_inc(dve_mid, 1)
                    return run

                def gat_o(d):
                    def run():
                        dve.wait_ge(pe_mid, PE(f"gat_o{d}"))
                        dve.wait_ge(dve_mid, D("gat_rec1" if d == 0 else "gat_acc0"))
                        tt_(tile(0).rearrange("p t (h g) -> p (t h) g", g=GAT_D), ps_m[:, d, :].rearrange("p (r g) -> p r g", g=GAT_D),
                            small_mid[:, 1 + d, :].unsqueeze(2).broadcast_to([P, 2 * GAT_H, GAT_D]), ALU.mult).then_inc(dve_mid, 1)
                        dve.wait_ge(dve_mid, D(f"gat_n{d}"))
                        tt_(tile(5), tile(5), tile(0), ALU.add).then_inc(dve_mid, 1)
                        if d == 1:
                            dve.wait_ge(dve_mid, D("gat_acc1"))
                            if later(b):
                                dve.wait_ge(dve_back, step_at(DVE_BACK, "z1", b - 1))
                                dve.wait_ge(pool_back, step_at(POOL_BACK, "xr4", b - 1))
                            V.scalar_tensor_tensor(x3[:], tile(5), 0.0, x_mid[:], ALU.max, ALU.add).then_inc(dve_mid, 1)
                    return run

                return {"attn_proj": attn_proj, "norm_t0": norm_t0, "up0": up0, "up1": up1, "down": down, "self_feat": self_feat,
                        "self_t": self_t, "gat_kvw": gat_kvw, "gat_k": gat_k, "gat_s0": gat_s(0), "gat_s1": gat_s(1),
                        "gat_e00": gat_e(0), "gat_e01": gat_e(1), "gat_o0": gat_o(0), "gat_o1": gat_o(1)}

            def back_steps(b):
                def PE(n): return step_at(PE_BACK, n, b)
                def A(n): return step_at(ACT_BACK, n, b)
                def D(n): return step_at(DVE_BACK, n, b)
                def PO(n): return step_at(POOL_BACK, n, b)

                def stats(n, x):
                    norm_stats(stat_back, x).then_inc(dve_back, 1)
                    dve.wait_ge(dve_back, D(f"stats{n}"))
                    norm_mv(mv_back, stat_back).then_inc(dve_back, 1)

                def zed(n, x):
                    def run():
                        dve.wait_ge(pool_back, PO(f"rstd{n}"))
                        norm_z(tile_b(4), x, mv_back, rstd_back, centre=n < 3).then_inc(dve_back, 1)
                    return run

                def norm_t1():
                    dve.wait_ge(act_back, b * len(ACT_BACK) + 1)
                    V.tensor_copy(cols_back[:], col_table[:, b, 2:5, :, :]).then_inc(dve_back, 1)
                    dve.wait_ge(dve_back, D("cols2"))
                    dve.wait_ge(dve_mid, step_at(DVE_MID, "x3", b))
                    stats(1, x3)
                    zed(1, x3)()

                def lin_q():
                    dve.wait_ge(pe_back, PE("lin_q"))
                    tt_(tile_b(0), back(1), per_tile(row("bq")), ALU.add).then_inc(dve_back, 1)
                    q3 = tile_b(0).rearrange("p t (h d) -> p (t h) d", d=16)
                    dve.wait_ge(dve_back, D("lin_qb"))
                    V.tensor_reduce(small_back[:, 0, :], q3, AX.X, ALU.max).then_inc(dve_back, 1)
                    dve.wait_ge(dve_back, D("lin_qmax"))
                    tt_(q3, q3, small_back[:, 0, :].unsqueeze(2).broadcast_to([P, 32, 16]), ALU.subtract).then_inc(dve_back, 1)

                def lin_k():
                    dve.wait_ge(pe_back, PE("lin_k"))
                    V.tensor_reduce(small_back[:, 1, 2:4], back(0), AX.X, ALU.max).then_inc(dve_back, 1)
                    k0 = COLS["bk"][0]
                    dve.wait_ge(dve_back, D("lin_kmax"))
                    tt_(small_back[:, 1, 4:6], small_back[:, 1, 2:4], cols[:, k0:k0 + DC], ALU.add).then_inc(dve_back, 1)
                    dve.wait_ge(dve_back, D("lin_kmb"))
                    tt_(small_back[:, 1, 0:2], cols[:, k0:k0 + DC], small_back[:, 1, 4:6], ALU.subtract).then_inc(dve_back, 1)

                def lin_v():
                    dve.wait_ge(pe_back, PE("lin_v"))
                    tt_(tile_b(1), back(1), per_tile(row("bv")), ALU.add).then_inc(dve_back, 1)

                def lin_k_t():
                    dve.wait_ge(act_back, A("lin_qexp"))
                    V.tensor_reduce(small_back[:, 0, :], tile_b(0).rearrange("p t (h d) -> p (t h) d", d=16), AX.X, ALU.add).then_inc(dve_back, 1)
                    dve.wait_ge(dve_back, D("lin_qden"))
                    V.reciprocal(small_back[:, 0, :], small_back[:, 0, :]).then_inc(dve_back, 1)
                    dve.wait_ge(act_back, A("lin_kexp"))
                    V.reciprocal(small_back[:, 2, 2:4], small_back[:, 2, 0:2]).then_inc(dve_back, 1)

                def lin_ctx():
                    dve.wait_ge(pe_back, PE("lin_ctx"))
                    dve.wait_ge(dve_back, D("lin_krec"))
                    for c in range(DC):
                        last = V.scalar_tensor_tensor(tmp_back[:, 2, c * P:(c + 1) * P], ps_b[:, 0, c * P:(c + 1) * P],
                                                      small_back[:, 2, 2 + c:3 + c], m["head_c"], ALU.mult, ALU.mult)
                    last.then_inc(dve_back, 1)

                def lin_y():
                    dve.wait_ge(pe_back, PE("lin_y"))
                    tt_(tile_b(0).rearrange("p t (h d) -> p (t h) d", d=16), ps_b[:, 1, :].rearrange("p (r d) -> p r d", d=16),
                        small_back[:, 0, :].unsqueeze(2).broadcast_to([P, 32, 16]), ALU.mult).then_inc(dve_back, 1)
                    dve.wait_ge(dve_back, D("y"))
                    stats(2, tile_b(0))

                def norm_t2():
                    zed(2, tile_b(0))()
                    dve.wait_ge(act_back, A("lin_tanh"))
                    V.scalar_tensor_tensor(tile_b(2), tile_b(1), 1.0, h_back[:], ALU.add, ALU.mult).then_inc(dve_back, 1)

                def lin_out():
                    dve.wait_ge(cond_in, 16 * b + 16)
                    dve.wait_ge(pe_back, PE("lin_out"))
                    for tt in range(TT):
                        last = V.scalar_tensor_tensor(x_back[:, tt, :], back(1)[:, tt, :], 0.5, cond_row[:], ALU.mult, ALU.mult)
                    last.then_inc(dve_back, 1)
                    dve.wait_ge(dve_back, D("x4_gated"))
                    dve.wait_ge(pool_back, PO("xr4"))
                    tt_(x_back[:], x_back[:], resid_back[:], ALU.add).then_inc(dve_back, 1)
                    dve.wait_ge(dve_back, D("x4"))
                    stats(3, x_back)

                def v3():
                    dve.wait_ge(pe_back, PE("v3"))
                    tt_(tile_b(2), back(1), per_tile(row("v_b3")), ALU.add).then_inc(dve_back, 1)

                def s3():
                    dve.wait_ge(pe_back, PE("s3"))
                    V.tensor_reduce(small_back[:, 3, 0:TT], back(0), AX.X, ALU.max, negate=True).then_inc(dve_back, 1)

                def p3_t():
                    dve.wait_ge(act_back, A("exp3"))
                    V.reciprocal(small_back[:, 4, 2:4], small_back[:, 4, 0:2]).then_inc(dve_back, 1)
                    dve.wait_ge(dve_back, D("rec3"))
                    for tt in range(TT):
                        last = V.tensor_scalar(tile_b(3)[:, tt, :], tile_b(3)[:, tt, :], small_back[:, 4, 2 + tt:3 + tt], None, ALU.mult)
                    last.then_inc(dve_back, 1)

                def proj3():
                    dve.wait_ge(pool_back, PO("xr5"))
                    dve.wait_ge(pe_back, PE("proj3"))
                    tt_(x_back[:], back(1), resid_back[:], ALU.add).then_inc(dve_back, 1)
                    dve.wait_ge(dve_back, D("x5"))
                    stats(4, x_back)

                def down3():
                    dve.wait_ge(pool_back, PO("xr6"))
                    dve.wait_ge(stored, 16 * b + 16)
                    dve.wait_ge(pe_back, PE("down3"))
                    tt_(y_out[:], back(0), resid_back[:], ALU.add).then_inc(dve_back, 1)

                return {"norm_t1": norm_t1, "lin_q": lin_q, "lin_k": lin_k, "lin_v": lin_v, "lin_k_t": lin_k_t, "lin_ctx": lin_ctx,
                        "lin_y": lin_y, "norm_t2": norm_t2, "lin_out": lin_out, "norm_t3": zed(3, x_back), "v3": v3, "s3": s3,
                        "p3_t": p3_t, "proj3": proj3, "norm_t4": zed(4, x_back), "down3": down3}

            def body(i, front, middle, rear, pre):
                mids = mid_steps(i - 1) if middle else {}
                backs = back_steps(i - 2) if rear else {}

                def run(at, steps, place):
                    for name in at[place]:
                        if name in steps:
                            steps[name]()
                run(BACK_AT, backs, 0)
                run(MID_AT, mids, 0)
                if front:
                    maxes(0, i)
                    normalise(0, i)
                for hd in range(HEADS):
                    if front:
                        copy_probs(hd, i)
                        if hd + 1 < HEADS:
                            maxes(hd + 1, i)
                    run(MID_AT, mids, hd + 1)
                    if hd == 11 and pre:
                        prelude_stats(i + 1)
                    if hd == 13 and pre:
                        prelude_z(i + 1)
                    if front and hd + 1 < HEADS:
                        normalise(hd + 1, i)
                    run(BACK_AT, backs, hd + 1)
                run(MID_AT, mids, 17)
                run(BACK_AT, backs, 17)

            prelude_stats(0)
            prelude_z(0)
            run_schedule(dve, body)

        @block.gpsimd
        def _(pool):
            G = nc.gpsimd
            pool.wait_ge(setup_dve, SETUP_DVE)
            G.memset(ms_back[:, 0], 0.0).then_inc(pool_mid, 1)
            G.memset(ms_back[:, 1], 0.0).then_inc(pool_back, 1)

            def prelude(i):
                pool.wait_ge(mv_a_ready, i + 1)
                G.tensor_tensor(var_a[:], mv_a[:, :, 1], eps[:, 0, :], ALU.add).then_inc(var_a_ready, 1)
                pool.wait_ge(var_a_ready, i + 1)
                G.tensor_tensor(rstd_a[:], var_a[:], minus_half[:], ALU.pow).then_inc(rstd_a_ready, 1)

            def front_resid(i):
                pool.wait_ge(gate_in, 16 * i + 16)
                pool.wait_ge(x_in, 16 * i + 16)
                G.tensor_tensor(gated_row[:], g_msa[:], row("b_out"), ALU.mult).then_inc(gated_row_ready, 1)
                pool.wait_ge(gated_row_ready, i + 1)
                if later(i):
                    pool.wait_ge(dve_mid, step_at(DVE_MID, "x1", i - 1))
                G.tensor_tensor(x_resid[:], xa[:], per_tile(gated_row[:]), ALU.add).then_inc(resid_ready, 1)

            def mid_steps(b):
                def D(n): return step_at(DVE_MID, n, b)
                def PO(n): return step_at(POOL_MID, n, b)

                def attn_proj():
                    pool.wait_ge(dve_mid, D("mv0"))
                    G.tensor_tensor(var_mid[:], mv_mid[:, :, 1], eps[:, 0, :], ALU.add).then_inc(pool_mid, 1)
                    pool.wait_ge(pool_mid, PO("var0"))
                    G.tensor_tensor(rstd_mid[:], var_mid[:], minus_half[:], ALU.pow).then_inc(pool_mid, 1)
                    pool.wait_ge(rows_in, 16 * b + 16)
                    G.tensor_tensor(gate_bias_mid[:], mod_rows[:, 0, :], row("b2"), ALU.mult).then_inc(pool_mid, 1)
                    pool.wait_ge(pool_mid, PO("gb2"))
                    G.tensor_tensor(resid_mid[:], x_mid[:], per_tile(gate_bias_mid[:]), ALU.add).then_inc(pool_mid, 1)

                def self_feat():
                    pool.wait_ge(dve_mid, D("u"))
                    G.tensor_tensor(tile(5), tile(1), per_tile(gat_row[:]), ALU.add).then_inc(pool_mid, 1)

                return {"attn_proj": attn_proj, "self_feat": self_feat}

            def back_steps(b):
                def D(n): return step_at(DVE_BACK, n, b)
                def PO(n): return step_at(POOL_BACK, n, b)

                def rstd(n):
                    pool.wait_ge(dve_back, D(f"mv{n}"))
                    if n >= 3:
                        G.tensor_tensor(ms_back[:, 0, :], mv_back[:, :, 0], mv_back[:, :, 0], ALU.mult).then_inc(pool_back, 1)
                        pool.wait_ge(pool_back, PO(f"sq{n}"))
                        G.tensor_tensor(ms_back[:, 1, :], ms_back[:, 0, :], mv_back[:, :, 1], ALU.add).then_inc(pool_back, 1)
                        pool.wait_ge(pool_back, PO(f"ms{n}"))
                        G.tensor_tensor(var_back[:], ms_back[:, 1, :], eps[:, 1, :], ALU.add).then_inc(pool_back, 1)
                    else:
                        G.tensor_tensor(var_back[:], mv_back[:, :, 1], eps[:, 0, :], ALU.add).then_inc(pool_back, 1)
                    pool.wait_ge(pool_back, PO(f"var{n}"))
                    G.tensor_tensor(rstd_back[:], var_back[:], minus_half[:], ALU.pow).then_inc(pool_back, 1)

                def norm_t1():
                    rstd(1)
                    pool.wait_ge(cond_in, 16 * b + 16)
                    G.tensor_tensor(gate_bias_back[:], cond_row[:], row("out_b"), ALU.mult).then_inc(pool_back, 1)
                    pool.wait_ge(pool_back, PO("gob"))
                    G.tensor_tensor(resid_back[:], x3[:], per_tile(gate_bias_back[:]), ALU.add).then_inc(pool_back, 1)

                def lin_y():
                    rstd(2)

                def lin_out():
                    rstd(3)
                    G.tensor_tensor(resid_back[:], x_back[:], per_tile(row("proj_b3")), ALU.add).then_inc(pool_back, 1)

                def proj3():
                    rstd(4)
                    G.tensor_tensor(resid_back[:], x_back[:], per_tile(row("b2_3")), ALU.add).then_inc(pool_back, 1)

                return {"norm_t1": norm_t1, "lin_y": lin_y, "lin_out": lin_out, "proj3": proj3}

            def body(i, front, middle, rear, pre):
                mids = mid_steps(i - 1) if middle else {}
                backs = back_steps(i - 2) if rear else {}

                def run(at, steps, place):
                    for name in at[place]:
                        if name in steps:
                            steps[name]()
                run(BACK_AT, backs, 0)
                run(MID_AT, mids, 0)
                for hd in range(HEADS):
                    run(MID_AT, mids, hd + 1)
                    if hd == 1 and front:
                        front_resid(i)
                    if hd == 11 and pre:
                        prelude(i + 1)
                    run(BACK_AT, backs, hd + 1)
                run(MID_AT, mids, 17)
                run(BACK_AT, backs, 17)

            prelude(0)
            run_schedule(pool, body)


def kernel(**inputs):
    import numpy as np
    import concourse.bacc as bacc
    from concourse.bass_utils import run_bass_kernel_spmd

    a = {k: np.asarray(v) for k, v in inputs.items()}

    def chunks(wt):
        return wt.reshape(wt.shape[0] // P, P, wt.shape[1]).transpose(1, 0, 2)

    def columns(vec):
        return vec.reshape(-1, P).T

    f1, f2 = "L3_cond_film1_", "L3_cond_film2_"
    w_mod, b_mod = a["L0_cond_W_mod"], a["L0_cond_b_mod"]
    parts = [(w_mod, b_mod, 1), (w_mod, b_mod, 0), (w_mod, b_mod, 4), (w_mod, b_mod, 3),
             (a["L2_cond_emb_W"], a["L2_cond_emb_b"], 0), (a["L2_cond_emb_W"], a["L2_cond_emb_b"], 1),
             (a[f1 + "w"], a[f1 + "b"], 0), (a[f1 + "w"], a[f1 + "b"], 1),
             (a[f2 + "w"], a[f2 + "b"], 0), (a[f2 + "w"], a[f2 + "b"], 1),
             (w_mod, b_mod, 2), (w_mod, b_mod, 5)]
    pieces = [chunks(wt[:, n * DIM:(n + 1) * DIM]) for wt, _, n in parts] + [chunks(a["L1_cond_W_self"][:, DIM:].T)]
    one, zero = np.ones(DIM, np.float32), np.zeros(DIM, np.float32)
    vectors = {
        "b1": a["L0_cond_b1"], "b1_3": a["L3_cond_mlp_b1"], "b_self": a["L1_cond_b_self"],
        "bq_a": a["L1_cond_bq"][0], "bq_b": a["L1_cond_bq"][1], "bk_a": a["L1_cond_bk"][0], "bk_b": a["L1_cond_bk"][1],
        "norm_g": a["L2_cond_norm_g"], "norm_b": a["L2_cond_norm_b"], "bk": a["L2_cond_bk"],
        "q_b3": a["L3_cond_q_b"], "k_b3": a["L3_cond_k_b"],
        "mod_b": np.concatenate([v[n * DIM:(n + 1) * DIM] for _, v, n in parts[:COL_PIECES]]),
        "mod_w": np.concatenate([one, one, a["L2_cond_sn_g"], a["L3_cond_norm1_w"], a["L3_cond_norm2_w"]]),
        "mod_0": np.concatenate([zero, zero, a["L2_cond_sn_b"], zero, zero]),
        "b_bias": np.broadcast_to(a["L1_cond_b_bias"], (P,)),
    }
    row_vectors = [a["L0_cond_b_out"], a["L0_cond_b2"], a["L2_cond_bq"], a["L2_cond_bv"], a["L2_cond_out_b"],
                   a["L3_cond_v_b"], a["L3_cond_proj_b"], a["L3_cond_mlp_b2"]]
    setup_row_vectors = [a["L1_cond_b_self"], a["L1_cond_bout"][0], a["L1_cond_bout"][1], b_mod[2 * DIM:3 * DIM], b_mod[5 * DIM:]]
    p = np.arange(P)[:, None]
    masks = np.concatenate([
        p == np.arange(P)[None, :],
        p // 16 == np.repeat(np.arange(8), NONGT)[None, :],
        p // NONGT == np.arange(DIM)[None, :] // GAT_D % GH,
        p // 16 == np.arange(P)[None, :] // 16], axis=1).astype(np.float32)
    mask = a["mask_BxSxSx11_ik0"]
    labels = np.stack([mask[:, :, :NONGT].reshape(BATCH, TT, P, NONGT, LABELS).transpose(0, 2, 1, 3, 4),
                       mask[:, :NONGT].transpose(0, 2, 1, 3).reshape(BATCH, TT, P, NONGT, LABELS).transpose(0, 2, 1, 3, 4)], axis=2)
    w2d = {
        "wqkv": a["L0_cond_W_qkv"], "w_out": a["L0_cond_W_out"], "w1": a["L0_cond_W1"], "w2": a["L0_cond_W2"],
        "w_self": a["L1_cond_W_self"][:, :DIM].T, "w_gq": np.concatenate([m.T for m in a["L1_cond_Wq"]], axis=1),
        "w_gk": np.concatenate([m.T for m in a["L1_cond_Wk"]], axis=1),
        "w_gout": np.concatenate([m.reshape(DIM, DIM).T for m in a["L1_cond_Wout"]], axis=1),
        "w_lq": a["L2_cond_Wq"], "w_lk": a["L2_cond_Wk"], "w_lv": a["L2_cond_Wv"], "w_lo": a["L2_cond_out_W"],
        "w_q3": a["L3_cond_q_w"], "w_k3": a["L3_cond_k_w"], "w_v3": a["L3_cond_v_w"], "w_p3": a["L3_cond_proj_w"],
        "w1_3": a["L3_cond_mlp_w1"], "w2_3": a["L3_cond_mlp_w2"],
    }
    arrays = {
        "x": a["x"].reshape(BATCH, TT, P, DIM).transpose(0, 2, 1, 3),
        "cond": a["cond_1024"], "cond_t": chunks(a["cond_1024"].T),
        "cols": np.concatenate([columns(vectors[n]) for n in COLS], axis=1),
        "rows": np.stack(row_vectors)[None], "setup_rows": np.stack(setup_row_vectors)[None], "masks": masks, "w_bias": a["L1_cond_w_bias"][None],
        "w_mod": np.stack(pieces), "adj": labels.reshape(BATCH, P, 2 * TT * NONGT, LABELS),
        **{n: chunks(w2d[n]) for n, _, _ in WEIGHTS},
    }
    arrays = {k: np.ascontiguousarray(v) for k, v in arrays.items()}

    nc = bacc.Bacc("TRN2", target_bir_lowering=False, num_devices=1)
    t = {k: nc.dram_tensor("in_" + k, v.shape, mybir.dt.from_np(v.dtype), kind="ExternalInput").ap() for k, v in arrays.items()}
    t["scratch"] = nc.dram_tensor("mod_rows_scratch", (BATCH, 3 * DIM), F32, kind="Internal").ap()
    out = nc.dram_tensor("out", (BATCH, P, TT, DIM), F32, kind="ExternalOutput").ap()
    build(nc, t, out)
    got = run_bass_kernel_spmd(nc, [{"in_" + k: v for k, v in arrays.items()}], core_ids=[0]).results[0]["out"]
    return got.reshape(BATCH, P, TT, DIM).transpose(0, 2, 1, 3).reshape(BATCH, TOK, DIM)
```

```python
from contextlib import ExitStack

import concourse.bass as bass
from concourse import mybir

F32 = mybir.dt.float32
F32R = mybir.dt.float32r
I32 = mybir.dt.int32
ALU = mybir.AluOpType
ACT = mybir.ActivationFunctionType
AX = mybir.AxisListType

P = 128
BATCH, TOK, DIM = 32, 256, 256
TT = TOK // P
DC = DIM // P
HEADS, DH = 16, 64
INNER = HEADS * DH
GROUPS, GH = 4, 4
PAIRS = HEADS // 2
MLP = 1024
FC = MLP // P
GAT_H, GAT_D, NONGT, LABELS = 16, 16, 20, 11
NEG = 9000000000000000.0
GAT_ROWS = GH * NONGT
EPS = (1e-5, 1e-6)
PIECES, COL_PIECES = 13, 10

PROJ_USES = [("qk", 0), ("v", 0), ("qk", 1)]
for _h in range(HEADS):
    if _h % 2 == 1 and (_h + 3) // 2 < PAIRS:
        PROJ_USES.append(("qk", (_h + 3) // 2))
    if _h % 4 == 2 and _h // 4 + 1 < GROUPS:
        PROJ_USES.append(("v", _h // 4 + 1))
NPROJ = len(PROJ_USES)

PE_MID = ("attn_proj", "norm_t0", "up0", "up1", "down0", "down1", "up2", "up3", "down2", "down", "x2_t", "self_feat",
          "self_t", "gat_kvw", "gat_k", "gat_q0", "gat_q1", "gat_s0", "gat_s1", "gat_e00", "gat_e01", "gat_o0",
          "gat_e10", "gat_e11", "gat_o1")
PE_BACK = ("norm_t1", "lin_q", "lin_k", "lin_v", "lin_k_t", "lin_q_t", "lin_ctx", "lin_y", "norm_t2", "lin_out",
           "norm_t3", "q3", "k3", "v3", "s3", "p3_t", "o3", "proj3", "norm_t4", "up3_0", "up3_1", "down3_0", "down3_1",
           "up3_2", "up3_3", "down3_2", "down3")
ACT_MID = ("norm_h0", "gelu0", "gelu1", "gelu2", "gelu3", "x2_c", "self_c", "gat_qc0", "gat_qc1", "gat_exp0",
           "gat_exp1", "gat_ec00", "gat_ec01", "gat_ec10", "gat_ec11")
ACT_BACK = ("norm_h1", "lin_qexp", "lin_kexp", "lin_k_c", "lin_q_c", "norm_h2", "lin_tanh", "norm_h3", "q3_c", "k3_c",
            "exp3", "p3_c", "o3_c", "norm_h4", "gelu3_0", "gelu3_1", "gelu3_2", "gelu3_3")
DVE_MID = ("cols0", "x1_gated", "x1", "stats0", "mv0", "z0", "adj_w", "adj_sum", "adj_on", "adj_neg", "adj_bias",
           "x2_gated", "x2", "row_sum", "row_on", "u", "kv_rep", "vbd", "kbd", "gat_m0", "gat_b0", "gat_max0",
           "gat_sub0", "gat_m1", "gat_b1", "gat_max1", "gat_sub1", "gat_den0", "gat_rec0", "gat_den1", "gat_rec1",
           "gat_n0", "gat_acc0", "gat_n1", "gat_acc1", "x3")
DVE_BACK = ("cols2", "stats1", "mv1", "z1", "lin_qb", "lin_qmax", "lin_qsub", "lin_kmax", "lin_kmb", "lin_kbias",
            "lin_vb", "lin_qden", "lin_qrec", "lin_krec", "ctx_s", "y", "stats2", "mv2", "z2", "silu2", "x4_gated",
            "x4", "stats3", "mv3", "z3", "v3_b", "max3", "rec3", "p3_n", "x5", "stats4", "mv4", "z4", "out")
POOL_MID = ("var0", "rstd0", "gb2", "xr2", "acc")
POOL_BACK = ("var1", "rstd1", "gob", "xr4", "var2", "rstd2", "sq3", "ms3", "var3", "rstd3", "xr5", "sq4", "ms4",
             "var4", "rstd4", "xr6")

COLS = {}
_n = 0
for _name, _k in (("b1", FC), ("b1_3", FC), ("b_self", DC), ("bq_a", DC), ("bq_b", DC), ("bk_a", DC),
                  ("bk_b", DC), ("norm_g", DC), ("norm_b", DC), ("bk", DC), ("q_b3", DC), ("k_b3", DC),
                  ("mod_b", 2 * 5 * DC), ("mod_w", 5 * DC), ("mod_0", 5 * DC), ("v_b3", DC), ("b_bias", 1)):
    COLS[_name] = (_n, _k)
    _n += _k
NCOLS = _n
WEIGHTS = (("wqkv", 2, 3 * INNER), ("w_out", INNER // P, DIM), ("w1", 2, MLP), ("w2", FC, DIM), ("w_self", 2, DIM),
           ("w_gq", 2, 2 * DIM), ("w_gk", 2, 2 * DIM), ("w_gout", 2, 2 * DIM), ("w_lq", 2, DIM), ("w_lk", 2, DIM),
           ("w_lv", 2, DIM), ("w_lo", 2, DIM), ("w_q3", 2, DIM), ("w_k3", 2, DIM), ("w_v3", 2, DIM), ("w_p3", 2, DIM),
           ("w1_3", 2, MLP), ("w2_3", FC, DIM))
SMALL_LOADS = 6
SETUP_DVE = 7
ROWS = ("b_out", "b2", "bq", "bv", "out_b", "proj_b3", "b2_3")
SETUP_ROWS = ("b_self", "bout_a", "bout_b", "mod_g", "mod_m")
MASKS = {"ident": P, "head_k": 8 * NONGT, "head_v": DIM, "head_c": P}
LAST_PLACE = 18
MID_AT = {1: ("attn_proj",), 3: ("norm_t0",), 6: ("x2_t",), 7: ("self_feat",), 8: ("self_t",), 9: ("gat_kvw", "gat_k"),
          11: ("gat_q0", "gat_q1"), 12: ("gat_s0",), 13: ("gat_s1",), 14: ("gat_e00", "gat_e01"), 15: ("gat_o0", "gat_e10"),
          16: ("gat_e11",), 17: ("gat_o1",)}
BACK_AT = {1: ("norm_t4",), 6: ("norm_t1",), 7: ("lin_q", "lin_k"), 8: ("lin_v", "lin_k_t"), 9: ("lin_q_t", "lin_ctx"),
           10: ("lin_y",), 11: ("norm_t2",), 12: ("lin_out",), 13: ("norm_t3",), 14: ("q3", "k3"), 15: ("v3", "s3"),
           16: ("p3_t",), 17: ("o3",), 18: ("proj3",)}
BACK_FIRST = 6
MLP_AT = {4: (("back", "up3_0"), ("mid", "up0"), ("back", "up3_1"), ("back", "down3_0"), ("mid", "up1"), ("mid", "down0"),
              ("back", "down3_1"), ("mid", "down1")),
          5: (("back", "up3_2"), ("mid", "up2"), ("back", "up3_3"), ("back", "down3_2"), ("mid", "up3"), ("mid", "down2"),
              ("back", "down3"), ("mid", "down"))}


def build(nc, t, out):
    with ExitStack() as ctx:
        def sb(name, shape, dt=F32):
            return ctx.enter_context(nc.sbuf_tensor(name, shape, dt))

        def sem(name):
            return ctx.enter_context(nc.semaphore(name))

        w = {n: sb("w_" + n, [P, k, c]) for n, k, c in WEIGHTS}
        cols = sb("cols", [P, NCOLS])
        rows = sb("rows", [P, len(ROWS), DIM])
        masks = sb("masks", [P, sum(MASKS.values())])
        w_bias = sb("w_bias", [P, LABELS])
        col_table = sb("col_table", [P, BATCH, 5, 2, DC])
        qs_cols = sb("qs_cols", [P, 3, DC])
        gat_row = sb("gat_row", [P, DIM])
        minus_half = sb("minus_half", [P, TT])
        eps = sb("eps", [P, 2, TT])
        wait_pad = sb("wait_pad", [P, 3])

        def col(name, k=0):
            return cols[:, COLS[name][0] + k:COLS[name][0] + k + 1]

        def row(name):
            return rows[:, ROWS.index(name), :]

        at, m = 0, {}
        for name, width in MASKS.items():
            m[name] = masks[:, at:at + width]
            at += width
        ident = m["ident"]

        def per_tile(ap):
            return ap.unsqueeze(1).broadcast_to([P, TT, ap.shape[-1]])

        xa = sb("xa", [P, TT, DIM])
        x_resid = sb("x_resid", [P, TT, DIM])
        g_msa = sb("g_msa", [P, DIM])
        ha = sb("ha", [P, DC, TOK])
        za = ha
        stat_a = sb("stat_a", [P, TT, 6])
        mv_a = sb("mv_a", [P, TT, 2])
        var_a = sb("var_a", [P, TT])
        rstd_a = sb("rstd_a", [P, TT])
        cols_a = sb("cols_a", [P, 2, DC])
        qk = sb("qk", [P, 3, 3, TOK], F32R)
        v = sb("v", [P, 2, TT, GH, 2, DH], F32R)
        neg_max = sb("neg_max", [P, 2, TT])
        row_sum = sb("row_sum", [P, 2, TT])
        row_rec = sb("row_rec", [P, 2, TT])
        probs = sb("probs", [P, 2, TT, TOK])
        probs_t = sb("probs_t", [P, 2, 2, TT, TOK], F32R)
        o_t = sb("o_t", [P, INNER // P, TOK])

        x_mid = sb("x_mid", [P, TT, DIM])
        mod_rows = sb("mod_rows", [P, 2, DIM])
        h_mid = sb("h_mid", [P, DC, TOK])
        g_mid = sb("g_mid", [P, 2, 2, TOK])
        tmp = sb("tmp", [P, 6, 2 * 256])
        kv_rep = sb("kv_rep", [P, DC, GH, NONGT])
        kbd = sb("kbd", [P, 2, DC, 8 * NONGT])
        vbd = sb("vbd", [P, 2, DIM])
        adj = sb("adj", [P, 2 * TT * NONGT, LABELS], I32)
        adj_v = sb("adj_v", [P, 3, 2 * TT * NONGT])
        cols_mid = sb("cols_mid", [P, 2, DC])
        small_mid = sb("small_mid", [P, 3, 2 * 16])
        x3 = sb("x3", [P, TT, DIM])
        x_back = sb("x_back", [P, TT, DIM])
        resid_back = sb("resid_back", [P, TT, DIM])
        cond_row = sb("cond_row", [P, DIM])
        h_back = sb("h_back", [P, DC, TOK])
        g_back = sb("g_back", [P, 2, 2, TOK])
        tmp_back = sb("tmp_back", [P, 5, 2 * 256])
        cols_back = sb("cols_back", [P, 3, 2, DC])
        small_back = sb("small_back", [P, 5, 2 * 16])
        ms_back = sb("ms_back", [P, 2, TT])
        stat_mid, stat_back = sb("stat_mid", [P, TT, 6]), sb("stat_back", [P, TT, 6])
        mv_mid, mv_back = sb("mv_mid", [P, TT, 2]), sb("mv_back", [P, TT, 2])
        var_mid, var_back = sb("var_mid", [P, TT]), sb("var_back", [P, TT])
        rstd_mid, rstd_back = sb("rstd_mid", [P, TT]), sb("rstd_back", [P, TT])

        tmp_flat = tmp[:, :, :].rearrange("p a b -> p (a b)")
        adj_mul = tmp_flat[:, 0:2 * TT * NONGT * LABELS].rearrange("p (r l) -> p r l", l=LABELS)
        e = [tmp_flat[:, 0:640], tmp_flat[:, 3 * 512:3 * 512 + 640]]
        e_t = g_mid[:, :, :, :].rearrange("p a b c -> p a (b c)")
        setup_rows = tmp_flat[0:BATCH, 0:3 * DIM]
        setup_in_rows = o_t[:, 0:len(SETUP_ROWS), :]

        def tile(k, rows_=P):
            return tmp[0:rows_, k, :].rearrange("p (a b) -> p a b", a=2)

        def tile_b(k):
            return tmp_back[:, k, :].rearrange("p (a b) -> p a b", a=2)

        resid_mid = tile(4)
        y_out = tile_b(1)
        silu_cond = h_mid

        ps_s = ctx.enter_context(nc.psum_tensor("ps_s", [P, 512], F32))
        ps_t = ctx.enter_context(nc.psum_tensor("ps_t", [P, 512], F32))
        ps_o = ctx.enter_context(nc.psum_tensor("ps_o", [P, 512], F32))
        ps_p = ctx.enter_context(nc.psum_tensor("ps_p", [P, 512], F32))
        ps_m = ctx.enter_context(nc.psum_tensor("ps_m", [P, 2, 512], F32))
        ps_b = ctx.enter_context(nc.psum_tensor("ps_b", [P, 2, 512], F32))

        def mid(k, rows_=P):
            return ps_m[0:rows_, k, :].rearrange("p (a b) -> p a b", a=2)

        def back(k):
            return ps_b[:, k, :].rearrange("p (a b) -> p a b", a=2)

        small_in = sem("small_in")
        front_w_in = sem("front_w_in")
        rest_w_in = sem("rest_w_in")
        piece_in = [sem(f"piece_in{k}") for k in range(6)]
        x_in = sem("x_in")
        gate_in = sem("gate_in")
        rows_in = sem("rows_in")
        cond_in = sem("cond_in")
        adj_in = sem("adj_in")
        stored = sem("stored")
        setup_act, setup_dve, setup_pe = sem("setup_act"), sem("setup_dve"), sem("setup_pe")
        stats_a_ready, mv_a_ready, var_a_ready, rstd_a_ready = (sem(n) for n in ("stats_a", "mv_a_s", "var_a_s", "rstd_a_s"))
        za_ready, za_turned, ha_ready, cols_a_ready = (sem(n) for n in ("za_ready", "za_turned", "ha_ready", "cols_a_ready"))
        gated_row_ready, resid_ready = sem("gated_row_ready"), sem("resid_ready")
        wq_scaled = sem("wq_scaled")
        projected, proj_high, proj_copied = sem("projected"), sem("proj_high"), sem("proj_copied")
        scored, max_ready, probs_ready = sem("scored"), sem("max_ready"), sem("probs_ready")
        probs_turned, probs_high, probs_copied = sem("probs_turned"), sem("probs_high"), sem("probs_copied")
        weighted = sem("weighted")
        sum_inverted, probs_normal = sem("sum_inverted"), sem("probs_normal")
        o_low, o_copied = sem("o_low"), sem("o_copied")
        pe_mid, act_mid, dve_mid, pool_mid = (sem(n) for n in ("pe_mid", "act_mid", "dve_mid", "pool_mid"))
        pe_back, act_back, dve_back, pool_back = (sem(n) for n in ("pe_back", "act_back", "dve_back", "pool_back"))

        def step_at(steps, name, b):
            return b * len(steps) + steps.index(name) + 2

        def proj_at(kind, k, i):
            return i * NPROJ + PROJ_USES.index((kind, k)) + 1

        def later(i):
            return not isinstance(i, int) or i > 0

        def run_steps(at, steps, place):
            for name in at.get(place, ()):
                if name in steps:
                    steps[name]()

        def run_schedule(eng, body):
            body(0, True, False, False, False, True)
            body(1, True, True, False, False, True)
            body(2, True, True, True, False, True)
            with eng.Fori(3, BATCH - 1) as i:
                body(i, True, True, True, True, True)
            body(BATCH - 1, True, True, True, True, False)
            body(BATCH, False, True, True, True, False)
            body(BATCH + 1, False, False, True, True, False)
            body(BATCH + 2, False, False, False, True, False)

        scratch = t["scratch"]
        block = ctx.enter_context(nc.Block())

        @block.sync
        def _(sp):
            sp.dma_start(cols[:], t["cols"]).then_inc(small_in, 16)
            sp.dma_start(ha[:, :, 0:BATCH], t["cond_t"]).then_inc(small_in, 16)
            for k in range(6):
                sp.dma_start(tile(k), t["w_mod"][k]).then_inc(piece_in[k], 16)
            sp.dma_start(rows[:], t["rows"].broadcast_to([P, len(ROWS), DIM])).then_inc(small_in, 16)
            sp.dma_start(setup_in_rows, t["setup_rows"].broadcast_to([P, len(SETUP_ROWS), DIM])).then_inc(small_in, 16)
            sp.dma_start(masks[:], t["masks"]).then_inc(small_in, 16)
            sp.dma_start(w_bias[:], t["w_bias"].broadcast_to([P, LABELS])).then_inc(small_in, 16)
            for k in range(6, PIECES):
                sp.wait_ge(setup_pe, k - 5)
                sp.dma_start(tile(k % 6), t["w_mod"][k]).then_inc(piece_in[k % 6], 16)
            sp.dma_start(xa[:], t["x"][0]).then_inc(x_in, 16)
            sp.dma_start(w["wqkv"][:], t["wqkv"]).then_inc(front_w_in, 16)
            sp.wait_ge(setup_dve, 3)
            sp.dma_start(scratch, setup_rows).then_inc(stored, 16)
            for name, _, _ in WEIGHTS:
                if name != "wqkv":
                    sp.dma_start(w[name][:], t[name]).then_inc(rest_w_in, 16)
            sp.wait_ge(stored, 16)

            def body(i, front, middle, rear, rear_end, pre):
                if middle:
                    b = i - 1
                    sp.wait_ge(dve_mid, b * len(DVE_MID) + 1)
                    sp.wait_ge(pool_mid, b * len(POOL_MID) + 1)
                    sp.dma_start(mod_rows[:], scratch[bass.ds(b, 1), DIM:3 * DIM].rearrange("a (r c) -> a r c", r=2)
                                 .broadcast_to([P, 2, DIM])).then_inc(rows_in, 16)
                    sp.dma_start(adj[:], t["adj"][bass.ds(b, 1)].rearrange("a p r l -> (a p) r l")).then_inc(adj_in, 16)
                if middle:
                    sp.wait_ge(dve_mid, step_at(DVE_MID, "x1", i - 1))
                if front:
                    sp.dma_start(g_msa[:], scratch[bass.ds(i, 1), 0:DIM].broadcast_to([P, DIM])).then_inc(gate_in, 16)
                if pre:
                    sp.wait_ge(resid_ready, i + 1)
                    sp.wait_ge(za_ready, i + 1)
                    sp.dma_start(xa[:], t["x"][bass.ds(i + 1, 1)].rearrange("a p t c -> (a p) t c")).then_inc(x_in, 16)
                if rear_end:
                    sp.wait_ge(dve_back, step_at(DVE_BACK, "out", i - 3))
                    sp.dma_start(out[bass.ds(i - 3, 1)].rearrange("a p t c -> (a p) t c"), y_out).then_inc(stored, 16)
                if rear:
                    b = i - 2
                    sp.wait_ge(dve_back, b * len(DVE_BACK) + 1)
                    sp.wait_ge(pool_back, b * len(POOL_BACK) + 1)
                    sp.dma_start(cond_row[:], t["cond"][bass.ds(b, 1), :].broadcast_to([P, DIM])).then_inc(cond_in, 16)

            run_schedule(sp, body)
            sp.wait_ge(stored, 16 * (BATCH + 1))

        @block.tensor
        def _(pe):
            mm = nc.tensor.matmul

            pe.wait_ge(small_in, 16 * SMALL_LOADS)
            pe.wait_ge(setup_dve, 2)
            for k in range(PIECES):
                pe.wait_ge(piece_in[k % 6], 16 * (k // 6 + 1))
                src = silu_cond if (k < 6 or k in (10, 11)) else ha
                for c in range(DC if k < COL_PIECES else 1):
                    for kk in range(DC):
                        if k < COL_PIECES:
                            n = (k * DC + c) * BATCH
                            last = mm(ps_b[:, n // 512, n % 512:n % 512 + BATCH], tile(k % 6)[:, kk, c * P:c * P + P],
                                      src[:, kk, 0:BATCH], start=(kk == 0), stop=(kk == 1))
                        else:
                            o = (k - COL_PIECES) * DIM
                            last = mm(ps_o[0:BATCH, o:o + DIM] if o < 512 else ps_t[0:BATCH, 0:DIM],
                                      src[:, kk, 0:BATCH], tile(k % 6)[:, kk, :], start=(kk == 0), stop=(kk == 1))
                last.then_inc(setup_pe, 1)
            pe.wait_ge(setup_dve, SETUP_DVE)
            pe.wait_ge(wq_scaled, 1)
            pe.nop().then_inc(pe_mid, 1)
            pe.nop().then_inc(pe_back, 1)

            def turn(dst, src):
                for a in range(2):
                    for c in range(2):
                        last = nc.tensor.transpose(dst[:, c, a * P:a * P + P], src[:, a, c * P:c * P + P], ident)
                return last

            def to_tokens(dst, src, weights):
                kk = src.shape[1]
                for tt in range(TT):
                    for k in range(kk):
                        last = mm(dst[:, tt, :], src[:, k, tt * P:tt * P + P], weights[:, k, :], start=(k == 0), stop=(k == kk - 1))
                return last

            def to_features(dst, src, weights, first=0):
                kk = src.shape[1]
                for c in range(2):
                    for k in range(kk):
                        last = mm(dst[:, c, :], weights[:, k, first + c * P:first + c * P + P], src[:, k, :],
                                  start=(k == 0), stop=(k == kk - 1))
                return last

            def down_part(dst, hidden, weights, j):
                for tt in range(TT):
                    for k in range(2):
                        last = mm(dst[:, tt, :], hidden[:, k, tt * P:tt * P + P], weights[:, 2 * j + k, :],
                                  start=(j == 0 and tt == 0 and k == 0), stop=(j == 3 and tt == 1 and k == 1),
                                  skip_group_check=True)
                return last

            def prelude(i):
                pe.wait_ge(za_ready, i + 1)
                if later(i):
                    pe.wait_ge(proj_copied, i * NPROJ)
                turn(ps_p[:].rearrange("p (a b) -> p a b", a=2), za).then_inc(za_turned, 1)

            def proj(kind, k, i):
                n = PROJ_USES.index((kind, k))
                bank_p = ps_p[:].rearrange("p (a b) -> p a b", a=2)
                if n == 0:
                    pe.wait_ge(ha_ready, i + 1)
                else:
                    pe.wait_ge(proj_copied, i * NPROJ + n)
                if kind == "qk":
                    for c in range(2):
                        for kk in range(DC):
                            last = mm(bank_p[:, c, :], w["wqkv"][:, kk, c * INNER + k * P:c * INNER + k * P + P],
                                      ha[:, kk, :], start=(kk == 0), stop=(kk == 1))
                else:
                    last = to_tokens(bank_p, ha, w["wqkv"][:, :, 2 * INNER + k * 256:2 * INNER + (k + 1) * 256])
                last.then_inc(projected, 1)

            def scores(hd, i):
                pe.wait_ge(proj_copied, proj_at("qk", hd // 2, i))
                h = qk[:, hd % 3]
                for tt in range(TT):
                    cut = slice(tt * P, tt * P + P)
                    mm(ps_s[:, tt * TOK:(tt + 1) * TOK], h[0:DH, 0, cut], h[0:DH, 1, :], start=True, stop=False)
                    last = mm(ps_s[:, tt * TOK:(tt + 1) * TOK], h[:, 0, cut], h[:, 2, :], start=False, stop=True)
                last.then_inc(scored, 1)

            def turn_probs(hd, i):
                pe.wait_ge(probs_normal, i * HEADS + hd + 1)
                if hd or later(i):
                    pe.wait_ge(probs_copied, i * HEADS + hd)
                turn(ps_t[:].rearrange("p (a b) -> p a b", a=2), probs[:, hd % 2]).then_inc(probs_turned, 1)

            def weigh(pair, i):
                grp = pair // 2
                if pair % 2 == 0:
                    pe.wait_ge(proj_copied, proj_at("v", grp, i))
                if pair or later(i):
                    pe.wait_ge(o_copied, i * PAIRS + pair)
                for hd in (2 * pair, 2 * pair + 1):
                    pe.wait_ge(probs_copied, i * HEADS + hd + 1)
                    for part in range(2):
                        for kt in range(TT):
                            last = mm(ps_o[:, hd % 2 * TOK:(hd % 2 + 1) * TOK], v[:, grp % 2, kt, hd % GH].rearrange("p a b -> p (a b)"),
                                      probs_t[:, hd % 2, part, kt, :], start=(part + kt == 0), stop=(part + kt == 2))
                last.then_inc(weighted, 1)

            def mid_steps(b):
                def A(n): return step_at(ACT_MID, n, b)
                def D(n): return step_at(DVE_MID, n, b)

                def attn_proj():
                    pe.wait_ge(o_copied, PAIRS * (b + 1))
                    pe.wait_ge(act_mid, b * len(ACT_MID) + 1)
                    return to_tokens(mid(0), o_t, w["w_out"])

                def norm_t0():
                    pe.wait_ge(dve_mid, D("z0"))
                    return turn(mid(1), tile(5))

                def up(j):
                    def run():
                        pe.wait_ge(act_mid, A("norm_h0") if j == 0 else A(f"gelu{j - 1}"))
                        return to_features(mid(0), h_mid, w["w1"], first=j * 256)
                    return run

                def down(j):
                    def run():
                        pe.wait_ge(act_mid, A(f"gelu{j}"))
                        return down_part(mid(1), g_mid[:, j % 2], w["w2"], j)
                    return run

                def x2_t():
                    pe.wait_ge(dve_mid, D("x2"))
                    return turn(mid(0), x_mid)

                def self_feat():
                    pe.wait_ge(act_mid, A("x2_c"))
                    return to_tokens(mid(1), tile(0), w["w_self"])

                def self_t():
                    pe.wait_ge(dve_mid, D("u"))
                    return turn(mid(0), tile(1))

                def gat_kvw():
                    pe.wait_ge(dve_mid, D("kv_rep"))
                    for d in range(2):
                        for k in range(DC):
                            last = mm(mid(1, GAT_ROWS)[:, d, :], kv_rep[:, k].rearrange("p a b -> p (a b)"),
                                      w["w_gout"][:, k, d * DIM:(d + 1) * DIM], start=(k == 0), stop=(k == 1))
                    return last

                def gat_k():
                    for d in range(2):
                        for c in range(DC):
                            for k in range(DC):
                                o = (d * DC + c) * NONGT
                                last = mm(ps_m[:, 0, o:o + NONGT], w["w_gk"][:, k, d * DIM + c * P:d * DIM + c * P + P],
                                          tile(2)[:, k, 0:NONGT], start=(k == 0), stop=(k == 1))
                    return last

                def gat_q(d):
                    def run():
                        pe.wait_ge(dve_mid, D("vbd") if d == 0 else D("kbd"))
                        return to_features(mid(1 - d), tile(2), w["w_gq"], first=d * DIM)
                    return run

                def gat_s(d):
                    def run():
                        if d == 0:
                            pe.wait_ge(act_mid, A("gat_qc1"))
                        else:
                            pe.wait_ge(dve_mid, D("gat_m0"))
                        for tt in range(TT):
                            for c in range(DC):
                                last = mm(ps_m[:, tt, c * 160:(c + 1) * 160], tile(3 + d)[:, c, tt * P:tt * P + P],
                                          kbd[:, d, c, :], start=True, stop=True)
                        return last
                    return run

                def gat_e(d, tt, bank, free):
                    def run():
                        pe.wait_ge(act_mid, A(f"gat_exp{d}"))
                        free()
                        for k in range(GROUPS):
                            last = nc.tensor.transpose(ps_m[0:GAT_ROWS, bank, k * P:(k + 1) * P],
                                                       e[d][:, tt * 320 + k * GAT_ROWS:tt * 320 + (k + 1) * GAT_ROWS], ident)
                        return last
                    return run

                def gat_o(d):
                    def run():
                        pe.wait_ge(act_mid, A(f"gat_ec{d}1"))
                        for tt in range(TT):
                            for k in range(GROUPS):
                                last = mm(mid(d)[:, tt, k * 64:(k + 1) * 64], e_t[0:GAT_ROWS, tt, k * P:(k + 1) * P],
                                          vbd[0:GAT_ROWS, d, k * 64:(k + 1) * 64], start=True, stop=True)
                        return last
                    return run

                return {"attn_proj": attn_proj, "norm_t0": norm_t0, "up0": up(0), "up1": up(1), "up2": up(2), "up3": up(3),
                        "down0": down(0), "down1": down(1), "down2": down(2), "down": down(3), "x2_t": x2_t,
                        "self_feat": self_feat, "self_t": self_t, "gat_kvw": gat_kvw, "gat_k": gat_k, "gat_q0": gat_q(0),
                        "gat_q1": gat_q(1), "gat_s0": gat_s(0), "gat_s1": gat_s(1),
                        "gat_e00": gat_e(0, 0, 0, lambda: pe.wait_ge(dve_mid, D("gat_m1"))),
                        "gat_e01": gat_e(0, 1, 1, lambda: None),
                        "gat_e10": gat_e(1, 0, 1, lambda: pe.wait_ge(act_mid, A("gat_ec01"))),
                        "gat_e11": gat_e(1, 1, 0, lambda: pe.wait_ge(dve_mid, D("gat_n0"))),
                        "gat_o0": gat_o(0), "gat_o1": gat_o(1)}

            def back_steps(b):
                def A(n): return step_at(ACT_BACK, n, b)
                def D(n): return step_at(DVE_BACK, n, b)

                def norm_t(n):
                    def run():
                        pe.wait_ge(dve_back, D(f"z{n}"))
                        return turn(back(0), tile_b(4))
                    return run

                def lin_q():
                    pe.wait_ge(act_back, A("norm_h1"))
                    return to_tokens(back(1), h_back, w["w_lq"])

                def lin_k():
                    return to_features(back(0), h_back, w["w_lk"])

                def lin_v():
                    pe.wait_ge(dve_back, D("lin_qb"))
                    return to_tokens(back(1), h_back, w["w_lv"])

                def lin_k_t():
                    pe.wait_ge(act_back, A("lin_kexp"))
                    for c in range(DC):
                        for tt in range(TT):
                            last = nc.tensor.transpose(back(0)[:, tt, c * P:(c + 1) * P], tile_b(2)[:, c, tt * P:(tt + 1) * P], ident)
                    return last

                def lin_q_t():
                    pe.wait_ge(dve_back, D("lin_vb"))
                    return turn(back(1), tile_b(0))

                def lin_ctx():
                    pe.wait_ge(act_back, A("lin_k_c"))
                    for c in range(DC):
                        for tt in range(TT):
                            last = mm(ps_b[:, 0, c * P:(c + 1) * P], tile_b(3)[:, tt, c * P:(c + 1) * P],
                                      tile_b(1)[:, tt, c * P:(c + 1) * P], start=(tt == 0), stop=(tt == 1))
                    return last

                def lin_y():
                    pe.wait_ge(act_back, A("lin_q_c"))
                    pe.wait_ge(dve_back, D("ctx_s"))
                    for tt in range(TT):
                        for c in range(DC):
                            last = mm(back(1)[:, tt, c * P:(c + 1) * P], tile_b(4)[:, c, tt * P:(tt + 1) * P],
                                      tmp_back[:, 2, c * P:(c + 1) * P], start=True, stop=True)
                    return last

                def lin_out():
                    pe.wait_ge(dve_back, D("silu2"))
                    return to_tokens(back(1), tile_b(2), w["w_lo"])

                def q3():
                    pe.wait_ge(act_back, A("norm_h3"))
                    return to_features(back(1), h_back, w["w_q3"])

                def k3():
                    return to_features(back(0), h_back, w["w_k3"])

                def v3():
                    pe.wait_ge(act_back, A("q3_c"))
                    return to_tokens(back(1), h_back, w["w_v3"])

                def s3():
                    pe.wait_ge(act_back, A("k3_c"))
                    for tt in range(TT):
                        for k in range(DC):
                            last = mm(back(0)[:, tt, :], tile_b(0)[:, k, tt * P:(tt + 1) * P], tile_b(1)[:, k, :],
                                      start=(k == 0), stop=(k == 1))
                    return last

                def p3_t():
                    pe.wait_ge(dve_back, D("p3_n"))
                    return turn(back(1), tile_b(3))

                def o3():
                    pe.wait_ge(act_back, A("p3_c"))
                    for c in range(DC):
                        for kt in range(TT):
                            last = mm(back(0)[:, c, :], tile_b(2)[:, kt, c * P:(c + 1) * P], tile_b(4)[:, kt, :],
                                      start=(kt == 0), stop=(kt == 1))
                    return last

                def proj3():
                    pe.wait_ge(act_back, A("o3_c"))
                    return to_tokens(back(1), tile_b(3), w["w_p3"])

                def up(j):
                    def run():
                        pe.wait_ge(act_back, A("norm_h4") if j == 0 else A(f"gelu3_{j - 1}"))
                        return to_features(back(1), h_back, w["w1_3"], first=j * 256)
                    return run

                def down(j):
                    def run():
                        pe.wait_ge(act_back, A(f"gelu3_{j}"))
                        return down_part(back(0), g_back[:, j % 2], w["w2_3"], j)
                    return run

                return {"norm_t1": norm_t(1), "lin_q": lin_q, "lin_k": lin_k, "lin_v": lin_v, "lin_k_t": lin_k_t,
                        "lin_q_t": lin_q_t, "lin_ctx": lin_ctx, "lin_y": lin_y, "norm_t2": norm_t(2), "lin_out": lin_out,
                        "norm_t3": norm_t(3), "q3": q3, "k3": k3, "v3": v3, "s3": s3, "p3_t": p3_t, "o3": o3, "proj3": proj3,
                        "norm_t4": norm_t(4), "up3_0": up(0), "up3_1": up(1), "up3_2": up(2), "up3_3": up(3),
                        "down3_0": down(0), "down3_1": down(1), "down3_2": down(2), "down3": down(3)}

            def body(i, front, middle, rear, rear_end, pre):
                mids = mid_steps(i - 1) if middle else {}
                backs = back_steps(i - 2) if rear else {}
                backs_end = back_steps(i - 3) if rear_end else {}

                def run_mid(place):
                    for name in MID_AT.get(place, ()) if middle else ():
                        mids[name]().then_inc(pe_mid, 1)

                def run_back(place):
                    steps = backs if place >= BACK_FIRST else backs_end
                    for name in BACK_AT.get(place, ()) if steps else ():
                        steps[name]().then_inc(pe_back, 1)

                run_back(0)
                run_mid(0)
                if front:
                    proj("qk", 1, i)
                for hd in range(HEADS):
                    if front:
                        turn_probs(hd, i)
                        if hd + 1 < HEADS:
                            scores(hd + 1, i)
                        elif pre:
                            scores(0, i + 1)
                    run_mid(hd + 1)
                    if front:
                        if hd % 2 == 1 and (hd + 3) // 2 < PAIRS:
                            proj("qk", (hd + 3) // 2, i)
                        if hd == 15 and pre:
                            proj("v", 0, i + 1)
                        if hd % 2 == 1:
                            weigh(hd // 2, i)
                        if hd % 4 == 2 and hd // 4 + 1 < GROUPS:
                            proj("v", hd // 4 + 1, i)
                        if hd == 13 and pre:
                            prelude(i + 1)
                        if hd == 14 and pre:
                            proj("qk", 0, i + 1)
                    if hd + 1 in MLP_AT:
                        for part, name in MLP_AT[hd + 1]:
                            if part == "mid" and middle:
                                mids[name]().then_inc(pe_mid, 1)
                            if part == "back" and rear_end:
                                backs_end[name]().then_inc(pe_back, 1)
                    run_back(hd + 1)
                for place in range(HEADS + 1, LAST_PLACE + 1):
                    run_mid(place)
                    run_back(place)
                if isinstance(i, int) and i == 0:
                    pe.wait_ge(rest_w_in, 16 * (len(WEIGHTS) - 1))

            prelude(0)
            proj("qk", 0, 0)
            scores(0, 0)
            proj("v", 0, 0)
            run_schedule(pe, body)

        @block.scalar
        def _(act):
            go = nc.scalar.activation
            act.wait_ge(small_in, 16 * SMALL_LOADS)
            go(silu_cond[:, :, 0:BATCH], ha[:, :, 0:BATCH], ACT.Tanh, scale=0.5).then_inc(setup_act, 1)
            go(qs_cols[:, 0, :], cols[:, COLS["bq_a"][0]:COLS["bq_a"][0] + DC], ACT.Copy, scale=GAT_D ** -0.5)
            go(qs_cols[:, 1, :], cols[:, COLS["bq_b"][0]:COLS["bq_b"][0] + DC], ACT.Copy, scale=GAT_D ** -0.5).then_inc(act_mid, 1)
            go(qs_cols[:, 2, :], cols[:, COLS["q_b3"][0]:COLS["q_b3"][0] + DC], ACT.Copy, scale=DIM ** -0.5).then_inc(act_back, 1)
            act.wait_ge(setup_dve, SETUP_DVE)
            act.wait_ge(setup_pe, PIECES)
            act.wait_ge(front_w_in, 16)
            go(w["wqkv"][:, :, 0:INNER], w["wqkv"][:, :, 0:INNER], ACT.Copy, scale=DH ** -0.5).then_inc(wq_scaled, 1)

            def affine(dst, src, scale_cols, shift_cols):
                for c in range(DC):
                    last = go(dst[:, c, :], src[:, c, :], ACT.Identity, bias=shift_cols[:, c:c + 1], scale=scale_cols[:, c:c + 1])
                return last

            def prelude(i):
                act.wait_ge(za_turned, i + 1)
                act.wait_ge(cols_a_ready, i + 1)
                affine(ha, ps_p[:].rearrange("p (a b) -> p a b", a=2), cols_a[:, 0], cols_a[:, 1]).then_inc(ha_ready, 1)

            def copy_proj(kind, k, i):
                act.wait_ge(projected, proj_at(kind, k, i))
                bank_p = ps_p[:].rearrange("p (a b) -> p a b", a=2)
                if kind == "qk":
                    for hd in (2 * k, 2 * k + 1):
                        r = hd % 2 * DH
                        go(qk[0:DH, hd % 3, 0:2, :], bank_p[r:r + DH], ACT.Copy)
                        last = go(qk[DH:, hd % 3, 2, :], bank_p[r:r + DH, 1, :], ACT.Copy)
                else:
                    for kt in range(TT):
                        last = go(v[:, k % 2, kt, :, 0, :], bank_p[:, kt].rearrange("p (h d) -> p h d", d=DH), ACT.Copy)
                last.then_inc(proj_high, 1)

            def exps(hd, i):
                act.wait_ge(max_ready, i * HEADS + hd + 1)
                for tt in range(TT):
                    last = go(probs[:, hd % 2, tt, :], ps_s[:, tt * TOK:(tt + 1) * TOK], ACT.Exp,
                              bias=neg_max[:, hd % 2, tt:tt + 1], accum_out=row_sum[:, hd % 2, tt:tt + 1])
                last.then_inc(probs_ready, 1)

            def high_probs(hd, i):
                act.wait_ge(probs_turned, i * HEADS + hd + 1)
                go(probs_t[:, hd % 2, 0], ps_t[:].rearrange("p (a b) -> p a b", a=2), ACT.Copy).then_inc(probs_high, 1)

            def copy_o(pair, i):
                act.wait_ge(weighted, i * PAIRS + pair + 1)
                if pair == 0 and later(i):
                    act.wait_ge(pe_mid, step_at(PE_MID, "attn_proj", i - 1))
                for k in range(2):
                    last = go(o_t[k * DH:(k + 1) * DH, pair, :], ps_o[DH:, k * TOK:(k + 1) * TOK], ACT.Copy)
                last.then_inc(o_low, 1)

            def mid_steps(b):
                def PE(n): return step_at(PE_MID, n, b)
                def D(n): return step_at(DVE_MID, n, b)

                def norm_h0():
                    act.wait_ge(pe_mid, PE("norm_t0"))
                    act.wait_ge(dve_mid, D("cols0"))
                    affine(h_mid, mid(1), cols_mid[:, 0], cols_mid[:, 1]).then_inc(act_mid, 1)

                def gelu(j):
                    def run():
                        act.wait_ge(pe_mid, PE(f"up{j}"))
                        for c in range(2):
                            last = go(g_mid[:, j % 2, c, :], mid(0)[:, c, :], ACT.Gelu, bias=col("b1", 2 * j + c))
                        last.then_inc(act_mid, 1)
                    return run

                def x2_c():
                    act.wait_ge(pe_mid, PE("x2_t"))
                    go(tile(0), mid(0), ACT.Copy).then_inc(act_mid, 1)

                def self_c():
                    act.wait_ge(pe_mid, PE("self_t"))
                    for c in range(DC):
                        last = go(tile(2)[:, c, :], mid(0)[:, c, :], ACT.Identity, bias=col("b_self", c))
                    last.then_inc(act_mid, 1)

                def gat_qc(d):
                    def run():
                        act.wait_ge(pe_mid, PE(f"gat_q{d}"))
                        for c in range(DC):
                            last = go(tile(3 + d)[:, c, :], mid(1 - d)[:, c, :], ACT.Identity, bias=qs_cols[:, d, c:c + 1],
                                      scale=GAT_D ** -0.5)
                        last.then_inc(act_mid, 1)
                    return run

                def gat_exp(d):
                    def run():
                        act.wait_ge(dve_mid, D(f"gat_sub{d}"))
                        go(e[d], e[d], ACT.Exp).then_inc(act_mid, 1)
                    return run

                def gat_ec(d, tt, bank):
                    def run():
                        act.wait_ge(pe_mid, PE(f"gat_e{d}{tt}"))
                        go(e_t[0:GAT_ROWS, tt, :], ps_m[0:GAT_ROWS, bank, :], ACT.Copy).then_inc(act_mid, 1)
                    return run

                def gat_exp1_ec00():
                    gat_exp(1)()
                    gat_ec(0, 0, 0)()

                return {"norm_t0": norm_h0, "up0": gelu(0), "up1": gelu(1), "up2": gelu(2), "up3": gelu(3), "x2_t": x2_c,
                        "self_t": self_c, "gat_q0": gat_qc(0), "gat_q1": gat_qc(1), "gat_s1": gat_exp(0),
                        "gat_e00": gat_exp1_ec00, "gat_e01": gat_ec(0, 1, 1), "gat_e10": gat_ec(1, 0, 1), "gat_e11": gat_ec(1, 1, 0)}

            def back_steps(b):
                def PE(n): return step_at(PE_BACK, n, b)
                def D(n): return step_at(DVE_BACK, n, b)

                def norm_h(n):
                    def run():
                        act.wait_ge(pe_back, PE(f"norm_t{n}"))
                        if n == 1:
                            act.wait_ge(dve_back, D("cols2"))
                            s, o = COLS["norm_g"][0], COLS["norm_b"][0]
                            affine(h_back, back(0), cols[:, s:s + DC], cols[:, o:o + DC]).then_inc(act_back, 1)
                        else:
                            affine(h_back, back(0), cols_back[:, n - 2, 0], cols_back[:, n - 2, 1]).then_inc(act_back, 1)
                    return run

                def norm_h2():
                    norm_h(2)()
                    act.wait_ge(act_back, step_at(ACT_BACK, "norm_h2", b))
                    go(tile_b(1), h_back[:], ACT.Tanh, scale=0.5).then_inc(act_back, 1)

                def lin_qexp():
                    act.wait_ge(dve_back, D("lin_qsub"))
                    go(tile_b(0), tile_b(0), ACT.Exp).then_inc(act_back, 1)

                def lin_kexp():
                    act.wait_ge(dve_back, D("lin_kbias"))
                    for c in range(DC):
                        last = go(tile_b(2)[:, c, :], back(0)[:, c, :], ACT.Exp, bias=small_back[:, 1, c:c + 1],
                                  accum_out=small_back[:, 2, c:c + 1])
                    last.then_inc(act_back, 1)

                def copy(dst, k, step):
                    def run():
                        act.wait_ge(pe_back, PE(step))
                        go(dst, back(k), ACT.Copy).then_inc(act_back, 1)
                    return run

                def q3_c():
                    act.wait_ge(pe_back, PE("q3"))
                    for c in range(DC):
                        last = go(tile_b(0)[:, c, :], back(1)[:, c, :], ACT.Identity, bias=qs_cols[:, 2, c:c + 1], scale=DIM ** -0.5)
                    last.then_inc(act_back, 1)

                def k3_c():
                    act.wait_ge(pe_back, PE("k3"))
                    for c in range(DC):
                        last = go(tile_b(1)[:, c, :], back(0)[:, c, :], ACT.Identity, bias=col("k_b3", c))
                    last.then_inc(act_back, 1)

                def o3_c():
                    act.wait_ge(pe_back, PE("o3"))
                    for c in range(DC):
                        last = go(tile_b(3)[:, c, :], back(0)[:, c, :], ACT.Identity, bias=col("v_b3", c))
                    last.then_inc(act_back, 1)

                def exp3():
                    act.wait_ge(dve_back, D("max3"))
                    for tt in range(TT):
                        last = go(tile_b(3)[:, tt, :], back(0)[:, tt, :], ACT.Exp, bias=small_back[:, 3, tt:tt + 1],
                                  accum_out=small_back[:, 4, tt:tt + 1])
                    last.then_inc(act_back, 1)

                def gelu(j):
                    def run():
                        act.wait_ge(pe_back, PE(f"up3_{j}"))
                        for c in range(2):
                            last = go(g_back[:, j % 2, c, :], back(1)[:, c, :], ACT.Gelu, bias=col("b1_3", 2 * j + c))
                        last.then_inc(act_back, 1)
                    return run

                return {"norm_t1": norm_h(1), "lin_q": lin_qexp, "lin_k": lin_kexp, "lin_k_t": copy(tile_b(3), 0, "lin_k_t"),
                        "lin_q_t": copy(tile_b(4), 1, "lin_q_t"), "norm_t2": norm_h2, "norm_t3": norm_h(3), "q3": q3_c, "k3": k3_c,
                        "s3": exp3, "p3_t": copy(tile_b(4), 1, "p3_t"), "o3": o3_c, "norm_t4": norm_h(4),
                        "up3_0": gelu(0), "up3_1": gelu(1), "up3_2": gelu(2), "up3_3": gelu(3)}

            def body(i, front, middle, rear, rear_end, pre):
                mids = mid_steps(i - 1) if middle else {}
                backs = back_steps(i - 2) if rear else {}
                backs_end = back_steps(i - 3) if rear_end else {}

                def run_back(place):
                    run_steps(BACK_AT, backs if place >= BACK_FIRST else backs_end, place)


                run_back(0)
                for hd in range(HEADS):
                    if front:
                        if hd == 0:
                            copy_proj("qk", 1, i)
                        high_probs(hd, i)
                        if hd + 1 < HEADS:
                            exps(hd + 1, i)
                        elif pre:
                            exps(0, i + 1)
                    run_steps(MID_AT, mids, hd + 1)
                    if front:
                        if hd % 2 == 1 and (hd + 3) // 2 < PAIRS:
                            copy_proj("qk", (hd + 3) // 2, i)
                        if hd == 15 and pre:
                            copy_proj("v", 0, i + 1)
                        if hd % 2 == 1:
                            copy_o(hd // 2, i)
                        if hd % 4 == 2 and hd // 4 + 1 < GROUPS:
                            copy_proj("v", hd // 4 + 1, i)
                        if hd == 13 and pre:
                            prelude(i + 1)
                        if hd == 14 and pre:
                            copy_proj("qk", 0, i + 1)
                    if hd + 1 in MLP_AT:
                        for part, name in MLP_AT[hd + 1]:
                            steps = mids if part == "mid" else backs_end
                            if name in steps:
                                steps[name]()
                    run_back(hd + 1)
                for place in range(HEADS + 1, LAST_PLACE + 1):
                    run_steps(MID_AT, mids, place)
                    run_back(place)

            prelude(0)
            copy_proj("qk", 0, 0)
            exps(0, 0)
            copy_proj("v", 0, 0)
            run_schedule(act, body)

        @block.vector
        def _(dve):
            V = nc.vector
            tt_ = V.tensor_tensor

            dve.wait_ge(setup_act, 1)
            dve.wait_ge(small_in, 16 * SMALL_LOADS)
            V.scalar_tensor_tensor(silu_cond[:, :, 0:BATCH], silu_cond[:, :, 0:BATCH], 1.0, ha[:, :, 0:BATCH], ALU.add, ALU.mult).then_inc(setup_dve, 1)
            dve.wait_ge(setup_dve, 1)
            V.tensor_scalar(silu_cond[:, :, 0:BATCH], silu_cond[:, :, 0:BATCH], 0.5, None, ALU.mult).then_inc(setup_dve, 1)
            srow = {n: setup_in_rows[:, k, :] for k, n in enumerate(SETUP_ROWS)}
            dve.wait_ge(setup_pe, PIECES)
            tt_(setup_rows[:, 0:DIM], ps_o[0:BATCH, 0:DIM], srow["mod_g"][0:BATCH], ALU.add)
            tt_(setup_rows[:, DIM:2 * DIM], ps_o[0:BATCH, DIM:2 * DIM], srow["mod_m"][0:BATCH], ALU.add)
            V.tensor_copy(setup_rows[:, 2 * DIM:], ps_t[0:BATCH, 0:DIM]).then_inc(setup_dve, 1)
            ncols = 5 * 2 * DC * BATCH
            mod = tmp_flat[:, 1024:1024 + ncols]
            scaled0 = tmp_flat[:, 2048:2048 + ncols // 2]
            for lo, hi, k in ((0, 512, 0), (512, ncols, 1)):
                n0, n1 = lo // BATCH + COLS["mod_b"][0], hi // BATCH + COLS["mod_b"][0]
                last = tt_(mod[:, lo:hi].rearrange("p (n b) -> p n b", b=BATCH),
                           ps_b[:, k, 0:hi - lo].rearrange("p (n b) -> p n b", b=BATCH),
                           cols[:, n0:n1].unsqueeze(2).broadcast_to([P, n1 - n0, BATCH]), ALU.add)
            last.then_inc(setup_dve, 1)
            dve.wait_ge(setup_dve, 4)
            mod5 = mod.rearrange("p (n s c b) -> p n s c b", n=5, s=2, c=DC)
            for n in range(5):
                for c in range(DC):
                    k = n * DC + c
                    jw, j0 = COLS["mod_w"][0] + k, COLS["mod_0"][0] + k
                    V.tensor_scalar(col_table[:, :, n, 0, c], mod5[:, n, 0, c, :], 1.0, cols[:, jw:jw + 1], ALU.add, ALU.mult)
                    last = V.tensor_scalar(scaled0[:, k * BATCH:(k + 1) * BATCH], mod5[:, n, 0, c, :],
                                           1.0, cols[:, j0:j0 + 1], ALU.add, ALU.mult)
            last.then_inc(setup_dve, 1)
            dve.wait_ge(setup_dve, 5)
            for n in range(5):
                for c in range(DC):
                    k = n * DC + c
                    tt_(col_table[:, :, n, 1, c], scaled0[:, k * BATCH:(k + 1) * BATCH], mod5[:, n, 1, c, :], ALU.add)
            V.memset(minus_half[:], -0.5)
            V.memset(eps[:, 0, :], EPS[0])
            V.memset(eps[:, 1, :], EPS[1])
            tt_(gat_row[:], srow["bout_a"], srow["bout_b"], ALU.add).then_inc(setup_dve, 1)
            dve.wait_ge(setup_dve, 6)
            tt_(gat_row[:], gat_row[:], srow["b_self"], ALU.add).then_inc(setup_dve, 1)
            V.memset(wait_pad[:, 0:1], 0.0).then_inc(dve_mid, 1)
            V.memset(wait_pad[:, 1:2], 0.0).then_inc(dve_back, 1)

            def norm_stats(dst, x):
                for tt in range(TT):
                    last = V.bn_stats(dst[:, tt, :], x[:, tt, :])
                return last

            def norm_mv(mv, src):
                V.memset(wait_pad[:, 2:3], 0.0)
                for tt in range(TT):
                    last = V.bn_aggr(mv[:, tt, :], src[:, tt, :])
                return last

            def norm_z(dst, x, mv, rstd, centre=True):
                for tt in range(TT):
                    if centre:
                        last = V.tensor_scalar(dst[:, tt, :], x[:, tt, :], mv[:, tt, 0:1], rstd[:, tt:tt + 1], ALU.subtract, ALU.mult)
                    else:
                        last = V.tensor_scalar(dst[:, tt, :], x[:, tt, :], rstd[:, tt:tt + 1], None, ALU.mult)
                return last

            def prelude_stats(i):
                dve.wait_ge(x_in, 16 * i + 16)
                norm_stats(stat_a, xa).then_inc(stats_a_ready, 1)
                dve.wait_ge(stats_a_ready, i + 1)
                norm_mv(mv_a, stat_a).then_inc(mv_a_ready, 1)

            def prelude_z(i):
                if later(i):
                    dve.wait_ge(ha_ready, i)
                else:
                    dve.wait_ge(setup_dve, SETUP_DVE)
                V.tensor_copy(cols_a[:], col_table[:, i, 0, :, :]).then_inc(cols_a_ready, 1)
                if later(i):
                    dve.wait_ge(projected, i * NPROJ)
                dve.wait_ge(rstd_a_ready, i + 1)
                norm_z(za, xa, mv_a, rstd_a).then_inc(za_ready, 1)

            def maxes(hd, i):
                dve.wait_ge(scored, i * HEADS + hd + 1)
                V.tensor_reduce(neg_max[:, hd % 2, :], ps_s[:].rearrange("p (a b) -> p a b", a=2), AX.X, ALU.max,
                                negate=True).then_inc(max_ready, 1)

            def normalise(hd, i):
                dve.wait_ge(probs_ready, i * HEADS + hd + 1)
                V.reciprocal(row_rec[:, hd % 2, :], row_sum[:, hd % 2, :]).then_inc(sum_inverted, 1)
                dve.wait_ge(sum_inverted, i * HEADS + hd + 1)
                for tt in range(TT):
                    last = V.tensor_scalar(probs[:, hd % 2, tt, :], probs[:, hd % 2, tt, :], row_rec[:, hd % 2, tt:tt + 1], None, ALU.mult)
                last.then_inc(probs_normal, 1)

            def low_probs(hd, i):
                dve.wait_ge(probs_high, i * HEADS + hd + 1)
                tt_(probs_t[:, hd % 2, 1], ps_t[:].rearrange("p (a b) -> p a b", a=2), probs_t[:, hd % 2, 0].bitcast(F32),
                    ALU.subtract).then_inc(probs_copied, 1)

            def low_proj(kind, k, i):
                dve.wait_ge(proj_high, proj_at(kind, k, i))
                bank_p = ps_p[:].rearrange("p (a b) -> p a b", a=2)
                if kind == "qk":
                    for hd in (2 * k, 2 * k + 1):
                        r, h = hd % 2 * DH, qk[:, hd % 3]
                        tt_(h[DH:, 0, :], bank_p[r:r + DH, 0, :], h[0:DH, 0, :].bitcast(F32), ALU.subtract)
                        last = tt_(h[0:DH, 2, :], bank_p[r:r + DH, 1, :], h[0:DH, 1, :].bitcast(F32), ALU.subtract)
                else:
                    for kt in range(TT):
                        vk = v[:, k % 2, kt]
                        last = tt_(vk[:, :, 1, :], bank_p[:, kt].rearrange("p (h d) -> p h d", d=DH), vk[:, :, 0, :].bitcast(F32), ALU.subtract)
                last.then_inc(proj_copied, 1)

            def add_o(pair, i):
                dve.wait_ge(o_low, i * PAIRS + pair + 1)
                for k in range(2):
                    o = o_t[k * DH:(k + 1) * DH, pair, :]
                    last = tt_(o, ps_o[0:DH, k * TOK:(k + 1) * TOK], o, ALU.add)
                last.then_inc(o_copied, 1)

            def mid_steps(b):
                def PE(n): return step_at(PE_MID, n, b)
                def A(n): return step_at(ACT_MID, n, b)
                def D(n): return step_at(DVE_MID, n, b)
                def PO(n): return step_at(POOL_MID, n, b)

                def attn_proj():
                    dve.wait_ge(act_mid, b * len(ACT_MID) + 1)
                    V.tensor_copy(cols_mid[:], col_table[:, b, 1, :, :]).then_inc(dve_mid, 1)
                    dve.wait_ge(dve_mid, D("cols0"))
                    dve.wait_ge(gate_in, 16 * b + 16)
                    dve.wait_ge(pe_mid, PE("attn_proj"))
                    tt_(x_mid[:], mid(0), per_tile(g_msa[:]), ALU.mult).then_inc(dve_mid, 1)
                    dve.wait_ge(dve_mid, D("x1_gated"))
                    dve.wait_ge(resid_ready, b + 1)
                    tt_(x_mid[:], x_mid[:], x_resid[:], ALU.add).then_inc(dve_mid, 1)
                    dve.wait_ge(dve_mid, D("x1"))
                    norm_stats(stat_mid, x_mid).then_inc(dve_mid, 1)
                    dve.wait_ge(dve_mid, D("stats0"))
                    norm_mv(mv_mid, stat_mid).then_inc(dve_mid, 1)

                def norm_t0():
                    dve.wait_ge(pool_mid, PO("rstd0"))
                    norm_z(tile(5), x_mid, mv_mid, rstd_mid).then_inc(dve_mid, 1)

                def up0():
                    dve.wait_ge(adj_in, 16 * b + 16)
                    dve.wait_ge(dve_mid, D("z0"))
                    tt_(adj_mul, adj[:], w_bias[:].unsqueeze(1).broadcast_to([P, 2 * TT * NONGT, LABELS]), ALU.mult).then_inc(dve_mid, 1)
                    dve.wait_ge(dve_mid, D("adj_w"))
                    V.tensor_reduce(adj_v[:, 0, :], adj_mul, AX.X, ALU.add)
                    V.tensor_reduce(adj_v[:, 1, :], adj[:], AX.X, ALU.add).then_inc(dve_mid, 1)

                def up1():
                    dve.wait_ge(dve_mid, D("adj_sum"))
                    V.tensor_scalar(adj_v[:, 1, :], adj_v[:, 1, :], 0.0, None, ALU.is_gt).then_inc(dve_mid, 1)
                    dve.wait_ge(dve_mid, D("adj_on"))
                    V.tensor_scalar(adj_v[:, 2, :], adj_v[:, 1, :], NEG, -NEG, ALU.mult, ALU.add).then_inc(dve_mid, 1)
                    dve.wait_ge(dve_mid, D("adj_neg"))
                    V.scalar_tensor_tensor(adj_v[:, 2, :], adj_v[:, 0, :], col("b_bias"), adj_v[:, 2, :], ALU.add, ALU.add).then_inc(dve_mid, 1)

                def down():
                    dve.wait_ge(rows_in, 16 * b + 16)
                    dve.wait_ge(pool_mid, PO("xr2"))
                    dve.wait_ge(pe_mid, PE("down"))
                    tt_(x_mid[:], mid(1), per_tile(mod_rows[:, 0, :]), ALU.mult).then_inc(dve_mid, 1)
                    dve.wait_ge(dve_mid, D("x2_gated"))
                    tt_(x_mid[:], x_mid[:], resid_mid, ALU.add).then_inc(dve_mid, 1)
                    dve.wait_ge(dve_mid, D("x2"))
                    V.tensor_reduce(small_mid[:, 0, 0:TT], x_mid[:], AX.X, ALU.add).then_inc(dve_mid, 1)
                    dve.wait_ge(dve_mid, D("row_sum"))
                    V.tensor_scalar(small_mid[:, 0, TT:2 * TT], small_mid[:, 0, 0:TT], 0.0, None, ALU.not_equal).then_inc(dve_mid, 1)

                def self_feat():
                    dve.wait_ge(pe_mid, PE("self_feat"))
                    dve.wait_ge(dve_mid, D("row_on"))
                    for tt in range(TT):
                        last = V.scalar_tensor_tensor(tile(1)[:, tt, :], mod_rows[:, 1, :], small_mid[:, 0, TT + tt:TT + tt + 1],
                                                      mid(1)[:, tt, :], ALU.mult, ALU.add)
                    last.then_inc(dve_mid, 1)

                def self_t():
                    dve.wait_ge(act_mid, A("self_c"))
                    for c in range(DC):
                        last = V.tensor_copy(kv_rep[:, c], tile(2)[:, c, 0:NONGT].unsqueeze(1).broadcast_to([P, GH, NONGT]))
                    last.then_inc(dve_mid, 1)

                def gat_kvw():
                    dve.wait_ge(pe_mid, PE("gat_kvw"))
                    tt_(vbd[0:GAT_ROWS], mid(1, GAT_ROWS), m["head_v"][0:GAT_ROWS].unsqueeze(1).broadcast_to([GAT_ROWS, 2, DIM]),
                        ALU.mult).then_inc(dve_mid, 1)

                def gat_k():
                    dve.wait_ge(pe_mid, PE("gat_k"))
                    for d in range(2):
                        for c in range(DC):
                            o = (d * DC + c) * NONGT
                            last = V.scalar_tensor_tensor(kbd[:, d, c, :].rearrange("p (a b) -> p a b", b=NONGT),
                                                          ps_m[:, 0, o:o + NONGT].unsqueeze(1).broadcast_to([P, 8, NONGT]),
                                                          col("bk_a" if d == 0 else "bk_b", c),
                                                          m["head_k"].rearrange("p (a b) -> p a b", b=NONGT), ALU.add, ALU.mult)
                    last.then_inc(dve_mid, 1)

                def gat_s(d):
                    on = adj_v[:, 1, d * TT * NONGT:(d + 1) * TT * NONGT].rearrange("p (t n) -> p t n", t=TT)
                    bias = adj_v[:, 2, d * TT * NONGT:(d + 1) * TT * NONGT].rearrange("p (t n) -> p t n", t=TT)
                    ed = e[d].rearrange("p (t h n) -> p t h n", t=TT, n=NONGT)
                    ed3 = e[d].rearrange("p (r n) -> p r n", n=NONGT)
                    wide = [P, TT, GAT_H, NONGT]

                    def run():
                        if d == 0:
                            dve.wait_ge(pool_mid, PO("acc"))
                        dve.wait_ge(pe_mid, PE(f"gat_s{d}"))
                        tt_(ed, ps_m[:, :, 0:320].rearrange("p t (h n) -> p t h n", n=NONGT), on.unsqueeze(2).broadcast_to(wide),
                            ALU.mult).then_inc(dve_mid, 1)
                        dve.wait_ge(dve_mid, D(f"gat_m{d}"))
                        tt_(ed, ed, bias.unsqueeze(2).broadcast_to(wide), ALU.add).then_inc(dve_mid, 1)
                        dve.wait_ge(dve_mid, D(f"gat_b{d}"))
                        V.tensor_reduce(small_mid[:, 1 + d, :], ed3, AX.X, ALU.max).then_inc(dve_mid, 1)
                        dve.wait_ge(dve_mid, D(f"gat_max{d}"))
                        tt_(ed3, ed3, small_mid[:, 1 + d, :].unsqueeze(2).broadcast_to([P, 2 * GAT_H, NONGT]), ALU.subtract).then_inc(dve_mid, 1)
                    return run

                def gat_e(d):
                    def run():
                        dve.wait_ge(act_mid, A(f"gat_exp{d}"))
                        V.tensor_reduce(small_mid[:, 1 + d, :], e[d].rearrange("p (r n) -> p r n", n=NONGT), AX.X, ALU.add).then_inc(dve_mid, 1)
                        dve.wait_ge(dve_mid, D(f"gat_den{d}"))
                        V.reciprocal(small_mid[:, 1 + d, :], small_mid[:, 1 + d, :]).then_inc(dve_mid, 1)
                    return run

                def gat_o(d):
                    def run():
                        dve.wait_ge(pe_mid, PE(f"gat_o{d}"))
                        dve.wait_ge(dve_mid, D("gat_rec1" if d == 0 else "gat_acc0"))
                        tt_(tile(0).rearrange("p t (h g) -> p (t h) g", g=GAT_D), ps_m[:, d, :].rearrange("p (r g) -> p r g", g=GAT_D),
                            small_mid[:, 1 + d, :].unsqueeze(2).broadcast_to([P, 2 * GAT_H, GAT_D]), ALU.mult).then_inc(dve_mid, 1)
                        dve.wait_ge(dve_mid, D(f"gat_n{d}"))
                        tt_(tile(5), tile(5), tile(0), ALU.add).then_inc(dve_mid, 1)
                        if d == 1:
                            dve.wait_ge(dve_mid, D("gat_acc1"))
                            if later(b):
                                dve.wait_ge(dve_back, step_at(DVE_BACK, "z1", b - 1))
                                dve.wait_ge(pool_back, step_at(POOL_BACK, "xr4", b - 1))
                            V.scalar_tensor_tensor(x3[:], tile(5), 0.0, x_mid[:], ALU.max, ALU.add).then_inc(dve_mid, 1)
                    return run

                before = {"norm_t0": norm_t0}
                after = {"attn_proj": attn_proj, "up0": up0, "up1": up1, "down": down, "self_feat": self_feat,
                         "self_t": self_t, "gat_kvw": gat_kvw, "gat_k": gat_k, "gat_s0": gat_s(0), "gat_s1": gat_s(1),
                         "gat_e00": gat_e(0), "gat_e01": gat_e(1), "gat_o0": gat_o(0), "gat_o1": gat_o(1)}
                return before, after

            def back_steps(b):
                def PE(n): return step_at(PE_BACK, n, b)
                def A(n): return step_at(ACT_BACK, n, b)
                def D(n): return step_at(DVE_BACK, n, b)
                def PO(n): return step_at(POOL_BACK, n, b)

                def stats(n, x):
                    norm_stats(stat_back, x).then_inc(dve_back, 1)
                    dve.wait_ge(dve_back, D(f"stats{n}"))
                    norm_mv(mv_back, stat_back).then_inc(dve_back, 1)

                def zed(n, x):
                    def run():
                        dve.wait_ge(pool_back, PO(f"rstd{n}"))
                        norm_z(tile_b(4), x, mv_back, rstd_back, centre=n < 3).then_inc(dve_back, 1)
                    return run

                def norm_t1():
                    dve.wait_ge(act_back, b * len(ACT_BACK) + 1)
                    V.tensor_copy(cols_back[:], col_table[:, b, 2:5, :, :]).then_inc(dve_back, 1)
                    dve.wait_ge(dve_back, D("cols2"))
                    dve.wait_ge(dve_mid, step_at(DVE_MID, "x3", b))
                    stats(1, x3)

                def lin_q():
                    dve.wait_ge(pe_back, PE("lin_q"))
                    tt_(tile_b(0), back(1), per_tile(row("bq")), ALU.add).then_inc(dve_back, 1)
                    q3 = tile_b(0).rearrange("p t (h d) -> p (t h) d", d=16)
                    dve.wait_ge(dve_back, D("lin_qb"))
                    V.tensor_reduce(small_back[:, 0, :], q3, AX.X, ALU.max).then_inc(dve_back, 1)
                    dve.wait_ge(dve_back, D("lin_qmax"))
                    tt_(q3, q3, small_back[:, 0, :].unsqueeze(2).broadcast_to([P, 32, 16]), ALU.subtract).then_inc(dve_back, 1)

                def lin_k():
                    dve.wait_ge(pe_back, PE("lin_k"))
                    V.tensor_reduce(small_back[:, 1, 2:4], back(0), AX.X, ALU.max).then_inc(dve_back, 1)
                    k0 = COLS["bk"][0]
                    dve.wait_ge(dve_back, D("lin_kmax"))
                    tt_(small_back[:, 1, 4:6], small_back[:, 1, 2:4], cols[:, k0:k0 + DC], ALU.add).then_inc(dve_back, 1)
                    dve.wait_ge(dve_back, D("lin_kmb"))
                    tt_(small_back[:, 1, 0:2], cols[:, k0:k0 + DC], small_back[:, 1, 4:6], ALU.subtract).then_inc(dve_back, 1)

                def lin_v():
                    dve.wait_ge(pe_back, PE("lin_v"))
                    dve.wait_ge(stored, 16 * b + 16)
                    tt_(tile_b(1), back(1), per_tile(row("bv")), ALU.add).then_inc(dve_back, 1)

                def lin_k_t():
                    dve.wait_ge(act_back, A("lin_qexp"))
                    V.tensor_reduce(small_back[:, 0, :], tile_b(0).rearrange("p t (h d) -> p (t h) d", d=16), AX.X, ALU.add).then_inc(dve_back, 1)
                    dve.wait_ge(dve_back, D("lin_qden"))
                    V.reciprocal(small_back[:, 0, :], small_back[:, 0, :]).then_inc(dve_back, 1)
                    dve.wait_ge(act_back, A("lin_kexp"))
                    V.reciprocal(small_back[:, 2, 2:4], small_back[:, 2, 0:2]).then_inc(dve_back, 1)

                def lin_ctx():
                    dve.wait_ge(pe_back, PE("lin_ctx"))
                    dve.wait_ge(dve_back, D("lin_krec"))
                    for c in range(DC):
                        last = V.scalar_tensor_tensor(tmp_back[:, 2, c * P:(c + 1) * P], ps_b[:, 0, c * P:(c + 1) * P],
                                                      small_back[:, 2, 2 + c:3 + c], m["head_c"], ALU.mult, ALU.mult)
                    last.then_inc(dve_back, 1)

                def lin_y():
                    dve.wait_ge(pe_back, PE("lin_y"))
                    tt_(tile_b(0).rearrange("p t (h d) -> p (t h) d", d=16), ps_b[:, 1, :].rearrange("p (r d) -> p r d", d=16),
                        small_back[:, 0, :].unsqueeze(2).broadcast_to([P, 32, 16]), ALU.mult).then_inc(dve_back, 1)
                    dve.wait_ge(dve_back, D("y"))
                    stats(2, tile_b(0))

                def silu2():
                    dve.wait_ge(act_back, A("lin_tanh"))
                    V.scalar_tensor_tensor(tile_b(2), tile_b(1), 1.0, h_back[:], ALU.add, ALU.mult).then_inc(dve_back, 1)

                def lin_out():
                    dve.wait_ge(cond_in, 16 * b + 16)
                    dve.wait_ge(pe_back, PE("lin_out"))
                    for tt in range(TT):
                        last = V.scalar_tensor_tensor(x_back[:, tt, :], back(1)[:, tt, :], 0.5, cond_row[:], ALU.mult, ALU.mult)
                    last.then_inc(dve_back, 1)
                    dve.wait_ge(dve_back, D("x4_gated"))
                    dve.wait_ge(pool_back, PO("xr4"))
                    tt_(x_back[:], x_back[:], resid_back[:], ALU.add).then_inc(dve_back, 1)
                    dve.wait_ge(dve_back, D("x4"))
                    stats(3, x_back)

                def v3():
                    dve.wait_ge(pe_back, PE("v3"))
                    V.tensor_copy(tile_b(2), back(1)).then_inc(dve_back, 1)

                def s3():
                    dve.wait_ge(pe_back, PE("s3"))
                    V.tensor_reduce(small_back[:, 3, 0:TT], back(0), AX.X, ALU.max, negate=True).then_inc(dve_back, 1)

                def p3_t():
                    dve.wait_ge(act_back, A("exp3"))
                    V.reciprocal(small_back[:, 4, 2:4], small_back[:, 4, 0:2]).then_inc(dve_back, 1)
                    dve.wait_ge(dve_back, D("rec3"))
                    for tt in range(TT):
                        last = V.tensor_scalar(tile_b(3)[:, tt, :], tile_b(3)[:, tt, :], small_back[:, 4, 2 + tt:3 + tt], None, ALU.mult)
                    last.then_inc(dve_back, 1)

                def proj3():
                    dve.wait_ge(pool_back, PO("xr5"))
                    dve.wait_ge(pe_back, PE("proj3"))
                    tt_(x_back[:], back(1), resid_back[:], ALU.add).then_inc(dve_back, 1)
                    dve.wait_ge(dve_back, D("x5"))
                    stats(4, x_back)

                def down3():
                    dve.wait_ge(pool_back, PO("xr6"))
                    dve.wait_ge(pe_back, PE("down3"))
                    tt_(y_out, back(0), resid_back[:], ALU.add).then_inc(dve_back, 1)

                before = {"stats1": norm_t1, "norm_t1": zed(1, x3), "norm_t2": zed(2, tile_b(0)), "norm_t3": zed(3, x_back), "p3_t": p3_t,
                          "norm_t4": zed(4, x_back)}
                after = {"lin_q": lin_q, "lin_k": lin_k, "lin_v": lin_v, "lin_k_t": lin_k_t, "lin_ctx": lin_ctx,
                         "lin_y": lin_y, "norm_t2": silu2, "lin_out": lin_out, "v3": v3, "s3": s3, "proj3": proj3, "down3": down3}
                return before, after

            def body(i, front, middle, rear, rear_end, pre):
                mids_before, mids = mid_steps(i - 1) if middle else ({}, {})
                backs_before, backs = back_steps(i - 2) if rear else ({}, {})
                ends_before, backs_end = back_steps(i - 3) if rear_end else ({}, {})

                def run_before(place):
                    run_steps(BACK_AT, backs_before if place >= BACK_FIRST else ends_before, place)

                def run_back(place):
                    run_steps(BACK_AT, backs if place >= BACK_FIRST else backs_end, place)

                run_before(0)
                run_back(0)
                for hd in range(HEADS):
                    if front:
                        if hd == 0:
                            low_proj("qk", 1, i)
                        if hd + 1 < HEADS:
                            maxes(hd + 1, i)
                        elif pre:
                            maxes(0, i + 1)
                        low_probs(hd, i)
                    run_before(hd + 1)
                    if front and hd + 1 < HEADS:
                        normalise(hd + 1, i)
                    elif pre:
                        normalise(0, i + 1)
                    if hd == 11 and pre:
                        prelude_stats(i + 1)
                    if hd == 12 and pre:
                        prelude_z(i + 1)
                    run_steps(MID_AT, mids, hd + 1)
                    run_steps(MID_AT, mids_before, hd + 2)
                    if front:
                        if hd % 2 == 1 and (hd + 3) // 2 < PAIRS:
                            low_proj("qk", (hd + 3) // 2, i)
                        if hd == 15 and pre:
                            low_proj("v", 0, i + 1)
                        if hd % 2 == 1:
                            add_o(hd // 2, i)
                        if hd % 4 == 2 and hd // 4 + 1 < GROUPS:
                            low_proj("v", hd // 4 + 1, i)
                        if hd == 14 and pre:
                            low_proj("qk", 0, i + 1)
                    if middle and hd + 1 == min(MLP_AT):
                        mids["up0"]()
                        mids["up1"]()
                    if hd + 1 == max(MLP_AT):
                        if rear_end:
                            backs_end["down3"]()
                        if rear:
                            backs_before["stats1"]()
                        if middle:
                            mids["down"]()
                    run_back(hd + 1)
                for place in range(HEADS + 1, LAST_PLACE + 1):
                    run_before(place)
                    run_steps(MID_AT, mids, place)
                    run_steps(MID_AT, mids_before, place + 1)
                    run_back(place)

            prelude_stats(0)
            prelude_z(0)
            low_proj("qk", 0, 0)
            maxes(0, 0)
            normalise(0, 0)
            low_proj("v", 0, 0)
            run_schedule(dve, body)

        @block.gpsimd
        def _(pool):
            G = nc.gpsimd
            pool.wait_ge(setup_dve, SETUP_DVE)
            G.memset(ms_back[:, 0], 0.0).then_inc(pool_mid, 1)
            G.memset(ms_back[:, 1], 0.0).then_inc(pool_back, 1)

            def prelude(i):
                pool.wait_ge(mv_a_ready, i + 1)
                G.tensor_tensor(var_a[:], mv_a[:, :, 1], eps[:, 0, :], ALU.add).then_inc(var_a_ready, 1)
                pool.wait_ge(var_a_ready, i + 1)
                G.tensor_tensor(rstd_a[:], var_a[:], minus_half[:], ALU.pow).then_inc(rstd_a_ready, 1)

            def front_resid(i):
                pool.wait_ge(gate_in, 16 * i + 16)
                pool.wait_ge(x_in, 16 * i + 16)
                if later(i):
                    pool.wait_ge(dve_mid, step_at(DVE_MID, "x1", i - 1))
                G.tensor_tensor(x_resid[:], per_tile(g_msa[:]), per_tile(row("b_out")), ALU.mult).then_inc(gated_row_ready, 1)
                pool.wait_ge(gated_row_ready, i + 1)
                G.tensor_tensor(x_resid[:], xa[:], x_resid[:], ALU.add).then_inc(resid_ready, 1)

            def mid_steps(b):
                def D(n): return step_at(DVE_MID, n, b)
                def PO(n): return step_at(POOL_MID, n, b)

                def attn_proj():
                    pool.wait_ge(dve_mid, D("mv0"))
                    G.tensor_tensor(var_mid[:], mv_mid[:, :, 1], eps[:, 0, :], ALU.add).then_inc(pool_mid, 1)
                    pool.wait_ge(pool_mid, PO("var0"))
                    G.tensor_tensor(rstd_mid[:], var_mid[:], minus_half[:], ALU.pow).then_inc(pool_mid, 1)
                    pool.wait_ge(rows_in, 16 * b + 16)
                    G.tensor_tensor(resid_mid, per_tile(mod_rows[:, 0, :]), per_tile(row("b2")), ALU.mult).then_inc(pool_mid, 1)
                    pool.wait_ge(pool_mid, PO("gb2"))
                    G.tensor_tensor(resid_mid, x_mid[:], resid_mid, ALU.add).then_inc(pool_mid, 1)

                def self_feat():
                    pool.wait_ge(dve_mid, D("u"))
                    G.tensor_tensor(tile(5), tile(1), per_tile(gat_row[:]), ALU.add).then_inc(pool_mid, 1)

                return {"attn_proj": attn_proj, "self_feat": self_feat}

            def back_steps(b):
                def D(n): return step_at(DVE_BACK, n, b)
                def PO(n): return step_at(POOL_BACK, n, b)

                def rstd(n):
                    pool.wait_ge(dve_back, D(f"mv{n}"))
                    if n >= 3:
                        G.tensor_tensor(ms_back[:, 0, :], mv_back[:, :, 0], mv_back[:, :, 0], ALU.mult).then_inc(pool_back, 1)
                        pool.wait_ge(pool_back, PO(f"sq{n}"))
                        G.tensor_tensor(ms_back[:, 1, :], ms_back[:, 0, :], mv_back[:, :, 1], ALU.add).then_inc(pool_back, 1)
                        pool.wait_ge(pool_back, PO(f"ms{n}"))
                        G.tensor_tensor(var_back[:], ms_back[:, 1, :], eps[:, 1, :], ALU.add).then_inc(pool_back, 1)
                    else:
                        G.tensor_tensor(var_back[:], mv_back[:, :, 1], eps[:, 0, :], ALU.add).then_inc(pool_back, 1)
                    pool.wait_ge(pool_back, PO(f"var{n}"))
                    G.tensor_tensor(rstd_back[:], var_back[:], minus_half[:], ALU.pow).then_inc(pool_back, 1)

                def norm_t1():
                    rstd(1)
                    pool.wait_ge(cond_in, 16 * b + 16)
                    G.tensor_tensor(resid_back[:], per_tile(cond_row[:]), per_tile(row("out_b")), ALU.mult).then_inc(pool_back, 1)
                    pool.wait_ge(pool_back, PO("gob"))
                    G.tensor_tensor(resid_back[:], x3[:], resid_back[:], ALU.add).then_inc(pool_back, 1)

                def lin_y():
                    rstd(2)

                def lin_out():
                    rstd(3)
                    G.tensor_tensor(resid_back[:], x_back[:], per_tile(row("proj_b3")), ALU.add).then_inc(pool_back, 1)

                def proj3():
                    rstd(4)
                    G.tensor_tensor(resid_back[:], x_back[:], per_tile(row("b2_3")), ALU.add).then_inc(pool_back, 1)

                return {"norm_t1": norm_t1}, {"lin_y": lin_y, "lin_out": lin_out, "proj3": proj3}

            def body(i, front, middle, rear, rear_end, pre):
                mids = mid_steps(i - 1) if middle else {}
                backs_before, backs = back_steps(i - 2) if rear else ({}, {})
                ends_before, backs_end = back_steps(i - 3) if rear_end else ({}, {})

                def run_before(place):
                    run_steps(BACK_AT, backs_before if place >= BACK_FIRST else ends_before, place)

                def run_back(place):
                    run_steps(BACK_AT, backs if place >= BACK_FIRST else backs_end, place)


                run_before(0)
                run_back(0)
                for hd in range(HEADS):
                    run_before(hd + 1)
                    if hd == 11 and pre:
                        prelude(i + 1)
                    if hd == 1 and front:
                        front_resid(i)
                    run_steps(MID_AT, mids, hd + 1)
                    run_back(hd + 1)
                for place in range(HEADS + 1, LAST_PLACE + 1):
                    run_before(place)
                    run_steps(MID_AT, mids, place)
                    run_back(place)

            prelude(0)
            run_schedule(pool, body)


def kernel(**inputs):
    import numpy as np
    import concourse.bacc as bacc
    from concourse.bass_utils import run_bass_kernel_spmd

    a = {k: np.asarray(v) for k, v in inputs.items()}

    def chunks(wt):
        return wt.reshape(wt.shape[0] // P, P, wt.shape[1]).transpose(1, 0, 2)

    def columns(vec):
        return vec.reshape(-1, P).T

    f1, f2 = "L3_cond_film1_", "L3_cond_film2_"
    w_mod, b_mod = a["L0_cond_W_mod"], a["L0_cond_b_mod"]
    parts = [(w_mod, b_mod, 1), (w_mod, b_mod, 0), (w_mod, b_mod, 4), (w_mod, b_mod, 3),
             (a["L2_cond_emb_W"], a["L2_cond_emb_b"], 0), (a["L2_cond_emb_W"], a["L2_cond_emb_b"], 1),
             (a[f1 + "w"], a[f1 + "b"], 0), (a[f1 + "w"], a[f1 + "b"], 1),
             (a[f2 + "w"], a[f2 + "b"], 0), (a[f2 + "w"], a[f2 + "b"], 1),
             (w_mod, b_mod, 2), (w_mod, b_mod, 5)]
    pieces = [chunks(wt[:, n * DIM:(n + 1) * DIM]) for wt, _, n in parts] + [chunks(a["L1_cond_W_self"][:, DIM:].T)]
    one, zero = np.ones(DIM, np.float32), np.zeros(DIM, np.float32)
    vectors = {
        "b1": a["L0_cond_b1"], "b1_3": a["L3_cond_mlp_b1"], "b_self": a["L1_cond_b_self"],
        "bq_a": a["L1_cond_bq"][0], "bq_b": a["L1_cond_bq"][1], "bk_a": a["L1_cond_bk"][0], "bk_b": a["L1_cond_bk"][1],
        "norm_g": a["L2_cond_norm_g"], "norm_b": a["L2_cond_norm_b"], "bk": a["L2_cond_bk"],
        "q_b3": a["L3_cond_q_b"], "k_b3": a["L3_cond_k_b"], "v_b3": a["L3_cond_v_b"],
        "mod_b": np.concatenate([v[n * DIM:(n + 1) * DIM] for _, v, n in parts[:COL_PIECES]]),
        "mod_w": np.concatenate([one, one, a["L2_cond_sn_g"], a["L3_cond_norm1_w"], a["L3_cond_norm2_w"]]),
        "mod_0": np.concatenate([zero, zero, a["L2_cond_sn_b"], zero, zero]),
        "b_bias": np.broadcast_to(a["L1_cond_b_bias"], (P,)),
    }
    row_vectors = [a["L0_cond_b_out"], a["L0_cond_b2"], a["L2_cond_bq"], a["L2_cond_bv"], a["L2_cond_out_b"],
                   a["L3_cond_proj_b"], a["L3_cond_mlp_b2"]]
    setup_row_vectors = [a["L1_cond_b_self"], a["L1_cond_bout"][0], a["L1_cond_bout"][1], b_mod[2 * DIM:3 * DIM], b_mod[5 * DIM:]]
    p = np.arange(P)[:, None]
    masks = np.concatenate([
        p == np.arange(P)[None, :],
        p // 16 == np.repeat(np.arange(8), NONGT)[None, :],
        p // NONGT == np.arange(DIM)[None, :] // GAT_D % GH,
        p // 16 == np.arange(P)[None, :] // 16], axis=1).astype(np.float32)
    mask = a["mask_BxSxSx11_ik0"]
    labels = np.stack([mask[:, :, :NONGT].reshape(BATCH, TT, P, NONGT, LABELS).transpose(0, 2, 1, 3, 4),
                       mask[:, :NONGT].transpose(0, 2, 1, 3).reshape(BATCH, TT, P, NONGT, LABELS).transpose(0, 2, 1, 3, 4)], axis=2)
    w2d = {
        "wqkv": a["L0_cond_W_qkv"], "w_out": a["L0_cond_W_out"], "w1": a["L0_cond_W1"], "w2": a["L0_cond_W2"],
        "w_self": a["L1_cond_W_self"][:, :DIM].T, "w_gq": np.concatenate([m.T for m in a["L1_cond_Wq"]], axis=1),
        "w_gk": np.concatenate([m.T for m in a["L1_cond_Wk"]], axis=1),
        "w_gout": np.concatenate([m.reshape(DIM, DIM).T for m in a["L1_cond_Wout"]], axis=1),
        "w_lq": a["L2_cond_Wq"], "w_lk": a["L2_cond_Wk"], "w_lv": a["L2_cond_Wv"], "w_lo": a["L2_cond_out_W"],
        "w_q3": a["L3_cond_q_w"], "w_k3": a["L3_cond_k_w"], "w_v3": a["L3_cond_v_w"], "w_p3": a["L3_cond_proj_w"],
        "w1_3": a["L3_cond_mlp_w1"], "w2_3": a["L3_cond_mlp_w2"],
    }
    arrays = {
        "x": a["x"].reshape(BATCH, TT, P, DIM).transpose(0, 2, 1, 3),
        "cond": a["cond_1024"], "cond_t": chunks(a["cond_1024"].T),
        "cols": np.concatenate([columns(vectors[n]) for n in COLS], axis=1),
        "rows": np.stack(row_vectors)[None], "setup_rows": np.stack(setup_row_vectors)[None], "masks": masks, "w_bias": a["L1_cond_w_bias"][None],
        "w_mod": np.stack(pieces), "adj": labels.reshape(BATCH, P, 2 * TT * NONGT, LABELS),
        **{n: chunks(w2d[n]) for n, _, _ in WEIGHTS},
    }
    arrays = {k: np.ascontiguousarray(v) for k, v in arrays.items()}

    nc = bacc.Bacc("TRN2", target_bir_lowering=False, num_devices=1)
    t = {k: nc.dram_tensor("in_" + k, v.shape, mybir.dt.from_np(v.dtype), kind="ExternalInput").ap() for k, v in arrays.items()}
    t["scratch"] = nc.dram_tensor("mod_rows_scratch", (BATCH, 3 * DIM), F32, kind="Internal").ap()
    out = nc.dram_tensor("out", (BATCH, P, TT, DIM), F32, kind="ExternalOutput").ap()
    build(nc, t, out)
    got = run_bass_kernel_spmd(nc, [{"in_" + k: v for k, v in arrays.items()}], core_ids=[0]).results[0]["out"]
    return got.reshape(BATCH, P, TT, DIM).transpose(0, 2, 1, 3).reshape(BATCH, TOK, DIM)
```
